# Optimizing a Trainium2 kernel written in Bass

```python
import numpy as np
import jax
import jax.numpy as jnp

def _softmax(x, axis=-1):
    return jax.nn.softmax(x, axis=axis)

def _gelu(x):
    return jax.nn.gelu(x, approximate=True)

def _silu(x):
    return jax.nn.silu(x)

def _sigmoid(x):
    return jax.nn.sigmoid(x)

def _layernorm(x, axis=-1, eps=1e-05):
    m = jnp.mean(x, axis=axis, keepdims=True)
    v = jnp.var(x, axis=axis, keepdims=True)
    return (x - m) / jnp.sqrt(v + eps)

def _scatter_add(tgt, idx, src, axis=0):
    return tgt.at[idx].add(src)

def _segment_sum(src, seg, n):
    return jax.ops.segment_sum(src, seg, n)
kernel_name = 'mk_hybrid_d1_jaxref_r4_d6ac92'

def setup_inputs(seed: int=0):
    np.random.seed(seed)
    _w = jnp.asarray

    def _L0_attn_a_setup():
        import jax, jax.numpy as jnp
        import numpy as np
        NUM_HEADS = 8
        ROPE_BASE = 10000.0

        def _rope(x):
            b, n, c = x.shape
            k_max = c // 2
            theta = 1.0 / ROPE_BASE ** (jnp.arange(k_max, dtype=jnp.float32) / k_max)
            angles = jnp.arange(n, dtype=jnp.float32)[:, None] * theta
            cos = jnp.cos(angles)
            sin = jnp.sin(angles)
            xr = x[..., 0::2]
            xi = x[..., 1::2]
            pr = cos * xr - sin * xi
            pi = cos * xi + sin * xr
            return jnp.concatenate([pr, pi], axis=-1)
        key = jax.random.key(seed)
        ks = jax.random.split(key, 5)
        b, n, c = (4, 1024, 256)
        x = jax.random.normal(ks[0], (b, n, c), dtype=jnp.float32)
        qk_w = jax.random.normal(ks[1], (c, 2 * c), dtype=jnp.float32) * (1.0 / np.sqrt(c))
        qk_b = jnp.zeros((2 * c,), dtype=jnp.float32)
        lepe_w = jax.random.normal(ks[2], (3, c, c), dtype=jnp.float32) * (1.0 / np.sqrt(3 * c))
        lepe_b = jnp.zeros((c,), dtype=jnp.float32)
        return {'x': x, 'qk_w': qk_w, 'qk_b': qk_b, 'lepe_w': lepe_w, 'lepe_b': lepe_b}
    _L0_attn_a_in = _L0_attn_a_setup()

    def _L0_attn_b_setup():
        import jax, jax.numpy as jnp
        import numpy as np
        B, T, D = (4, 1024, 256)
        F = 4 * D
        EPS_INIT = -1e+30

        def layer_norm(x, w, b, eps=1e-05):
            mu = jnp.mean(x, axis=-1, keepdims=True)
            var = jnp.var(x, axis=-1, keepdims=True)
            return (x - mu) * jax.lax.rsqrt(var + eps) * w + b

        def time_shift(x):
            return jnp.concatenate([jnp.zeros_like(x[:, :1]), x[:, :-1]], axis=1)

        def wkv(w, u, k, v):
            bsz, _, dim = k.shape
            alpha0 = jnp.zeros((bsz, dim), k.dtype)
            beta0 = jnp.zeros((bsz, dim), k.dtype)
            eps0 = jnp.full((bsz, dim), EPS_INIT, k.dtype)

            def step(carry, kv_t):
                alpha, beta, eps = carry
                kt, vt = kv_t
                ukt = u + kt
                tau = jnp.maximum(ukt, eps)
                e1 = jnp.exp(eps - tau)
                e2 = jnp.exp(ukt - tau)
                out = (e1 * alpha + e2 * vt) / (e1 * beta + e2)
                weps = eps - w
                tau2 = jnp.maximum(weps, kt)
                d1 = jnp.exp(weps - tau2)
                d2 = jnp.exp(kt - tau2)
                return ((d1 * alpha + d2 * vt, d1 * beta + d2, tau2), out)
            kT = jnp.swapaxes(k, 0, 1)
            vT = jnp.swapaxes(v, 0, 1)
            _, outT = jax.lax.scan(step, (alpha0, beta0, eps0), (kT, vT))
            return jnp.swapaxes(outT, 0, 1)
        key = jax.random.key(seed)
        ks = jax.random.split(key, 20)
        n = lambda k, shape, s: jax.random.normal(k, shape, jnp.float32) * s
        u = lambda k, shape: jax.random.uniform(k, shape, jnp.float32)
        s = 0.02
        return {'x': jax.random.normal(ks[0], (B, T, D), jnp.float32), 'ln1_w': jnp.ones((D,), jnp.float32), 'ln1_b': jnp.zeros((D,), jnp.float32), 'ln2_w': jnp.ones((D,), jnp.float32), 'ln2_b': jnp.zeros((D,), jnp.float32), 'time_decay': n(ks[1], (D,), 0.5), 'time_first': n(ks[2], (D,), 0.5), 'time_mix_k': u(ks[3], (1, 1, D)), 'time_mix_v': u(ks[4], (1, 1, D)), 'time_mix_r': u(ks[5], (1, 1, D)), 'w_key': n(ks[6], (D, D), s), 'w_value': n(ks[7], (D, D), s), 'w_recept': n(ks[8], (D, D), s), 'w_output': n(ks[9], (D, D), s), 'f_time_mix_k': u(ks[10], (1, 1, D)), 'f_time_mix_r': u(ks[11], (1, 1, D)), 'f_w_key': n(ks[12], (D, F), s), 'f_w_recept': n(ks[13], (D, D), s), 'f_w_value': n(ks[14], (F, D), s)}
    _L0_attn_b_in = _L0_attn_b_setup()

    def _L0_ffn_setup():
        import jax, jax.numpy as jnp
        import numpy as np
        E, K, D, H = (8, 2, 256, 512)
        B, S = (1, 256)

        def _grouped_swiglu(x_sorted, counts, w1, w2, w3):
            if hasattr(jax.lax, 'ragged_dot'):
                gs = counts.astype(jnp.int32)
                h = jax.nn.silu(jax.lax.ragged_dot(x_sorted, w1, gs)) * jax.lax.ragged_dot(x_sorted, w3, gs)
                return jax.lax.ragged_dot(h, w2, gs)
            pos = jnp.arange(x_sorted.shape[0])
            eid = jnp.searchsorted(jnp.cumsum(counts), pos, side='right')
            out = jnp.zeros((x_sorted.shape[0], w2.shape[-1]), x_sorted.dtype)
            for e in range(w1.shape[0]):
                xm = jnp.where((eid == e)[:, None], x_sorted, 0.0)
                he = jax.nn.silu(xm @ w1[e]) * (xm @ w3[e])
                out = out + he @ w2[e]
            return out
        key = jax.random.key(seed)
        k0, k1, k2, k3, k4 = jax.random.split(key, 5)
        sD = 1.0 / np.sqrt(D)
        sH = 1.0 / np.sqrt(H)
        return {'hidden_states': jax.random.normal(k0, (B, S, D), jnp.float32), 'gate_w': jax.random.normal(k1, (E, D), jnp.float32) * sD, 'w1': jax.random.normal(k2, (E, D, H), jnp.float32) * sD, 'w2': jax.random.normal(k3, (E, H, D), jnp.float32) * sH, 'w3': jax.random.normal(k4, (E, D, H), jnp.float32) * sD}
    _L0_ffn_in = _L0_ffn_setup()
    _d = {'L0_attn_a_x': _L0_attn_a_in['x'], 'L0_attn_a_qk_w': _L0_attn_a_in['qk_w'], 'L0_attn_a_qk_b': _L0_attn_a_in['qk_b'], 'L0_attn_a_lepe_w': _L0_attn_a_in['lepe_w'], 'L0_attn_a_lepe_b': _L0_attn_a_in['lepe_b'], 'L0_attn_b_ln1_w': _L0_attn_b_in['ln1_w'], 'L0_attn_b_ln1_b': _L0_attn_b_in['ln1_b'], 'L0_attn_b_ln2_w': _L0_attn_b_in['ln2_w'], 'L0_attn_b_ln2_b': _L0_attn_b_in['ln2_b'], 'L0_attn_b_time_decay': _L0_attn_b_in['time_decay'], 'L0_attn_b_time_first': _L0_attn_b_in['time_first'], 'L0_attn_b_time_mix_k': _L0_attn_b_in['time_mix_k'], 'L0_attn_b_time_mix_v': _L0_attn_b_in['time_mix_v'], 'L0_attn_b_time_mix_r': _L0_attn_b_in['time_mix_r'], 'L0_attn_b_w_key': _L0_attn_b_in['w_key'], 'L0_attn_b_w_value': _L0_attn_b_in['w_value'], 'L0_attn_b_w_recept': _L0_attn_b_in['w_recept'], 'L0_attn_b_w_output': _L0_attn_b_in['w_output'], 'L0_attn_b_f_time_mix_k': _L0_attn_b_in['f_time_mix_k'], 'L0_attn_b_f_time_mix_r': _L0_attn_b_in['f_time_mix_r'], 'L0_attn_b_f_w_key': _L0_attn_b_in['f_w_key'], 'L0_attn_b_f_w_recept': _L0_attn_b_in['f_w_recept'], 'L0_attn_b_f_w_value': _L0_attn_b_in['f_w_value'], 'L0_ffn_gate_w': _L0_ffn_in['gate_w'], 'L0_ffn_w1': _L0_ffn_in['w1'], 'L0_ffn_w2': _L0_ffn_in['w2'], 'L0_ffn_w3': _L0_ffn_in['w3']}
    _x0 = _d['L0_attn_a_x']
    _d['L0_attn_a_x'] = jax.random.normal(jax.random.fold_in(jax.random.key(seed), 1), (8, 512, 256), dtype=_x0.dtype)
    del _x0
    return _d

def reference(L0_attn_a_x, L0_attn_a_qk_w, L0_attn_a_qk_b, L0_attn_a_lepe_w, L0_attn_a_lepe_b, L0_attn_b_ln1_w, L0_attn_b_ln1_b, L0_attn_b_ln2_w, L0_attn_b_ln2_b, L0_attn_b_time_decay, L0_attn_b_time_first, L0_attn_b_time_mix_k, L0_attn_b_time_mix_v, L0_attn_b_time_mix_r, L0_attn_b_w_key, L0_attn_b_w_value, L0_attn_b_w_recept, L0_attn_b_w_output, L0_attn_b_f_time_mix_k, L0_attn_b_f_time_mix_r, L0_attn_b_f_w_key, L0_attn_b_f_w_recept, L0_attn_b_f_w_value, L0_ffn_gate_w, L0_ffn_w1, L0_ffn_w2, L0_ffn_w3):

    def _L0_attn_a_ref(x, qk_w, qk_b, lepe_w, lepe_b):
        import jax, jax.numpy as jnp
        import numpy as np
        NUM_HEADS = 8
        ROPE_BASE = 10000.0

        def _rope(x):
            b, n, c = x.shape
            k_max = c // 2
            theta = 1.0 / ROPE_BASE ** (jnp.arange(k_max, dtype=jnp.float32) / k_max)
            angles = jnp.arange(n, dtype=jnp.float32)[:, None] * theta
            cos = jnp.cos(angles)
            sin = jnp.sin(angles)
            xr = x[..., 0::2]
            xi = x[..., 1::2]
            pr = cos * xr - sin * xi
            pi = cos * xi + sin * xr
            return jnp.concatenate([pr, pi], axis=-1)
        b, n, c = x.shape
        h = NUM_HEADS
        d = c // h
        qk = x @ qk_w + qk_b
        q, k = jnp.split(qk, 2, axis=-1)
        q = jax.nn.elu(q) + 1.0
        k = jax.nn.elu(k) + 1.0
        q_rope = _rope(q)
        k_rope = _rope(k)

        def to_heads(t):
            return t.reshape(b, n, h, d).transpose(0, 2, 1, 3)
        qh = to_heads(q)
        kh = to_heads(k)
        qr = to_heads(q_rope)
        kr = to_heads(k_rope)
        vh = to_heads(x)
        k_mean = jnp.mean(kh, axis=2, keepdims=True)
        z = 1.0 / (jnp.einsum('bhnd,bhmd->bhnm', qh, k_mean) + 1e-06)
        kv = jnp.einsum('bhnd,bhne->bhde', kr, vh) * (1.0 / jnp.sqrt(jnp.float32(n)))
        out = jnp.einsum('bhnd,bhde->bhne', qr, kv) * z
        out = out.transpose(0, 2, 1, 3).reshape(b, n, c)
        lepe = jax.lax.conv_general_dilated(x, lepe_w, window_strides=(1,), padding='SAME', dimension_numbers=('NWC', 'WIO', 'NWC')) + lepe_b
        return out + lepe

    def _L0_attn_b_ref(x, ln1_w, ln1_b, ln2_w, ln2_b, time_decay, time_first, time_mix_k, time_mix_v, time_mix_r, w_key, w_value, w_recept, w_output, f_time_mix_k, f_time_mix_r, f_w_key, f_w_recept, f_w_value):
        import jax, jax.numpy as jnp
        import numpy as np
        B, T, D = (4, 1024, 256)
        F = 4 * D
        EPS_INIT = -1e+30

        def layer_norm(x, w, b, eps=1e-05):
            mu = jnp.mean(x, axis=-1, keepdims=True)
            var = jnp.var(x, axis=-1, keepdims=True)
            return (x - mu) * jax.lax.rsqrt(var + eps) * w + b

        def time_shift(x):
            return jnp.concatenate([jnp.zeros_like(x[:, :1]), x[:, :-1]], axis=1)

        def wkv(w, u, k, v):
            bsz, _, dim = k.shape
            alpha0 = jnp.zeros((bsz, dim), k.dtype)
            beta0 = jnp.zeros((bsz, dim), k.dtype)
            eps0 = jnp.full((bsz, dim), EPS_INIT, k.dtype)

            def step(carry, kv_t):
                alpha, beta, eps = carry
                kt, vt = kv_t
                ukt = u + kt
                tau = jnp.maximum(ukt, eps)
                e1 = jnp.exp(eps - tau)
                e2 = jnp.exp(ukt - tau)
                out = (e1 * alpha + e2 * vt) / (e1 * beta + e2)
                weps = eps - w
                tau2 = jnp.maximum(weps, kt)
                d1 = jnp.exp(weps - tau2)
                d2 = jnp.exp(kt - tau2)
                return ((d1 * alpha + d2 * vt, d1 * beta + d2, tau2), out)
            kT = jnp.swapaxes(k, 0, 1)
            vT = jnp.swapaxes(v, 0, 1)
            _, outT = jax.lax.scan(step, (alpha0, beta0, eps0), (kT, vT))
            return jnp.swapaxes(outT, 0, 1)
        xn = layer_norm(x, ln1_w, ln1_b)
        lx = time_shift(xn)
        k = (xn * time_mix_k + lx * (1.0 - time_mix_k)) @ w_key
        v = (xn * time_mix_v + lx * (1.0 - time_mix_v)) @ w_value
        r = (xn * time_mix_r + lx * (1.0 - time_mix_r)) @ w_recept
        sr = jax.nn.sigmoid(r)
        w = jnp.exp(time_decay)
        out = wkv(w, time_first, k, v)
        x = x + out * sr @ w_output
        xn2 = layer_norm(x, ln2_w, ln2_b)
        lx2 = time_shift(xn2)
        fk = (xn2 * f_time_mix_k + lx2 * (1.0 - f_time_mix_k)) @ f_w_key
        fr = (xn2 * f_time_mix_r + lx2 * (1.0 - f_time_mix_r)) @ f_w_recept
        vk = jnp.square(jax.nn.relu(fk)) @ f_w_value
        x = x + jax.nn.sigmoid(fr) * vk
        return x

    def _L0_ffn_ref(hidden_states, gate_w, w1, w2, w3):
        import jax, jax.numpy as jnp
        import numpy as np
        E, K, D, H = (8, 2, 256, 512)
        B, S = (1, 256)

        def _grouped_swiglu(x_sorted, counts, w1, w2, w3):
            if hasattr(jax.lax, 'ragged_dot'):
                gs = counts.astype(jnp.int32)
                h = jax.nn.silu(jax.lax.ragged_dot(x_sorted, w1, gs)) * jax.lax.ragged_dot(x_sorted, w3, gs)
                return jax.lax.ragged_dot(h, w2, gs)
            pos = jnp.arange(x_sorted.shape[0])
            eid = jnp.searchsorted(jnp.cumsum(counts), pos, side='right')
            out = jnp.zeros((x_sorted.shape[0], w2.shape[-1]), x_sorted.dtype)
            for e in range(w1.shape[0]):
                xm = jnp.where((eid == e)[:, None], x_sorted, 0.0)
                he = jax.nn.silu(xm @ w1[e]) * (xm @ w3[e])
                out = out + he @ w2[e]
            return out
        x = hidden_states.reshape(-1, D)
        N = x.shape[0]
        scores = jax.nn.softmax(x @ gate_w.T, axis=-1)
        top_scores, sel = jax.lax.top_k(scores, K)
        sel_flat = sel.T.reshape(-1)
        scores_flat = top_scores.T.reshape(-1)
        order = jnp.argsort(sel_flat, stable=True)
        tok_sorted = order % N
        scores_sorted = scores_flat[order]
        counts = jnp.bincount(sel_flat, length=E)
        x_sorted = x[tok_sorted]
        y = _grouped_swiglu(x_sorted, counts, w1, w2, w3)
        weighted = y * scores_sorted[:, None]
        out = jnp.zeros((N, D), x.dtype).at[tok_sorted].add(weighted)
        return out.reshape(hidden_states.shape)
    x = L0_attn_a_x
    x = x + _L0_attn_a_ref(_layernorm(x, axis=-1), L0_attn_a_qk_w, L0_attn_a_qk_b, L0_attn_a_lepe_w, L0_attn_a_lepe_b)
    x = x + _L0_ffn_ref(_layernorm(x, axis=-1), L0_ffn_gate_w, L0_ffn_w1, L0_ffn_w2, L0_ffn_w3)
    x = x + _L0_attn_b_ref(_layernorm(x, axis=-1), L0_attn_b_ln1_w, L0_attn_b_ln1_b, L0_attn_b_ln2_w, L0_attn_b_ln2_b, L0_attn_b_time_decay, L0_attn_b_time_first, L0_attn_b_time_mix_k, L0_attn_b_time_mix_v, L0_attn_b_time_mix_r, L0_attn_b_w_key, L0_attn_b_w_value, L0_attn_b_w_recept, L0_attn_b_w_output, L0_attn_b_f_time_mix_k, L0_attn_b_f_time_mix_r, L0_attn_b_f_w_key, L0_attn_b_f_w_recept, L0_attn_b_f_w_value)
    x = x + _L0_ffn_ref(_layernorm(x, axis=-1), L0_ffn_gate_w, L0_ffn_w1, L0_ffn_w2, L0_ffn_w3)
    return x

_drawn_inputs = setup_inputs


def setup_inputs(seed=0):
    import zlib

    import numpy as np

    out = dict(_drawn_inputs(seed))
    spreads = {'L0_attn_a_qk_b': (0.0, 0.379),
     'L0_attn_a_lepe_b': (0.0, 0.1),
     'L0_attn_b_ln1_w': (1.0, 0.6),
     'L0_attn_b_ln1_b': (0.0, 0.8),
     'L0_attn_b_ln2_w': (1.0, 0.6),
     'L0_attn_b_ln2_b': (0.0, 0.8)}
    factors = {'L0_attn_b_time_decay': 8.0,
     'L0_attn_b_time_first': 8.0,
     'L0_attn_b_time_mix_k': 8.0,
     'L0_attn_b_time_mix_v': 8.0,
     'L0_attn_b_time_mix_r': 8.0,
     'L0_attn_b_w_key': 8.0,
     'L0_attn_b_w_value': 3.761,
     'L0_attn_b_w_recept': 8.0,
     'L0_attn_b_w_output': 3.681,
     'L0_attn_b_f_time_mix_k': 8.0,
     'L0_attn_b_f_time_mix_r': 8.0,
     'L0_attn_b_f_w_key': 4.434,
     'L0_attn_b_f_w_recept': 8.0,
     'L0_attn_b_f_w_value': 4.017}
    for name, (base, spread) in spreads.items():
        noise = np.random.default_rng([zlib.crc32(name.encode()), seed]).standard_normal(out[name].shape)
        drawn = base * np.exp(spread * noise) if base else spread * noise
        out[name] = jnp.asarray(drawn.astype(out[name].dtype))
    for name, factor in factors.items():
        out[name] = (out[name] * factor).astype(out[name].dtype)
    return out
```

```python
import concourse.bass as bass
from concourse import mybir
from contextlib import ExitStack

F32 = mybir.dt.float32
I32 = mybir.dt.int32
U32 = mybir.dt.uint32
ALU = mybir.AluOpType
ACT = mybir.ActivationFunctionType
AXX = mybir.AxisListType.X

P = 128
B, N, C = 8, 512, 256
TB = N // P
T = B * TB
KC = C // P
HEADS, HD = 8, C // 8
LT = 3
EX, H = 8, 512
HC = H // P
TOPK = 2
NBLK = TOPK * B * N // P + EX - 1
F = 4 * C
FCH = F // P
EPS = 1e-5
EPS_INIT = -1e30


def over_batches(engine, body):
    body(0, 0)
    with engine.Fori(1, B - 2, 2) as b:
        body(b, 1)
        body(b + 1, 0)
    body(B - 1, 1)


def is_first(b):
    return isinstance(b, int) and b == 0


def is_last(b):
    return isinstance(b, int) and b == B - 1


def wait_count(engine, sem, value):
    if isinstance(value, int) and value <= 0:
        return
    engine.wait_ge(sem, value)


def wait_apart(engine, sem, value, passed):
    wait_count(engine, sem, value)
    engine.sem_inc(passed, 1)


class OwnSteps:

    def __init__(self, engine, sem, per_round):
        self.engine, self.sem, self.per_round = engine, sem, per_round
        self.base, self.k = 0, 0

    def round(self, r):
        assert self.k in (0, self.per_round), (self.k, self.per_round)
        self.base, self.k = r * self.per_round, 0

    def link(self, ins, passed=None):
        self.k += 1
        ins.then_inc(self.sem, 1)
        self.engine.wait_ge(self.sem, self.base + self.k)
        if passed is not None:
            self.engine.sem_inc(passed, 1)

    def pad(self):
        while self.k < self.per_round:
            self.k += 1
            self.engine.sem_inc(self.sem, 1)


def sequence_tiles(x, b):
    return x[:, bass.ds(b * TB, TB)] if not isinstance(b, int) else x[:, b * TB:(b + 1) * TB]


def tile_of(x, b, j):
    if isinstance(b, int):
        return x[:, b * TB + j, :]
    return x[:, bass.ds(b * TB + j, 1), :].rearrange("p a c -> p (a c)")


def stage_constants(nc, ident, head_mask, block_mask, neg_half):
    with ExitStack() as ctx:
        made = ctx.enter_context(nc.semaphore("const_made"))
        block = ctx.enter_context(nc.Block())

        @block.gpsimd
        def _(pool):
            nc.gpsimd.memset(neg_half[:], -0.5).then_inc(made, 1)
            nc.gpsimd.memset(ident[:], 0.0).then_inc(made, 1)
            nc.gpsimd.memset(head_mask[:], 1.0 / N).then_inc(made, 1)
            nc.gpsimd.memset(block_mask[:], 1.0 / float(N) ** 0.5).then_inc(made, 1)
            pool.wait_ge(made, 4)
            nc.gpsimd.affine_select(out=ident[:], in_=ident[:], compare_op=ALU.not_equal, fill=1.0, base=0,
                                    pattern=[[-1, P]], channel_multiplier=1).then_inc(made, 1)
            pair = HD // 2
            nc.gpsimd.affine_select(out=head_mask[:], in_=head_mask[:], compare_op=ALU.is_ge, fill=0.0, base=0,
                                    pattern=[[-pair, HEADS]], channel_multiplier=1).then_inc(made, 1)
            bm = block_mask[:].rearrange("p (g e) -> p g e", e=HD)
            nc.gpsimd.affine_select(out=bm, in_=bm, compare_op=ALU.is_ge, fill=0.0, base=0,
                                    pattern=[[-HD, P // HD], [0, HD]], channel_multiplier=1).then_inc(made, 1)
            pool.wait_ge(made, 7)
            nc.gpsimd.affine_select(out=head_mask[:], in_=head_mask[:], compare_op=ALU.is_ge, fill=0.0,
                                    base=pair - 1, pattern=[[pair, HEADS]], channel_multiplier=-1).then_inc(made, 1)
            nc.gpsimd.affine_select(out=bm, in_=bm, compare_op=ALU.is_ge, fill=0.0, base=HD - 1,
                                    pattern=[[HD, P // HD], [0, HD]], channel_multiplier=-1).then_inc(made, 1)
            pool.wait_ge(made, 9)


def phase_attention(nc, x_dram, qk_w, qk_b, lepe_w, lepe_b, gate_w, cos_t, sin_t,
                    x, stat_all, logits, ident, head_mask, block_mask, neg_half, bank):
    tb0, tb1, q0, q1, q2, q3, l0, l1 = bank
    q, tbk, lb = [q0, q1, q2, q3], [tb0, tb1], [l0, l1]
    ORDER = (2, 3, 0, 1)
    with ExitStack() as ctx:
        def sb(name, shape, dt=F32):
            return ctx.enter_context(nc.sbuf_tensor(name, shape, dt))

        def sem(name):
            return ctx.enter_context(nc.semaphore(name))

        qk_raw = sb("a_qk_raw", [P, KC, 2 * C])
        qk_s = sb("a_qk_s", [P, KC, 4, P])
        qk_bias = sb("a_qk_bias", [P, 4])
        lepe_s = sb("a_lepe_s", [P, LT, KC, C])
        lepe_bias = sb("a_lepe_bias", [P, 1, C])
        gate_s = sb("a_gate_s", [P, KC, EX])
        cos_s = sb("a_cos", [P, 1, N])
        sin_s = sb("a_sin", [P, N])
        nsin_s = sb("a_nsin", [P, N])
        bn = sb("a_bn", [P, TB, 6])
        mv = sb("a_mv", [P, TB, 2])
        bn2 = sb("a_bn2", [P, TB, 6])
        mv2 = sb("a_mv2", [P, TB, 2])
        xn = [sb(f"a_xn{i}", [P, TB, C]) for i in range(2)]
        xnT = sb("a_xnT", [P, KC, N + 2])
        ex = sb("a_ex", [P, 4, N])
        re = sb("a_re", [P, 4, N])
        el = sb("a_el", [P, 4, N])
        ksum = sb("a_ksum", [P, 2])
        kz = sb("a_kz", [P, 2, HEADS])
        kA = sb("a_kA", [P, 2, N])
        kB = sb("a_kB", [P, 2, N])
        kr = sb("a_kr", [P, 2, N])
        qA = sb("a_qA", [P, 2, N])
        qB = sb("a_qB", [P, 2, N])
        qr = sb("a_qr", [P, 2, N])
        krt = sb("a_krt", [P, KC, TB, P])
        kvb = sb("a_kvb", [P, KC, P])
        zr = sb("a_zr", [P, TB * HEADS])
        u = sb("a_u", [P, 2, N])
        v = sb("a_v", [P, 2, 2, C])
        xg = sb("a_xg", [P, TB, C])
        xgT = sb("a_xgT", [P, KC, N])

        x0_in, x_in, w_in, wg_in, tab_in = sem("a_x0_in"), sem("a_x_in"), sem("a_w_in"), sem("a_wg_in"), sem("a_tab_in")
        own_dve, own_pool = sem("a_own_dve"), sem("a_own_pool")
        var_ready, rstd_ready, xn_ready = sem("a_var_ready"), sem("a_rstd_ready"), sem("a_xn_ready")
        qk_done, qk_evac, q_ready, kr_ready, qr_ready = (sem("a_qk_done"), sem("a_qk_evac"), sem("a_q_ready"),
                                                         sem("a_kr_ready"), sem("a_qr_ready"))
        t_filled, t_emptied = sem("a_t_filled"), sem("a_t_emptied")
        lepe_done, kv_done, z_done, attn_done, kvb_ready = (sem("a_lepe_done"), sem("a_kv_done"), sem("a_z_done"),
                                                            sem("a_attn_done"), sem("a_kvb_ready"))
        v_ready, x1_ready = sem("a_v_ready"), sem("a_x1_ready")
        var2_ready, rstd2_ready, xg_ready = sem("a_var2_ready"), sem("a_rstd2_ready"), sem("a_xg_ready")
        w_ready = sem("a_w_ready")
        passed_dve, passed_pool = sem("a_passed_dve"), sem("a_passed_pool")
        block = ctx.enter_context(nc.Block())

        def round_gate(b):
            return 4 * b - 1 if not (isinstance(b, int) and b == B) else 4 * B - 2

        def round_next(b):
            return 4 * b + 1

        def round_k(b):
            return 4 * b + 2 if not is_last(b) else 4 * b + 1

        @block.sync
        def _(sp):
            xv = x_dram.rearrange("b (t p) c -> p (b t) c", p=P)
            sp.dma_start(x[:, 0:TB, :], xv[:, 0:TB, :]).then_inc(x0_in, 16)
            sp.dma_start(qk_raw[:], qk_w.rearrange("(k p) n -> p k n", p=P)).then_inc(w_in, 16)
            sp.dma_start(qk_bias[:].rearrange("p (h two) -> p h two", two=2),
                         qk_b.rearrange("(h i two) -> i h two", h=2, two=2)).then_inc(w_in, 16)
            sp.dma_start(x[:, TB:, :], xv[:, TB:, :]).then_inc(x_in, 16)

        @block.scalar
        def _(act):
            act.dma_start(lepe_s[:], lepe_w.rearrange("t (k p) n -> p t k n", p=P)).then_inc(w_in, 16)
            act.dma_start(lepe_bias[:, 0, :], lepe_b.partition_broadcast(P)).then_inc(tab_in, 16)
            act.dma_start(cos_s[:, 0, :], cos_t).then_inc(tab_in, 16)
            act.dma_start(sin_s[:], sin_t).then_inc(tab_in, 16)
            for k in range(KC):
                act.dma_start(gate_s[:, k, :], gate_w[:, k * P:(k + 1) * P].rearrange("e p -> p e"),
                              allow_slow_non_contiguous=True).then_inc(wg_in, 16)

            def evacuate_next(r):
                act.wait_ge(t_filled, r + 1)
                for k in range(KC):
                    last = nc.scalar.activation(xnT[:, k, 1:N + 1], tbk[k][:], ACT.Copy)
                last.then_inc(t_emptied, 1)

            def gate_part(b):
                r = round_gate(b)
                act.wait_ge(t_filled, r + 1)
                for k in range(KC):
                    last = nc.scalar.activation(xgT[:, k, :], tbk[k][:], ACT.Copy)
                last.then_inc(t_emptied, 1)
                act.wait_ge(t_filled, r + 2)
                nc.scalar.activation(sequence_tiles(logits, b - 1),
                                     tb0[:, 0:TB * EX].rearrange("p (t e) -> p t e", e=EX),
                                     ACT.Copy).then_inc(t_emptied, 1)

            evacuate_next(0)
            act.wait_ge(w_in, 48)

            def period(b, par):
                wait_count(act, q_ready, b)
                for n, m in enumerate(ORDER):
                    act.wait_ge(qk_done, 4 * b + n + 1)
                    nc.scalar.activation(ex[:, m, :], q[m][:], ACT.Exp, bias=qk_bias[:, m:m + 1])
                    nc.scalar.activation(re[:, m, :], q[m][:], ACT.Relu, bias=qk_bias[:, m:m + 1]).then_inc(qk_evac, 1)
                if not is_first(b):
                    gate_part(b)
                if not is_last(b):
                    evacuate_next(round_next(b))
                act.wait_ge(t_filled, round_k(b) + 1)
                for k in range(KC):
                    last = nc.scalar.activation(krt[:, k, :, :].rearrange("p t d -> p (t d)"), tbk[k][:], ACT.Copy)
                last.then_inc(t_emptied, 1)

            over_batches(act, period)
            gate_part(B)

        @block.gpsimd
        def _(pool):
            own = OwnSteps(pool, own_pool, 4)

            def rstd(mvt, ready, done):
                own.link(nc.gpsimd.tensor_scalar(mvt[:, :, 1], mvt[:, :, 1], EPS, None, ALU.add))
                nc.gpsimd.tensor_tensor(mvt[:, :, 1], mvt[:, :, 1], neg_half[:, 0:TB], ALU.pow).then_inc(done, 1)

            def add_bias(b):
                xt = sequence_tiles(x, b)
                nc.gpsimd.tensor_tensor(xt, xt, lepe_bias[:].to_broadcast([P, TB, C]), ALU.add)

            own.round(0)
            pool.wait_ge(var_ready, 1)
            rstd(mv, var_ready, rstd_ready)
            pool.wait_ge(tab_in, 48)
            pool.wait_ge(xn_ready, 1)
            add_bias(0)
            own.pad()

            def period(b, par):
                own.round(b + 1)
                if not is_last(b):
                    wait_apart(pool, var_ready, b + 2, passed_pool)
                    rstd(mv, var_ready, rstd_ready)
                if not is_first(b):
                    wait_apart(pool, var2_ready, b, passed_pool)
                    rstd(mv2, var2_ready, rstd2_ready)
                pool.wait_ge(q_ready, b + 1)
                wait_count(pool, attn_done, 2 * b)
                nc.gpsimd.tensor_tensor(qA[:], el[:, 0:2, :], cos_s[:].to_broadcast([P, 2, N]), ALU.mult)
                nc.gpsimd.tensor_tensor(qB[:, 0, :], el[:, 1, :], nsin_s[:], ALU.mult)
                own.link(nc.gpsimd.tensor_tensor(qB[:, 1, :], el[:, 0, :], sin_s[:], ALU.mult))
                nc.gpsimd.tensor_tensor(qr[:], qA[:], qB[:], ALU.add).then_inc(qr_ready, 1)
                if not is_last(b):
                    wait_apart(pool, xn_ready, b + 2, passed_pool)
                    add_bias(b + 1)
                for h in range(2):
                    wait_apart(pool, v_ready, 2 * b + h + 1, passed_pool)
                    xt = x[:, bass.ds(b * TB + 2 * h, 2), :] if not isinstance(b, int) else x[:, b * TB + 2 * h:b * TB + 2 * h + 2, :]
                    nc.gpsimd.tensor_tensor(xt, xt, v[:, h, :, :], ALU.add).then_inc(x1_ready, 1)
                own.pad()

            over_batches(pool, period)
            own.round(B + 1)
            pool.wait_ge(var2_ready, B)
            rstd(mv2, var2_ready, rstd2_ready)

        @block.vector
        def _(dve):
            own = OwnSteps(dve, own_dve, 8)

            def statistics(bnt, mvt, b, done):
                for j in range(TB):
                    last = nc.vector.bn_stats(bnt[:, j, :], tile_of(x, b, j))
                own.link(last, passed_dve)
                for j in range(TB):
                    last = nc.vector.bn_aggr(mvt[:, j, :], bnt[:, j, :])
                last.then_inc(done, 1)

            def normalise(dst, mvt, b, done):
                for j in range(TB):
                    last = nc.vector.tensor_scalar(dst[:, j, :], tile_of(x, b, j), mvt[:, j, 0:1], mvt[:, j, 1:2],
                                                   ALU.subtract, ALU.mult)
                last.then_inc(done, 1)

            own.round(0)
            nc.vector.memset(xnT[:, :, 0:1], 0.0)
            nc.vector.memset(xnT[:, :, N + 1:N + 2], 0.0)
            dve.wait_ge(x0_in, 16)
            statistics(bn, mv, 0, var_ready)
            dve.wait_ge(w_in, 48)
            for h in range(2):
                for par in range(2):
                    last = nc.vector.tensor_copy(qk_s[:, :, 2 * h + par, :],
                                                 qk_raw[:, :, h * C + par:(h + 1) * C:2])
            last.then_inc(w_ready, 1)
            dve.wait_ge(rstd_ready, 1)
            normalise(xn[0], mv, 0, xn_ready)
            dve.wait_ge(tab_in, 48)
            own.link(nc.vector.tensor_scalar(nsin_s[:], sin_s[:], -1.0, None, ALU.mult))
            dve.wait_ge(x_in, 16)
            own.pad()

            def route_before(b):
                dve.wait_ge(rstd2_ready, b)
                nc.vector.tensor_copy(sequence_tiles(stat_all, b - 1), mv2[:])
                normalise(xg, mv2, b - 1, xg_ready)

            def period(b, par):
                own.round(b + 1)
                if not is_last(b):
                    statistics(bn, mv, b + 1, var_ready)
                if not is_first(b):
                    dve.wait_ge(x1_ready, 2 * b)
                    statistics(bn2, mv2, b - 1, var2_ready)
                dve.wait_ge(qk_evac, 4 * b + 2)
                for m in (2, 3):
                    last = nc.vector.scalar_tensor_tensor(out=el[:, m, :], in0=ex[:, m, :], scalar=1.0, in1=re[:, m, :],
                                                          op0=ALU.min, op1=ALU.add, accum_out=ksum[:, m - 2:m - 1])
                own.link(last)
                for m in range(2):
                    nc.vector.tensor_scalar(kz[:, m, :], head_mask[:], ksum[:, m:m + 1], None, ALU.mult)
                nc.vector.tensor_tensor(kA[:], el[:, 2:4, :], cos_s[:].to_broadcast([P, 2, N]), ALU.mult)
                nc.vector.tensor_tensor(kB[:, 0, :], el[:, 3, :], nsin_s[:], ALU.mult)
                own.link(nc.vector.tensor_tensor(kB[:, 1, :], el[:, 2, :], sin_s[:], ALU.mult))
                nc.vector.tensor_tensor(kr[:], kA[:], kB[:], ALU.add).then_inc(kr_ready, 1)
                dve.wait_ge(qk_evac, 4 * b + 4)
                wait_count(dve, qr_ready, b)
                nc.vector.scalar_tensor_tensor(out=el[:, 0:2, :], in0=ex[:, 0:2, :], scalar=1.0, in1=re[:, 0:2, :],
                                               op0=ALU.min, op1=ALU.add).then_inc(q_ready, 1)
                if not is_first(b):
                    route_before(b)
                if not is_last(b):
                    dve.wait_ge(rstd_ready, b + 2)
                    normalise(xn[1 - par], mv, b + 1, xn_ready)
                dve.wait_ge(kv_done, b + 1)
                nc.vector.tensor_tensor(kvb[:], q0[:, 0:C].rearrange("p (k e) -> p k e", k=KC),
                                        block_mask[:].unsqueeze(1).to_broadcast([P, KC, P]), ALU.mult).then_inc(kvb_ready, 1)
                dve.wait_ge(z_done, b + 1)
                own.link(nc.vector.tensor_scalar(zr[:], q1[:, 0:TB * HEADS], 1e-6, None, ALU.add))
                own.link(nc.vector.reciprocal(zr[:], zr[:]))
                dve.wait_ge(lepe_done, 2 * b + 2)
                for h in range(2):
                    dve.wait_ge(attn_done, 2 * b + h + 1)
                    zb = zr[:, h * 2 * HEADS:(h + 1) * 2 * HEADS].unsqueeze(2).to_broadcast([P, 2 * HEADS, HD])
                    own.link(nc.vector.tensor_tensor(u[:, h, :].rearrange("p (g e) -> p g e", e=HD),
                                                     q[2 + h][:].rearrange("p (g e) -> p g e", e=HD), zb, ALU.mult))
                    wait_count(dve, x1_ready, 2 * b + h - 1)
                    nc.vector.tensor_tensor(v[:, h, :, :].rearrange("p t c -> p (t c)"), u[:, h, :], lb[h][:],
                                            ALU.add).then_inc(v_ready, 1)
                own.pad()

            over_batches(dve, period)
            own.round(B + 1)
            dve.wait_ge(x1_ready, 2 * B)
            statistics(bn2, mv2, B - 1, var2_ready)
            route_before(B)
            own.pad()

        @block.tensor
        def _(pe):
            def transposes(src, filled_round):
                wait_count(pe, t_emptied, filled_round)
                for k in range(KC):
                    for j in range(TB):
                        last = nc.tensor.transpose(tbk[k][:, j * P:(j + 1) * P], src[:, j, k * P:(k + 1) * P], ident[:])
                last.then_inc(t_filled, 1)

            def gate_part(b):
                r = round_gate(b)
                pe.wait_ge(xg_ready, b)
                transposes(xg, r)
                pe.wait_ge(t_emptied, r + 1)
                for j in range(TB):
                    for k in range(KC):
                        last = nc.tensor.matmul(tb0[:, j * EX:(j + 1) * EX], xgT[:, k, j * P:(j + 1) * P], gate_s[:, k, :],
                                                start=(k == 0), stop=(k == KC - 1))
                last.then_inc(t_filled, 1)

            pe.wait_ge(xn_ready, 1)
            transposes(xn[0], 0)
            pe.wait_ge(w_ready, 1)
            pe.wait_ge(w_in, 48)
            pe.wait_ge(wg_in, 16 * KC)

            def period(b, par):
                pe.wait_ge(t_emptied, round_next(b - 1) + 1 if not is_first(b) else 1)
                wait_count(pe, v_ready, 2 * b)
                for m in ORDER:
                    for k in range(KC):
                        last = nc.tensor.matmul(q[m][:], qk_s[:, k, m, :], xnT[:, k, 1:N + 1], start=(k == 0), stop=(k == KC - 1))
                    last.then_inc(qk_done, 1)
                for j in range(TB):
                    n = 0
                    for t in range(LT):
                        for k in range(KC):
                            last = nc.tensor.matmul(lb[j // 2][:, (j % 2) * C:(j % 2 + 1) * C],
                                                    xnT[:, k, j * P + t:j * P + t + P], lepe_s[:, t, k, :],
                                                    start=(n == 0), stop=(n == LT * KC - 1))
                            n += 1
                    if j % 2:
                        last.then_inc(lepe_done, 1)
                if not is_first(b):
                    gate_part(b)
                if not is_last(b):
                    pe.wait_ge(xn_ready, b + 2)
                    transposes(xn[1 - par], round_next(b))
                pe.wait_ge(kr_ready, b + 1)
                pe.wait_ge(t_emptied, round_k(b))
                for k in range(KC):
                    for j in range(TB):
                        last = nc.tensor.transpose(tbk[k][:, j * P:(j + 1) * P], kr[:, k, j * P:(j + 1) * P], ident[:])
                last.then_inc(t_filled, 1)
                pe.wait_ge(q_ready, b + 1)
                for j in range(TB):
                    for m in range(2):
                        last = nc.tensor.matmul(q1[:, j * HEADS:(j + 1) * HEADS], el[:, m, j * P:(j + 1) * P], kz[:, m, :],
                                                start=(m == 0), stop=(m == 1))
                last.then_inc(z_done, 1)
                pe.wait_ge(t_emptied, round_k(b) + 1)
                for k in range(KC):
                    for j in range(TB):
                        last = nc.tensor.matmul(q0[:, k * P:(k + 1) * P], krt[:, k, j, :], xn[par][:, j, k * P:(k + 1) * P],
                                                start=(j == 0), stop=(j == TB - 1))
                last.then_inc(kv_done, 1)
                pe.wait_ge(kvb_ready, b + 1)
                pe.wait_ge(qr_ready, b + 1)
                for j in range(TB):
                    for k in range(KC):
                        last = nc.tensor.matmul(q[2 + j // 2][:, (j % 2) * C + k * P:(j % 2) * C + (k + 1) * P],
                                                qr[:, k, j * P:(j + 1) * P], kvb[:, k, :], start=True, stop=True)
                    if j % 2:
                        last.then_inc(attn_done, 1)

            over_batches(pe, period)
            gate_part(B)


def phase_route(nc, tag, x, stat_all, logits, xs_dram, score, pos, block_expert, bank):
    BLOCKS = NBLK
    with ExitStack() as ctx:
        def sb(name, shape, dt=F32):
            return ctx.enter_context(nc.sbuf_tensor(name, shape, dt))

        def sem(name):
            return ctx.enter_context(nc.semaphore(name))

        top = sb(tag + "r_top", [P, T, 8])
        topi = sb(tag + "r_topi", [P, T, 8], U32)
        idx = sb(tag + "r_idx", [P, TOPK, T])
        diff = sb(tag + "r_diff", [P, T, EX])
        prob = sb(tag + "r_prob", [P, T, EX])
        d2 = sb(tag + "r_d2", [P, T])
        p2 = sb(tag + "r_p2", [P, T])
        tot_p = sb(tag + "r_tot_p", [P, T])
        rz = sb(tag + "r_rz", [P, T])
        expert_id = sb(tag + "r_expert_id", [P, EX, T])
        keep = sb(tag + "r_keep", [P, EX * T])
        ones_e = sb(tag + "r_ones_e", [P, EX])
        hot = sb(tag + "r_hot", [P, TOPK, EX, T])
        both = sb(tag + "r_both", [P, EX, T])
        before = sb(tag + "r_before", [P, P])
        ones = sb(tag + "r_ones", [P, P])
        tot = sb(tag + "r_tot", [P, EX, T])
        incl = sb(tag + "r_incl", [P, EX, T])
        counti = sb(tag + "r_counti", [P, EX], I32)
        padded = sb(tag + "r_padded", [P, EX])
        endp = sb(tag + "r_endp", [P, EX])
        base = sb(tag + "r_base", [P, EX, 1])
        place = sb(tag + "r_place", [P, EX, T])
        prod = sb(tag + "r_prod", [P, TOPK, EX, T])
        posf = sb(tag + "r_posf", [P, TOPK, T])
        row0 = sb(tag + "r_row0", [1, BLOCKS, EX])
        past = sb(tag + "r_past", [1, BLOCKS, EX])
        ebf = sb(tag + "r_ebf", [1, BLOCKS])
        RING = 4
        xs = sb(tag + "r_xs", [P, RING, C])
        own_dve, made, top_ready, exp_done, both_ready, count_done, pos_ready = (
            sem(tag + "r_own_dve"), sem(tag + "r_made"), sem(tag + "r_top_ready"), sem(tag + "r_exp_done"), sem(tag + "r_both_ready"),
            sem(tag + "r_count_done"), sem(tag + "r_pos_ready"))
        xs_ready = sem(tag + "r_xs_ready")
        scattered = [sem(tag + f"r_scattered{i}") for i in range(RING)]
        block = ctx.enter_context(nc.Block())

        @block.gpsimd
        def _(pool):
            nc.gpsimd.iota(expert_id[:], pattern=[[1, EX], [0, T]], base=0, channel_multiplier=0,
                           allow_small_or_imprecise_dtypes=True).then_inc(made, 1)
            nc.gpsimd.iota(row0[:], pattern=[[P, BLOCKS], [0, EX]], base=0, channel_multiplier=0,
                           allow_small_or_imprecise_dtypes=True).then_inc(made, 1)
            nc.gpsimd.memset(keep[:], 1.0).then_inc(made, 1)
            nc.gpsimd.memset(ones_e[:], 1.0).then_inc(made, 1)
            nc.gpsimd.memset(ones[:], 1.0).then_inc(made, 1)
            nc.gpsimd.memset(before[:], 1.0).then_inc(made, 1)
            pool.wait_ge(made, 6)
            nc.gpsimd.memset(keep[:].rearrange("p (e t) -> p e t", t=T)[:, :, 0:1], 0.0).then_inc(made, 1)
            nc.gpsimd.affine_select(out=before[:], in_=before[:], compare_op=ALU.is_ge, fill=0.0, base=-1,
                                    pattern=[[1, P]], channel_multiplier=-1).then_inc(made, 1)
            pool.wait_ge(pos_ready, 1)
            for t in range(T):
                pool.wait_ge(xs_ready, t + 1)
                for k in range(TOPK):
                    nc.gpsimd.indirect_dma_start(
                        xs_dram[:], bass.IndirectOffsetOnAxis(ap=pos[:, k, t:t + 1], axis=0),
                        xs[:, t % RING, :], None).then_inc(scattered[t % RING], 16)
            for r in range(RING):
                pool.wait_ge(scattered[r], 16 * TOPK * (T // RING))

        @block.scalar
        def _(act):
            act.wait_ge(top_ready, 1)
            nc.scalar.activation(prob[:], diff[:], ACT.Exp)
            nc.scalar.activation(p2[:], d2[:], ACT.Exp).then_inc(exp_done, 1)

        @block.tensor
        def _(pe):
            pe.wait_ge(made, 8)
            pe.wait_ge(both_ready, 1)
            m = both[:].rearrange("p e t -> p (e t)")
            nc.tensor.matmul(bank[0][:, 0:EX * T], before[:], m, start=True, stop=True)
            nc.tensor.matmul(bank[1][:, 0:EX * T], ones[:], m, start=True, stop=True).then_inc(count_done, 1)

        @block.vector
        def _(dve):
            own = OwnSteps(dve, own_dve, 0)
            for t in range(T):
                last = nc.vector.max(top[:, t, :], logits[:, t, :])
            own.link(last)
            for t in range(T):
                last = nc.vector.max_index(topi[:, t, :], top[:, t, :], logits[:, t, :])
            nc.vector.tensor_tensor(d2[:], top[:, :, 1], top[:, :, 0], ALU.subtract)
            nc.vector.tensor_tensor(diff[:], logits[:], top[:, :, 0:1].to_broadcast([P, T, EX]),
                                    ALU.subtract).then_inc(top_ready, 1)
            dve.wait_ge(top_ready, 1)
            own.link(nc.vector.tensor_copy(idx[:], topi[:, :, 0:TOPK].rearrange("p t k -> p k t")))
            dve.wait_ge(made, 8)
            for k in range(TOPK):
                last = nc.vector.tensor_tensor(hot[:, k, :, :], idx[:, k:k + 1, :].to_broadcast([P, EX, T]),
                                               expert_id[:], ALU.is_equal)
            own.link(last)
            nc.vector.tensor_tensor(both[:], hot[:, 0, :, :], hot[:, 1, :, :], ALU.add).then_inc(both_ready, 1)
            dve.wait_ge(exp_done, 1)
            own.link(nc.vector.tensor_reduce(tot_p[:], prob[:], AXX, ALU.add))
            own.link(nc.vector.reciprocal(rz[:], tot_p[:]))
            nc.vector.tensor_copy(score[:, 0, :], rz[:])
            nc.vector.tensor_tensor(score[:, 1, :], p2[:], rz[:], ALU.mult)
            dve.wait_ge(count_done, 1)
            own.link(nc.vector.tensor_copy(tot[:].rearrange("p e t -> p (e t)"), bank[1][:, 0:EX * T]))
            own.link(nc.vector.tensor_tensor_scan(incl[:].rearrange("p e t -> p (e t)"), keep[:],
                                                  tot[:].rearrange("p e t -> p (e t)"), 0.0, ALU.mult, ALU.add))
            own.link(nc.vector.tensor_scalar(counti[:], incl[:, :, T - 1], float(P - 1), None, ALU.add))
            own.link(nc.vector.tensor_scalar(counti[:], counti[:], 7, 7, ALU.arith_shift_right, ALU.logical_shift_left))
            own.link(nc.vector.tensor_copy(padded[:], counti[:]))
            own.link(nc.vector.tensor_tensor_scan(endp[:], ones_e[:], padded[:], 0.0, ALU.mult, ALU.add))
            nc.vector.tensor_tensor(base[:, :, 0], endp[:], padded[:], ALU.subtract)
            own.link(nc.vector.tensor_tensor(place[:], incl[:], tot[:], ALU.subtract))
            own.link(nc.vector.tensor_tensor(place[:], place[:], base[:].to_broadcast([P, EX, T]), ALU.add))
            own.link(nc.vector.tensor_tensor(place[:], place[:], bank[0][:, 0:EX * T].rearrange("p (e t) -> p e t", t=T),
                                             ALU.add))
            own.link(nc.vector.tensor_tensor(prod[:], hot[:], place[:].unsqueeze(1).to_broadcast([P, TOPK, EX, T]), ALU.mult))
            own.link(nc.vector.tensor_reduce(posf[:], prod[:].rearrange("p k e t -> p k t e"), AXX, ALU.add))
            nc.vector.tensor_copy(pos[:], posf[:]).then_inc(pos_ready, 1)
            own.link(nc.vector.tensor_tensor(past[:], row0[:], endp[0:1, :].unsqueeze(1).to_broadcast([1, BLOCKS, EX]), ALU.is_ge))
            own.link(nc.vector.tensor_reduce(ebf[:], past[:], AXX, ALU.add))
            own.link(nc.vector.tensor_scalar(block_expert[:], ebf[:], float(EX - 1), None, ALU.min))
            for t in range(T):
                if t >= RING:
                    dve.wait_ge(scattered[t % RING], 16 * TOPK * (t // RING))
                nc.vector.tensor_scalar(xs[:, t % RING, :], x[:, t, :], stat_all[:, t, 0:1], stat_all[:, t, 1:2],
                                        ALU.subtract, ALU.mult).then_inc(xs_ready, 1)


def over_blocks(engine, body):
    assert NBLK % 2 == 1
    for i in range(3):
        body(i, i % 2)
    with engine.Fori(3, NBLK - 3, 2) as i:
        body(i, 1)
        body(i + 1, 0)
    for i in range(NBLK - 2, NBLK):
        body(i, i % 2)


def phase_experts(nc, tag, xs_dram, ys_dram, w1, w2, w3, block_expert, ident, bank):
    a_bank, b_bank, th_bank, xt_bank, y_bank = bank[0:2], bank[2:4], bank[4:6], bank[6], bank[7]
    with ExitStack() as ctx:
        def sb(name, shape, dt=F32):
            return ctx.enter_context(nc.sbuf_tensor(name, shape, dt))

        def sem(name):
            return ctx.enter_context(nc.semaphore(name))

        w1_s = sb(tag + "m_w1", [P, EX, KC * H])
        w3_s = sb(tag + "m_w3", [P, EX, KC * H])
        w2_s = sb(tag + "m_w2", [P, EX, HC * C])
        xs = [sb(tag + f"m_xs{i}", [P, C]) for i in range(2)]
        xT = [sb(tag + f"m_xT{i}", [P, KC, P]) for i in range(2)]
        g = [sb(tag + f"m_g{i}", [P, H]) for i in range(2)]
        h = [sb(tag + f"m_h{i}", [P, H]) for i in range(2)]
        hT = [sb(tag + f"m_hT{i}", [P, HC, P]) for i in range(2)]
        y = [sb(tag + f"m_y{i}", [P, C]) for i in range(2)]
        w_in = sem(tag + "m_w_in")
        w_in_act = sem(tag + "m_w_in_act")
        loaded = [sem(tag + f"m_loaded{i}") for i in range(2)]
        stored = [sem(tag + f"m_stored{i}") for i in range(2)]
        a_done, b_done, th_done, xt_done, y_done = (sem(tag + "m_a_done"), sem(tag + "m_b_done"), sem(tag + "m_th_done"),
                                                    sem(tag + "m_xt_done"), sem(tag + "m_y_done"))
        silu_done, th_evac, h_ready, xT_ready, y_evac = (sem(tag + "m_silu_done"), sem(tag + "m_th_evac"), sem(tag + "m_h_ready"),
                                                         sem(tag + "m_xT_ready"), sem(tag + "m_y_evac"))
        block = ctx.enter_context(nc.Block())

        def rows(dram, i):
            return dram[bass.ds(i * P, P), :] if not isinstance(i, int) else dram[i * P:(i + 1) * P, :]

        @block.sync
        def _(sp):
            for e in range(EX):
                sp.dma_start(w1_s[:, e, :].rearrange("p (k h) -> p k h", h=H),
                             w1[e].rearrange("(k p) h -> p k h", p=P)).then_inc(w_in, 16)
                sp.dma_start(w2_s[:, e, :].rearrange("p (k c) -> p k c", c=C),
                             w2[e].rearrange("(k p) c -> p k c", p=P)).then_inc(w_in, 16)
            for i in range(2):
                sp.dma_start(xs[i][:], rows(xs_dram, i)).then_inc(loaded[i], 16)

            def step(i, par):
                if not (isinstance(i, int) and i >= NBLK - 2):
                    sp.wait_ge(xt_done, i + 1)
                    sp.dma_start(xs[par][:], rows(xs_dram, i + 2)).then_inc(loaded[par], 16)
                if not is_first(i):
                    sp.wait_ge(y_evac, i)
                    sp.dma_start(rows(ys_dram, i - 1), y[1 - par][:]).then_inc(stored[1 - par], 16)

            over_blocks(sp, step)
            sp.wait_ge(y_evac, NBLK)
            sp.dma_start(rows(ys_dram, NBLK - 1), y[0][:]).then_inc(stored[0], 16)
            sp.wait_ge(stored[0], 16 * ((NBLK + 1) // 2))
            sp.wait_ge(stored[1], 16 * (NBLK // 2))

        @block.scalar
        def _(act):
            for e in range(EX):
                act.dma_start(w3_s[:, e, :].rearrange("p (k h) -> p k h", h=H),
                              w3[e].rearrange("(k p) h -> p k h", p=P)).then_inc(w_in_act, 16)

            def evacuate_h(i, par):
                act.wait_ge(th_done, i + 1)
                wait_count(act, y_done, i - 1)
                nc.scalar.activation(hT[par][:].rearrange("p k t -> p (k t)"), th_bank[par][:], ACT.Copy).then_inc(th_evac, 1)

            def step(i, par):
                act.wait_ge(a_done, i + 1)
                wait_count(act, h_ready, i - 1)
                nc.scalar.activation(g[par][:], a_bank[par][:], ACT.Silu).then_inc(silu_done, 1)
                if not is_first(i):
                    evacuate_h(i - 1, 1 - par)

            over_blocks(act, step)
            evacuate_h(NBLK - 1, 0)

        @block.vector
        def _(dve):
            def evacuate_x(i, par):
                dve.wait_ge(xt_done, i + 1)
                wait_count(dve, b_done, i - 1)
                nc.vector.tensor_copy(xT[par][:].rearrange("p k t -> p (k t)"), xt_bank[:, 0:C]).then_inc(xT_ready, 1)

            def evacuate_y(i, par):
                dve.wait_ge(y_done, i + 1)
                if not (isinstance(i, int) and i < 2):
                    dve.wait_ge(stored[par], 8 * (i - par))
                nc.vector.tensor_copy(y[par][:], y_bank[:, 0:C]).then_inc(y_evac, 1)

            evacuate_x(0, 0)

            def step(i, par):
                if not is_first(i):
                    pass
                dve.wait_ge(silu_done, i + 1)
                dve.wait_ge(b_done, i + 1)
                wait_count(dve, th_done, i - 1)
                nc.vector.tensor_tensor(h[par][:], g[par][:], b_bank[par][:], ALU.mult).then_inc(h_ready, 1)
                if not is_first(i):
                    evacuate_y(i - 1, 1 - par)
                if not (isinstance(i, int) and i == NBLK - 1):
                    evacuate_x(i + 1, 1 - par)

            over_blocks(dve, step)
            evacuate_y(NBLK - 1, 0)

        @block.tensor
        def _(pe):
            def transpose_x(i, par):
                pe.wait_ge(loaded[par], 8 * (i - par) + 16)
                wait_count(pe, xT_ready, i)
                for k in range(KC):
                    last = nc.tensor.transpose(xt_bank[:, k * P:(k + 1) * P], xs[par][:, k * P:(k + 1) * P], ident[:])
                last.then_inc(xt_done, 1)

            def expert_of(i):
                return pe.value_load(block_expert[0:1, bass.ds(i, 1)] if not isinstance(i, int) else block_expert[0:1, i:i + 1],
                                     min_val=0, max_val=EX - 1)

            def weights(w, e):
                return w[:, bass.ds(e, 1), :].rearrange("p a n -> p (a n)")

            def up(w, e, par, out, done):
                for k in range(KC):
                    last = nc.tensor.matmul(out[:], xT[par][:, k, :], weights(w, e)[:, k * H:(k + 1) * H],
                                            start=(k == 0), stop=(k == KC - 1))
                last.then_inc(done, 1)

            def transpose_h(i, par):
                pe.wait_ge(h_ready, i + 1)
                wait_count(pe, th_evac, i - 1)
                for k in range(HC):
                    last = nc.tensor.transpose(th_bank[par][:, k * P:(k + 1) * P], h[par][:, k * P:(k + 1) * P], ident[:])
                last.then_inc(th_done, 1)

            def down(i, par, e):
                pe.wait_ge(th_evac, i + 1)
                wait_count(pe, y_evac, i)
                for k in range(HC):
                    last = nc.tensor.matmul(y_bank[:, 0:C], hT[par][:, k, :], weights(w2_s, e)[:, k * C:(k + 1) * C],
                                            start=(k == 0), stop=(k == HC - 1))
                last.then_inc(y_done, 1)

            transpose_x(0, 0)
            pe.wait_ge(w_in, 16 * 2 * EX)
            pe.wait_ge(w_in_act, 16 * EX)

            def step(i, par):
                e = expert_of(i)
                pe.wait_ge(xT_ready, i + 1)
                wait_count(pe, silu_done, i - 1)
                up(w1_s, e, par, a_bank[par], a_done)
                if not is_first(i):
                    transpose_h(i - 1, 1 - par)
                wait_count(pe, h_ready, i - 1)
                up(w3_s, e, par, b_bank[par], b_done)
                if not is_first(i):
                    down(i - 1, 1 - par, expert_of(i - 1))
                if not (isinstance(i, int) and i == NBLK - 1):
                    transpose_x(i + 1, 1 - par)

            over_blocks(pe, step)
            transpose_h(NBLK - 1, 0)
            down(NBLK - 1, 0, expert_of(NBLK - 1))


def phase_combine(nc, tag, x, ys_dram, score, pos, out_dram=None):
    with ExitStack() as ctx:
        RING = 4
        ya = ctx.enter_context(nc.sbuf_tensor(tag + "c_y", [P, RING, TOPK, C], F32))
        gathered = [ctx.enter_context(nc.semaphore(tag + f"c_gathered{i}")) for i in range(RING)]
        added = ctx.enter_context(nc.semaphore(tag + "c_added"))
        half = ctx.enter_context(nc.semaphore(tag + "c_half"))
        stored = ctx.enter_context(nc.semaphore(tag + "c_stored"))
        block = ctx.enter_context(nc.Block())

        @block.gpsimd
        def _(pool):
            for t in range(T):
                if t >= RING:
                    pool.wait_ge(added, t - RING + 1)
                for k in range(TOPK):
                    nc.gpsimd.indirect_dma_start(ya[:, t % RING, k, :], None, ys_dram[:],
                                                 bass.IndirectOffsetOnAxis(ap=pos[:, k, t:t + 1], axis=0)
                                                 ).then_inc(gathered[t % RING], 16)

        @block.vector
        def _(dve):
            for t in range(T):
                dve.wait_ge(gathered[t % RING], 16 * TOPK * (t // RING + 1))
                nc.vector.scalar_tensor_tensor(out=ya[:, t % RING, 0, :], in0=ya[:, t % RING, 0, :],
                                               scalar=score[:, 0, t:t + 1], in1=x[:, t, :],
                                               op0=ALU.mult, op1=ALU.add).then_inc(half, 1)
                dve.wait_ge(half, t + 1)
                nc.vector.scalar_tensor_tensor(out=x[:, t, :], in0=ya[:, t % RING, 1, :],
                                               scalar=score[:, 1, t:t + 1], in1=ya[:, t % RING, 0, :],
                                               op0=ALU.mult, op1=ALU.add).then_inc(added, 1)

        if out_dram is not None:
            @block.sync
            def _(sp):
                ov = out_dram.rearrange("b (t p) c -> p (b t) c", p=P)
                for t in range(0, T, 2):
                    sp.wait_ge(added, t + 2)
                    sp.dma_start(ov[:, t:t + 2, :], x[:, t:t + 2, :]).then_inc(stored, 16)
                sp.wait_ge(stored, 16 * T // 2)


def zero_rows(nc, xs_dram):
    with ExitStack() as ctx:
        zeros = ctx.enter_context(nc.sbuf_tensor("z_zeros", [P, C], F32))
        cleared = ctx.enter_context(nc.semaphore("z_cleared"))
        written = ctx.enter_context(nc.semaphore("z_written"))
        block = ctx.enter_context(nc.Block())

        @block.vector
        def _(dve):
            nc.vector.memset(zeros[:], 0.0).then_inc(cleared, 1)

        @block.sync
        def _(sp):
            sp.wait_ge(cleared, 1)
            sp.dma_start(xs_dram.rearrange("(n p) c -> p n c", p=P),
                         zeros[:].unsqueeze(1).to_broadcast([P, NBLK, C])).then_inc(written, 16)
            sp.wait_ge(written, 16)


def phase_mix(nc, ln1_w, ln1_b, ln2_w, ln2_b, time_decay, time_first, mix_k, mix_v, mix_r, w_key, w_value, w_recept,
              w_output, f_mix_k, f_mix_r, f_w_key, f_w_recept, f_w_value, gate_w,
              x, stat_all, logits, ident, neg_half, bank):
    tbk, xb_ = bank[0:2], bank[2:8]
    with ExitStack() as ctx:
        def sb(name, shape, dt=F32):
            return ctx.enter_context(nc.sbuf_tensor("b_" + name, shape, dt))

        def sem(name):
            return ctx.enter_context(nc.semaphore("b_" + name))

        wk_s, wv_s, wr_s, wo_s, wf_s = (sb(f"w{n}", [P, KC, C]) for n in "kvrof")
        fk_s, fv_s, gate_s = sb("fk", [P, KC, F]), sb("fv", [P, FCH, C]), sb("gate", [P, KC, EX])
        vec = {n: sb(f"v_{n}", [P, KC]) for n in ("ln1_w", "ln1_b", "ln2_w", "ln2_b", "decay", "first", "mk", "mv", "mr",
                                                  "fmk", "fmr", "ndecay")}
        bn, mv, bn1, mv1 = sb("bn", [P, TB, 6]), sb("mv", [P, TB, 2]), sb("bn1", [P, TB, 6]), sb("mv1", [P, TB, 2])
        bn2, mv2, bng, mvg = sb("bn2", [P, TB, 6]), sb("mv2", [P, TB, 2]), sb("bng", [P, TB, 6]), sb("mvg", [P, TB, 2])
        mv_all = sb("mv_all", [P, T, 2])
        a, xn = sb("a", [P, TB, C]), sb("xn", [P, TB, C])
        xnT = sb("xnT", [P, KC, N + 1])
        dT = sb("dT", [P, KC, N])
        xk, xv, xr = sb("xk", [P, KC, N]), sb("xv", [P, KC, N]), sb("xr", [P, KC, N])
        k, v, sg = sb("k", [P, KC, N]), sb("v", [P, KC, N]), sb("sg", [P, KC, N])
        eps = sb("eps", [P, KC, N + 1])
        e1, e2, d1, d2 = (sb(n, [P, KC, N]) for n in ("e1", "e2", "d1", "d2"))
        al, be = sb("al", [P, KC, N + 1]), sb("be", [P, KC, N + 1])
        dv, ev, gT = sb("dv", [P, KC, N]), sb("ev", [P, KC, N]), sb("gT", [P, KC, N])
        xb, xn2, xn2T = sb("xb", [P, TB, C]), sb("xn2", [P, TB, C]), sb("xn2T", [P, KC, N + 1])
        xfk, xfr = sb("xfk", [P, KC, N]), sb("xfr", [P, KC, N])
        hT, fs = sb("hT", [P, FCH, N]), sb("fs", [P, 2, N])
        xg, xgT = sb("xg", [P, TB, C]), sb("xgT", [P, KC, N])

        w_in, v_in, prep = sem("w_in"), sem("v_in"), sem("prep")
        own_f, own_m, own_e, own_r, own_w, own_g, own_p = (sem(f"own_{n}") for n in "fmerwgp")
        own_pool, passed_dve, passed_pool = sem("own_pool"), sem("passed_dve"), sem("passed_pool")
        var_ready, rstd_ready, var1_ready, rstd1_ready = sem("var_ready"), sem("rstd_ready"), sem("var1_ready"), sem("rstd1_ready")
        var2_ready, rstd2_ready, varg_ready, rstdg_ready = sem("var2_ready"), sem("rstd2_ready"), sem("varg_ready"), sem("rstdg_ready")
        xn_ready, t_filled, t_emptied, mix_ready = sem("xn_ready"), sem("t_filled"), sem("t_emptied"), sem("mix_ready")
        kvr_done, kvr_evac, s_ready, expd = sem("kvr_done"), sem("kvr_evac"), sem("s_ready"), sem("expd")
        dv_ready, ev_ready, sg_ready, g_ready = sem("dv_ready"), sem("ev_ready"), sem("sg_ready"), sem("g_ready")
        wo_done, xb_ready, xn2_ready, mix2_ready = sem("wo_done"), sem("xb_ready"), sem("xn2_ready"), sem("mix2_ready")
        fk_done, h_relu, h_ready, fr_done = sem("fk_done"), sem("h_relu"), sem("h_ready"), sem("fr_done")
        fs_ready, fs2_ready, vk_done, sum_ready, x3_ready, xg_ready = (sem("fs_ready"), sem("fs2_ready"), sem("vk_done"),
                                                                       sem("sum_ready"), sem("x3_ready"), sem("xg_ready"))
        block = ctx.enter_context(nc.Block())

        def static(b, value):
            return isinstance(b, int) and b == value

        def round_xn2(b):
            return 2 if static(b, 0) else 4 * b - 1 if static(b, B - 1) else 4 * b

        def round_gate(b):
            return 4 * b if static(b, B - 1) else 4 * b - 2 if static(b, B) else 4 * b + 1

        def round_xn(b):
            return b if isinstance(b, int) and b < 2 else 4 * b - 5

        def has_next(b, n):
            return not (isinstance(b, int) and b + n >= B)

        def over_periods(engine, body):
            body(0)
            with engine.Fori(1, B - 2) as b:
                body(b)
            body(B - 2)
            body(B - 1)

        loads = (("ln1_w", ln1_w), ("ln1_b", ln1_b), ("ln2_w", ln2_w), ("ln2_b", ln2_b), ("decay", time_decay),
                 ("first", time_first), ("mk", mix_k), ("mv", mix_v), ("mr", mix_r), ("fmk", f_mix_k), ("fmr", f_mix_r))
        V_IN = 16 * len(loads)
        W_IN = 16 * (7 + KC)

        @block.sync
        def _(sp):
            for dst, src in ((wk_s, w_key), (wv_s, w_value), (wr_s, w_recept), (wo_s, w_output), (wf_s, f_w_recept),
                             (fk_s, f_w_key), (fv_s, f_w_value)):
                sp.dma_start(dst[:], src.rearrange("(k p) n -> p k n", p=P)).then_inc(w_in, 16)
            for i in range(KC):
                sp.dma_start(gate_s[:, i, :], gate_w[:, i * P:(i + 1) * P].rearrange("e p -> p e"),
                             allow_slow_non_contiguous=True).then_inc(w_in, 16)

        @block.scalar
        def _(act):
            for name, src in loads:
                flat = src if len(src.shape) == 1 else src.rearrange("a b c -> (a b c)")
                act.dma_start(vec[name][:], flat.rearrange("(k p) -> p k", p=P),
                              allow_slow_non_contiguous=True).then_inc(v_in, 16)
            act.wait_ge(v_in, V_IN)
            nc.scalar.activation(vec["decay"][:], vec["decay"][:], ACT.Exp).then_inc(prep, 1)

            def evacuate_norm(dst, w, bias, r):
                act.wait_ge(t_filled, r + 1)
                for i in range(KC):
                    last = nc.scalar.activation(dst[:, i, 1:N + 1], tbk[i][:], ACT.Identity, bias=vec[bias][:, i:i + 1],
                                                scale=vec[w][:, i:i + 1])
                last.then_inc(t_emptied, 1)

            def evacuate_xn(b):
                wait_count(act, mix_ready, b)
                evacuate_norm(xnT, "ln1_w", "ln1_b", round_xn(b))

            def evacuate_kvr(b):
                wait_count(act, g_ready, b)
                for n, (dst, src) in enumerate(((k, 2), (k, 3), (v, 4), (v, 5), (sg, 0), (sg, 1))):
                    act.wait_ge(kvr_done, 6 * b + n + 1)
                    f, scale = (ACT.Tanh, 0.5) if dst is sg else (ACT.Copy, 1.0)
                    nc.scalar.activation(dst[:, n % 2, :], xb_[src][:], f, scale=scale).then_inc(kvr_evac, 1)

            def exponentials(b):
                for n, (z, other) in enumerate(((d1, d2), (e1, e2))):
                    act.wait_ge(s_ready, 2 * b + n + 1)
                    nc.scalar.activation(other[:], z[:], ACT.Relu, scale=-1.0).then_inc(expd, 1)
                    act.wait_ge(expd, 8 * b + 4 * n + 1)
                    nc.scalar.activation(z[:], z[:], ACT.Relu).then_inc(expd, 1)
                    nc.scalar.activation(other[:], other[:], ACT.Exp, scale=-1.0).then_inc(expd, 1)
                    act.wait_ge(expd, 8 * b + 4 * n + 3)
                    nc.scalar.activation(z[:], z[:], ACT.Exp, scale=-1.0).then_inc(expd, 1)

            def hidden(b):
                wait_count(act, vk_done, 2 * b)
                for m in range(FCH):
                    act.wait_ge(fk_done, FCH * b + m + 1)
                    nc.scalar.activation(hT[:, m, :], xb_[m % 4][:], ACT.Relu).then_inc(h_relu, 1)
                    act.wait_ge(h_relu, FCH * b + m + 1)
                    nc.scalar.activation(hT[:, m, :], hT[:, m, :], ACT.Square).then_inc(h_ready, 1)
                wait_count(act, x3_ready, b)
                for h in range(2):
                    act.wait_ge(fr_done, 2 * b + h + 1)
                    nc.scalar.activation(fs[:, h, :], xb_[4 + h][:], ACT.Tanh, scale=0.5).then_inc(fs_ready, 1)

            def gate_part(b):
                r = round_gate(b)
                act.wait_ge(t_filled, r + 1)
                for i in range(KC):
                    last = nc.scalar.activation(xgT[:, i, :], tbk[i][:], ACT.Copy)
                last.then_inc(t_emptied, 1)
                act.wait_ge(t_filled, r + 2)
                nc.scalar.activation(sequence_tiles(logits, b - 1),
                                     tbk[0][:, 0:TB * EX].rearrange("p (t e) -> p t e", e=EX),
                                     ACT.Copy).then_inc(t_emptied, 1)

            evacuate_xn(0)
            evacuate_kvr(0)
            evacuate_xn(1)
            exponentials(0)

            def period(b):
                if has_next(b, 1):
                    evacuate_kvr(b + 1)
                wait_count(act, mix2_ready, b)
                evacuate_norm(xn2T, "ln2_w", "ln2_b", round_xn2(b))
                if not static(b, 0):
                    gate_part(b)
                if has_next(b, 1):
                    exponentials(b + 1)
                hidden(b)
                if has_next(b, 2):
                    evacuate_xn(b + 2)

            over_periods(act, period)
            gate_part(B)

        @block.gpsimd
        def _(pool):
            def rstd(mvt, ready, done, count, value):
                wait_apart(pool, ready, count, passed_pool)
                nc.gpsimd.tensor_scalar(mvt[:, :, 1], mvt[:, :, 1], EPS, None, ALU.add).then_inc(own_pool, 1)
                pool.wait_ge(own_pool, value)
                nc.gpsimd.tensor_tensor(mvt[:, :, 1], mvt[:, :, 1], neg_half[:, 0:TB], ALU.pow).then_inc(done, 1)

            def begin(b, value):
                rstd(mv, var_ready, rstd_ready, b + 1, value + 1)
                rstd(mv1, var1_ready, rstd1_ready, b + 1, value + 2)

            def recurrence(b):
                wait_count(pool, g_ready, b)
                wait_apart(pool, kvr_evac, 6 * b + 6, passed_pool)
                nc.gpsimd.tensor_scalar(sg[:], sg[:], 0.5, 0.5, ALU.mult, ALU.add).then_inc(sg_ready, 1)
                pool.wait_ge(expd, 8 * b + 3)
                nc.gpsimd.tensor_tensor(dv[:], d2[:], v[:], ALU.mult).then_inc(dv_ready, 1)
                pool.wait_ge(expd, 8 * b + 7)
                nc.gpsimd.tensor_tensor(ev[:], e2[:], v[:], ALU.mult).then_inc(ev_ready, 1)

            begin(0, 0)
            begin(1, 2)
            recurrence(0)

            def period(b):
                done = 4 if static(b, 0) else 4 * b + 3
                if static(b, B - 1):
                    done = 4 * (B - 2) + 3 + 2
                rstd(mv2, var2_ready, rstd2_ready, b + 1, done + 1)
                if not static(b, 0):
                    rstd(mvg, varg_ready, rstdg_ready, b, done + 2)
                    done = done + 1
                if has_next(b, 1):
                    recurrence(b + 1)
                if has_next(b, 2):
                    begin(b + 2, done + 1)
                wait_apart(pool, fs_ready, 2 * b + 2, passed_pool)
                nc.gpsimd.tensor_scalar(fs[:], fs[:], 0.5, 0.5, ALU.mult, ALU.add).then_inc(fs2_ready, 1)
                wait_apart(pool, sum_ready, b + 1, passed_pool)
                xt = sequence_tiles(x, b)
                nc.gpsimd.tensor_tensor(xt, xt, fs[:].rearrange("p h (t c) -> p (h t) c", c=C), ALU.add).then_inc(x3_ready, 1)

            over_periods(pool, period)
            rstd(mvg, varg_ready, rstdg_ready, B, 4 * (B - 2) + 3 + 4 + 1)

        @block.vector
        def _(dve):
            f, m_, e_, r_, w_, g_, p_ = (OwnSteps(dve, sm, n) for sm, n in ((own_f, 3), (own_m, 1), (own_e, 1), (own_r, 5),
                                                                        (own_w, 3), (own_g, 1), (own_p, 1)))
            m2 = OwnSteps(dve, sem("own_m2"), 1)

            def statistics(src, bnt, mvt, own, done):
                for j in range(TB):
                    last = nc.vector.bn_stats(bnt[:, j, :], src(j))
                own.link(last, passed_dve)
                for j in range(TB):
                    last = nc.vector.bn_aggr(mvt[:, j, :], bnt[:, j, :])
                last.then_inc(done, 1)

            def normalise(dst, src, mvt):
                for j in range(TB):
                    last = nc.vector.tensor_scalar(dst[:, j, :], src(j), mvt(j)[:, 0:1], mvt(j)[:, 1:2],
                                                   ALU.subtract, ALU.mult)
                return last

            def begin(b):
                f.round(b)
                statistics(lambda j: tile_of(x, b, j), bn, mv, f, var_ready)
                dve.wait_ge(rstd_ready, b + 1)
                nc.vector.tensor_copy(sequence_tiles(mv_all, b), mv[:])
                f.link(normalise(a, lambda j: tile_of(x, b, j), lambda j: mv[:, j, :]))
                statistics(lambda j: a[:, j, :], bn1, mv1, f, var1_ready)
                dve.wait_ge(rstd1_ready, b + 1)
                normalise(xn, lambda j: a[:, j, :], lambda j: mv1[:, j, :]).then_inc(xn_ready, 1)

            def mixes(own, src, outs, b, done):
                own.round(b)
                own.link(nc.vector.tensor_tensor(dT[:], src[:, :, 1:N + 1], src[:, :, 0:N], ALU.subtract))
                for dst, m in outs:
                    for i in range(KC):
                        last = nc.vector.scalar_tensor_tensor(out=dst[:, i, :], in0=dT[:, i, :], scalar=vec[m][:, i:i + 1],
                                                              in1=src[:, i, 0:N], op0=ALU.mult, op1=ALU.add)
                last.then_inc(done, 1)

            def mix_time(b):
                dve.wait_ge(t_emptied, round_xn(b) + 1)
                wait_count(dve, kvr_done, 6 * b)
                mixes(m_, xnT, ((xk, "mk"), (xv, "mv"), (xr, "mr")), b, mix_ready)

            def exponents(b):
                dve.wait_ge(kvr_evac, 6 * b + 2)
                e_.round(b)
                for i in range(KC):
                    last = nc.vector.tensor_tensor_scan(eps[:, i, 1:N + 1], vec["ndecay"][:, i:i + 1].to_broadcast([P, N]),
                                                        k[:, i, :], EPS_INIT, ALU.add, ALU.max)
                e_.link(last)
                for dst, c in ((d1, "decay"), (e1, "first")):
                    for i in range(KC):
                        last = nc.vector.scalar_tensor_tensor(out=dst[:, i, :], in0=k[:, i, :], scalar=vec[c][:, i:i + 1],
                                                              in1=eps[:, i, 0:N], op0=ALU.add, op1=ALU.subtract)
                    last.then_inc(s_ready, 1)

            def recurrence(b):
                r_.round(b)
                dve.wait_ge(expd, 8 * b + 4)
                for i in range(KC):
                    nc.vector.tensor_tensor_scan(be[:, i, 1:N + 1], d1[:, i, :], d2[:, i, :], 0.0, ALU.mult, ALU.add)
                dve.wait_ge(dv_ready, b + 1)
                for i in range(KC):
                    last = nc.vector.tensor_tensor_scan(al[:, i, 1:N + 1], d1[:, i, :], dv[:, i, :], 0.0, ALU.mult, ALU.add)
                r_.link(last)
                dve.wait_ge(expd, 8 * b + 8)
                nc.vector.tensor_tensor(d1[:], e1[:], be[:, :, 0:N], ALU.mult)
                r_.link(nc.vector.tensor_tensor(dv[:], e1[:], al[:, :, 0:N], ALU.mult))
                nc.vector.tensor_tensor(d1[:], d1[:], e2[:], ALU.add)
                dve.wait_ge(ev_ready, b + 1)
                r_.link(nc.vector.tensor_tensor(dv[:], dv[:], ev[:], ALU.add))
                nc.vector.reciprocal(d1[:], d1[:])
                dve.wait_ge(sg_ready, b + 1)
                r_.link(nc.vector.tensor_tensor(dv[:], dv[:], sg[:], ALU.mult))
                nc.vector.tensor_tensor(gT[:], dv[:], d1[:], ALU.mult).then_inc(g_ready, 1)
                r_.pad()

            def time_output(b):
                w_.round(b)
                wait_count(dve, sum_ready, b)
                w_.link(normalise(xb, lambda j: tile_of(x, b, j), lambda j: tile_of(mv_all, b, j)))
                for h in range(2):
                    dve.wait_ge(wo_done, 2 * b + h + 1)
                    t = xb[:, 2 * h:2 * h + 2, :].rearrange("p t c -> p (t c)")
                    nc.vector.tensor_tensor(t, t, xb_[h][:], ALU.add).then_inc(xb_ready, 1)
                dve.wait_ge(xb_ready, 2 * b + 2)
                statistics(lambda j: xb[:, j, :], bn2, mv2, w_, var2_ready)
                w_.pad()

            def norm2(b):
                dve.wait_ge(rstd2_ready, b + 1)
                normalise(xn2, lambda j: xb[:, j, :], lambda j: mv2[:, j, :]).then_inc(xn2_ready, 1)

            def mix_channel(b):
                dve.wait_ge(t_emptied, round_xn2(b) + 1)
                mixes(m2, xn2T, ((xfk, "fmk"), (xfr, "fmr")), b, mix2_ready)

            def route_statistics(b):
                g_.round(b)
                dve.wait_ge(x3_ready, b + 1)
                statistics(lambda j: tile_of(x, b, j), bng, mvg, g_, varg_ready)

            def route_norm(b):
                dve.wait_ge(rstdg_ready, b + 1)
                nc.vector.tensor_copy(sequence_tiles(stat_all, b), mvg[:])
                normalise(xg, lambda j: tile_of(x, b, j), lambda j: mvg[:, j, :]).then_inc(xg_ready, 1)

            def finish(b):
                p_.round(b)
                dve.wait_ge(fs2_ready, b + 1)
                for h in range(2):
                    dve.wait_ge(vk_done, 2 * b + h + 1)
                    last = nc.vector.tensor_tensor(fs[:, h, :], fs[:, h, :], xb_[2 + h][:], ALU.mult)
                p_.link(last)
                nc.vector.tensor_tensor(fs[:], fs[:], xb[:].rearrange("p (h t) c -> p h (t c)", h=2), ALU.add).then_inc(sum_ready, 1)

            nc.vector.memset(xnT[:, :, 0:1], 0.0)
            nc.vector.memset(xn2T[:, :, 0:1], 0.0)
            nc.vector.memset(eps[:, :, 0:1], EPS_INIT)
            nc.vector.memset(al[:, :, 0:1], 0.0)
            nc.vector.memset(be[:, :, 0:1], 0.0)
            begin(0)
            dve.wait_ge(v_in, V_IN)
            dve.wait_ge(prep, 1)
            nc.vector.tensor_scalar(vec["ndecay"][:], vec["decay"][:], -1.0, None, ALU.mult).then_inc(prep, 1)
            dve.wait_ge(prep, 2)
            mix_time(0)
            begin(1)
            exponents(0)
            recurrence(0)
            mix_time(1)

            def period(b):
                time_output(b)
                if not static(b, 0):
                    route_statistics(b - 1)
                norm2(b)
                if not static(b, 0):
                    route_norm(b - 1)
                if has_next(b, 1):
                    exponents(b + 1)
                mix_channel(b)
                if has_next(b, 1):
                    recurrence(b + 1)
                if has_next(b, 2):
                    begin(b + 2)
                    mix_time(b + 2)
                finish(b)

            over_periods(dve, period)
            route_statistics(B - 1)
            route_norm(B - 1)

        @block.tensor
        def _(pe):
            def transposes(src, r):
                wait_count(pe, t_emptied, r)
                for i in range(KC):
                    for j in range(TB):
                        last = nc.tensor.transpose(tbk[i][:, j * P:(j + 1) * P], src[:, j, i * P:(i + 1) * P], ident[:])
                last.then_inc(t_filled, 1)

            def token_product(out, src, w, chunks):
                for j in range(2):
                    for i in range(chunks):
                        last = nc.tensor.matmul(out[:, j * C:(j + 1) * C], src(i, j), w[:, i, :],
                                                start=(i == 0), stop=(i == chunks - 1))
                return last

            def cut(src, h):
                return lambda i, j: src[:, i, (2 * h + j) * P:(2 * h + j + 1) * P]

            def project(b):
                pe.wait_ge(mix_ready, b + 1)
                n = 0
                for w, src, banks in ((wk_s, xk, (2, 3)), (wv_s, xv, (4, 5)), (wr_s, xr, (0, 1))):
                    if not static(b, 0):
                        if n == 0:
                            wait_count(pe, sum_ready, b - 1)
                        elif n == 2:
                            wait_count(pe, fs_ready, 2 * b - 2)
                        else:
                            pe.wait_ge(xb_ready, 2 * b)
                    for c in range(KC):
                        for i in range(KC):
                            last = nc.tensor.matmul(xb_[banks[c]][:], w[:, i, c * P:(c + 1) * P], src[:, i, :],
                                                    start=(i == 0), stop=(i == KC - 1))
                        last.then_inc(kvr_done, 1)
                        n += 1

            def gate_part(b):
                r = round_gate(b)
                pe.wait_ge(xg_ready, b)
                transposes(xg, r)
                pe.wait_ge(t_emptied, r + 1)
                for j in range(TB):
                    for i in range(KC):
                        last = nc.tensor.matmul(tbk[0][:, j * EX:(j + 1) * EX], xgT[:, i, j * P:(j + 1) * P], gate_s[:, i, :],
                                                start=(i == 0), stop=(i == KC - 1))
                last.then_inc(t_filled, 1)

            pe.wait_ge(w_in, W_IN)
            pe.wait_ge(xn_ready, 1)
            transposes(xn, 0)
            project(0)
            pe.wait_ge(xn_ready, 2)
            transposes(xn, 1)

            def period(b):
                pe.wait_ge(g_ready, b + 1)
                wait_count(pe, h_relu, FCH * b)
                if static(b, 0):
                    pe.wait_ge(kvr_evac, 6)
                for h in range(2):
                    token_product(xb_[h], cut(gT, h), wo_s, KC).then_inc(wo_done, 1)
                if has_next(b, 1):
                    project(b + 1)
                pe.wait_ge(xn2_ready, b + 1)
                transposes(xn2, round_xn2(b))
                if not static(b, 0):
                    gate_part(b)
                pe.wait_ge(mix2_ready, b + 1)
                if has_next(b, 1):
                    pe.wait_ge(kvr_evac, 6 * b + 12)
                else:
                    pe.wait_ge(xb_ready, 2 * b + 2)
                    pe.wait_ge(sum_ready, b)
                for m in range(FCH):
                    if m >= 4:
                        pe.wait_ge(h_relu, FCH * b + m - 3)
                    for i in range(KC):
                        last = nc.tensor.matmul(xb_[m % 4][:], fk_s[:, i, m * P:(m + 1) * P], xfk[:, i, :],
                                                start=(i == 0), stop=(i == KC - 1))
                    last.then_inc(fk_done, 1)
                wait_count(pe, fs_ready, 2 * b)
                for h in range(2):
                    token_product(xb_[4 + h], cut(xfr, h), wf_s, KC).then_inc(fr_done, 1)
                if has_next(b, 2):
                    pe.wait_ge(xn_ready, b + 3)
                    transposes(xn, round_xn(b + 2))
                pe.wait_ge(h_ready, FCH * b + FCH)
                for h in range(2):
                    token_product(xb_[2 + h], cut(hT, h), fv_s, FCH).then_inc(vk_done, 1)

            over_periods(pe, period)
            gate_part(B)


def build(nc, x_in, qk_w, qk_b, lepe_w, lepe_b, ln1_w, ln1_b, ln2_w, ln2_b, time_decay, time_first, mix_k, mix_v, mix_r,
          w_key, w_value, w_recept, w_output, f_mix_k, f_mix_r, f_w_key, f_w_recept, f_w_value, gate_w, w1, w2, w3,
          cos_t, sin_t, out):
    xs_dram = nc.dram_tensor("rows_sorted", (NBLK * P, C), F32, kind="Internal").ap()
    ys_dram = nc.dram_tensor("rows_of_experts", (NBLK * P, C), F32, kind="Internal").ap()
    with ExitStack() as ctx:
        def sb(name, shape, dt=F32):
            return ctx.enter_context(nc.sbuf_tensor(name, shape, dt))

        x = sb("x", [P, T, C])
        stat_all = sb("stat_all", [P, T, 2])
        logits = sb("logits", [P, T, EX])
        score = sb("score", [P, TOPK, T])
        pos = sb("pos", [P, TOPK, T], U32)
        block_expert = sb("block_expert", [1, NBLK], I32)
        ident = sb("ident", [P, P])
        head_mask = sb("head_mask", [P, HEADS])
        block_mask = sb("block_mask", [P, P])
        neg_half = sb("neg_half", [P, TB])
        bank = [ctx.enter_context(nc.psum_tensor(f"bank{i}", [P, N], F32)) for i in range(8)]

        def experts(tag, out_dram=None):
            phase_route(nc, tag, x, stat_all, logits, xs_dram, score, pos, block_expert, bank)
            phase_experts(nc, tag, xs_dram, ys_dram, w1, w2, w3, block_expert, ident, bank)
            phase_combine(nc, tag, x, ys_dram, score, pos, out_dram)

        stage_constants(nc, ident, head_mask, block_mask, neg_half)
        zero_rows(nc, xs_dram)
        phase_attention(nc, x_in, qk_w, qk_b, lepe_w, lepe_b, gate_w, cos_t, sin_t, x, stat_all, logits, ident,
                        head_mask, block_mask, neg_half, bank)
        experts("first_")
        phase_mix(nc, ln1_w, ln1_b, ln2_w, ln2_b, time_decay, time_first, mix_k, mix_v, mix_r, w_key, w_value, w_recept,
                  w_output, f_mix_k, f_mix_r, f_w_key, f_w_recept, f_w_value, gate_w, x, stat_all, logits, ident,
                  neg_half, bank)
        experts("second_", out)


_INS = ["L0_attn_a_x", "L0_attn_a_qk_w", "L0_attn_a_qk_b", "L0_attn_a_lepe_w", "L0_attn_a_lepe_b",
        "L0_attn_b_ln1_w", "L0_attn_b_ln1_b", "L0_attn_b_ln2_w", "L0_attn_b_ln2_b", "L0_attn_b_time_decay",
        "L0_attn_b_time_first", "L0_attn_b_time_mix_k", "L0_attn_b_time_mix_v", "L0_attn_b_time_mix_r",
        "L0_attn_b_w_key", "L0_attn_b_w_value", "L0_attn_b_w_recept", "L0_attn_b_w_output", "L0_attn_b_f_time_mix_k",
        "L0_attn_b_f_time_mix_r", "L0_attn_b_f_w_key", "L0_attn_b_f_w_recept", "L0_attn_b_f_w_value",
        "L0_ffn_gate_w", "L0_ffn_w1", "L0_ffn_w2", "L0_ffn_w3"]


def kernel(**inputs):
    import numpy as _np
    import concourse.bacc as _bacc
    from concourse import mybir as _mybir
    from concourse.bass_utils import run_bass_kernel_spmd as _run

    nc = _bacc.Bacc("TRN2", target_bir_lowering=False, num_devices=1)
    f = _np.float32
    theta = (f(1.0) / f(10000.0) ** (_np.arange(C // 2, dtype=f) / f(C // 2))).astype(f)
    angles = (theta[:, None] * _np.arange(N, dtype=f)[None, :]).astype(f)
    arrays, args = {}, []
    for name, a in [(n, inputs[n]) for n in _INS] + [("rope_cos", _np.cos(angles)), ("rope_sin", _np.sin(angles))]:
        a = _np.ascontiguousarray(a)
        arrays[f"in_{name}"] = a
        args.append(nc.dram_tensor(f"in_{name}", a.shape, _mybir.dt.from_np(a.dtype), kind="ExternalInput").ap())
    args.append(nc.dram_tensor("out_x", (B, N, C), F32, kind="ExternalOutput").ap())
    build(nc, *args)
    r = _run(nc, [arrays], core_ids=[0])
    return r.results[0]["out_x"]
```

```python
import concourse.bass as bass
from concourse import mybir
from contextlib import ExitStack

F32 = mybir.dt.float32
I32 = mybir.dt.int32
U32 = mybir.dt.uint32
ALU = mybir.AluOpType
ACT = mybir.ActivationFunctionType
AXX = mybir.AxisListType.X

P = 128
B, N, C = 8, 512, 256
TB = N // P
T = B * TB
KC = C // P
HEADS, HD = 8, C // 8
LT = 3
EX, H = 8, 512
HC = H // P
TOPK = 2
NBLK = TOPK * B * N // P + EX - 1
ROWS = T * P + P
F = 4 * C
FCH = F // P
EPS = 1e-5
EPS_INIT = -1e30


def over_batches(engine, body):
    body(0, 0)
    with engine.Fori(1, B - 2, 2) as b:
        body(b, 1)
        body(b + 1, 0)
    body(B - 1, 1)


def is_first(b):
    return isinstance(b, int) and b == 0


def is_last(b):
    return isinstance(b, int) and b == B - 1


def wait_count(engine, sem, value):
    if isinstance(value, int) and value <= 0:
        return
    engine.wait_ge(sem, value)


def wait_apart(engine, sem, value, passed):
    wait_count(engine, sem, value)
    engine.sem_inc(passed, 1)


class OwnSteps:

    def __init__(self, engine, sem, per_round):
        self.engine, self.sem, self.per_round = engine, sem, per_round
        self.base, self.k = 0, 0

    def round(self, r):
        assert self.k in (0, self.per_round), (self.k, self.per_round)
        self.base, self.k = r * self.per_round, 0

    def link(self, ins, passed=None):
        self.k += 1
        ins.then_inc(self.sem, 1)
        self.engine.wait_ge(self.sem, self.base + self.k)
        if passed is not None:
            self.engine.sem_inc(passed, 1)

    def pad(self):
        while self.k < self.per_round:
            self.k += 1
            self.engine.sem_inc(self.sem, 1)


def sequence_tiles(x, b):
    return x[:, bass.ds(b * TB, TB)] if not isinstance(b, int) else x[:, b * TB:(b + 1) * TB]


def tile_of(x, b, j):
    if isinstance(b, int):
        return x[:, b * TB + j, :]
    return x[:, bass.ds(b * TB + j, 1), :].rearrange("p a c -> p (a c)")


def token_rows(table, b):
    first = b * TB * P
    rows = table[first:first + TB * P, :] if isinstance(b, int) else table[bass.ds(first, TB * P), :]
    return rows.rearrange("(t p) c -> p t c", p=P)


def stage_constants(nc, ident, head_mask, block_mask, neg_half, tables):
    with ExitStack() as ctx:
        made = ctx.enter_context(nc.semaphore("const_made"))
        zeros = ctx.enter_context(nc.sbuf_tensor("zeros", [P, C], F32))
        cleared = ctx.enter_context(nc.semaphore("const_cleared"))
        written = ctx.enter_context(nc.semaphore("const_written"))
        block = ctx.enter_context(nc.Block())

        @block.gpsimd
        def _(pool):
            nc.gpsimd.memset(neg_half[:], -0.5).then_inc(made, 1)
            nc.gpsimd.memset(ident[:], 0.0).then_inc(made, 1)
            nc.gpsimd.memset(head_mask[:], 1.0 / N).then_inc(made, 1)
            nc.gpsimd.memset(block_mask[:], 1.0 / float(N) ** 0.5).then_inc(made, 1)
            pool.wait_ge(made, 4)
            nc.gpsimd.affine_select(out=ident[:], in_=ident[:], compare_op=ALU.not_equal, fill=1.0, base=0,
                                    pattern=[[-1, P]], channel_multiplier=1).then_inc(made, 1)
            pair = HD // 2
            nc.gpsimd.affine_select(out=head_mask[:], in_=head_mask[:], compare_op=ALU.is_ge, fill=0.0, base=0,
                                    pattern=[[-pair, HEADS]], channel_multiplier=1).then_inc(made, 1)
            bm = block_mask[:].rearrange("p (g e) -> p g e", e=HD)
            nc.gpsimd.affine_select(out=bm, in_=bm, compare_op=ALU.is_ge, fill=0.0, base=0,
                                    pattern=[[-HD, P // HD], [0, HD]], channel_multiplier=1).then_inc(made, 1)
            pool.wait_ge(made, 7)
            nc.gpsimd.affine_select(out=head_mask[:], in_=head_mask[:], compare_op=ALU.is_ge, fill=0.0,
                                    base=pair - 1, pattern=[[pair, HEADS]], channel_multiplier=-1).then_inc(made, 1)
            nc.gpsimd.affine_select(out=bm, in_=bm, compare_op=ALU.is_ge, fill=0.0, base=HD - 1,
                                    pattern=[[HD, P // HD], [0, HD]], channel_multiplier=-1).then_inc(made, 1)
            pool.wait_ge(made, 9)

        @block.vector
        def _(dve):
            nc.vector.memset(zeros[:], 0.0).then_inc(cleared, 1)

        @block.sync
        def _(sp):
            sp.wait_ge(cleared, 1)
            for table in tables:
                sp.dma_start(table[T * P:ROWS, :], zeros[:]).then_inc(written, 16)
            sp.wait_ge(written, 16 * len(tables))


def phase_attention(nc, x_dram, qk_w, qk_b, lepe_w, lepe_b, gate_w, cos_t, sin_t,
                    normed_dram, x_dram_out, logits, ident, head_mask, block_mask, neg_half, bank):
    tb0, tb1, q0, q1, q2, q3, l0, l1 = bank
    q, tbk, lb = [q0, q1, q2, q3], [tb0, tb1], [l0, l1]
    ORDER = (2, 3, 0, 1)
    proj = {2: q0, 3: q1, 0: q2, 1: q3}
    with ExitStack() as ctx:
        def sb(name, shape, dt=F32):
            return ctx.enter_context(nc.sbuf_tensor(name, shape, dt))

        def sem(name):
            return ctx.enter_context(nc.semaphore(name))

        x = sb("a_x", [P, T, C])
        qk_raw = sb("a_qk_raw", [P, KC, 2 * C])
        qk_s = sb("a_qk_s", [P, KC, 4, P])
        qk_bias = sb("a_qk_bias", [P, 4])
        lepe_s = sb("a_lepe_s", [P, LT, KC, C])
        lepe_bias = sb("a_lepe_bias", [P, 1, C])
        gate_s = sb("a_gate_s", [P, KC, EX])
        cos_s = sb("a_cos", [P, 1, N])
        sin_s = sb("a_sin", [P, N])
        nsin_s = sb("a_nsin", [P, N])
        bn = sb("a_bn", [P, TB, 6])
        mv = sb("a_mv", [P, TB, 2])
        bn2 = sb("a_bn2", [P, TB, 6])
        mv2 = sb("a_mv2", [P, TB, 2])
        xn = [sb(f"a_xn{i}", [P, TB, C]) for i in range(2)]
        xnT = [sb(f"a_xnT{i}", [P, KC, N + 2]) for i in range(2)]
        ex = sb("a_ex", [P, 4, N])
        re = sb("a_re", [P, 4, N])
        el = sb("a_el", [P, 4, N])
        ksum = sb("a_ksum", [P, 2])
        kz = sb("a_kz", [P, 2, HEADS])
        kA = sb("a_kA", [P, 2, N])
        kB = sb("a_kB", [P, 2, N])
        kr = sb("a_kr", [P, 2, N])
        qA = sb("a_qA", [P, 2, N])
        qB = sb("a_qB", [P, 2, N])
        qr = sb("a_qr", [P, 2, N])
        krt = sb("a_krt", [P, KC, TB, P])
        kvb = sb("a_kvb", [P, KC, P])
        zr = sb("a_zr", [P, TB * HEADS])
        u = sb("a_u", [P, 2, N])
        v = sb("a_v", [P, 2, 2, C])
        xg = sb("a_xg", [P, TB, C])
        xgT = sb("a_xgT", [P, KC, N])

        x1_in, wl_in = sem("a_x1_in"), sem("a_wl_in")
        x0_in, x_in, w_in, wg_in, tab_in = sem("a_x0_in"), sem("a_x_in"), sem("a_w_in"), sem("a_wg_in"), sem("a_tab_in")
        own_dve, own_pool = sem("a_own_dve"), sem("a_own_pool")
        var_ready, rstd_ready, xn_ready = sem("a_var_ready"), sem("a_rstd_ready"), sem("a_xn_ready")
        qk_done, qk_evac, q_ready, kr_ready, qr_ready = (sem("a_qk_done"), sem("a_qk_evac"), sem("a_q_ready"),
                                                         sem("a_kr_ready"), sem("a_qr_ready"))
        t_filled, t_emptied = sem("a_t_filled"), sem("a_t_emptied")
        lepe_done, kv_done, z_done, attn_done, kvb_ready = (sem("a_lepe_done"), sem("a_kv_done"), sem("a_z_done"),
                                                            sem("a_attn_done"), sem("a_kvb_ready"))
        v_ready, x1_ready = sem("a_v_ready"), sem("a_x1_ready")
        var2_ready, rstd2_ready, xg_ready = sem("a_var2_ready"), sem("a_rstd2_ready"), sem("a_xg_ready")
        w_ready = sem("a_w_ready")
        x_stored, xg_stored = sem("a_x_stored"), sem("a_xg_stored")
        passed_dve, passed_pool = sem("a_passed_dve"), sem("a_passed_pool")
        block = ctx.enter_context(nc.Block())

        def round_gate(b):
            return 4 * b - 1 if not (isinstance(b, int) and b == B) else 4 * B - 2

        def round_next(b):
            return 4 * b + 1

        def round_k(b):
            return 4 * b + 2 if not is_last(b) else 4 * b + 1

        @block.sync
        def _(sp):
            xv = x_dram.rearrange("b (t p) c -> p (b t) c", p=P)
            sp.dma_start(x[:, 0:TB, :], xv[:, 0:TB, :]).then_inc(x0_in, 16)
            sp.dma_start(qk_raw[:], qk_w.rearrange("(k p) n -> p k n", p=P)).then_inc(w_in, 16)
            sp.dma_start(qk_bias[:].rearrange("p (h two) -> p h two", two=2),
                         qk_b.rearrange("(h i two) -> i h two", h=2, two=2)).then_inc(w_in, 16)
            sp.dma_start(x[:, TB:2 * TB, :], xv[:, TB:2 * TB, :]).then_inc(x1_in, 16)
            sp.dma_start(lepe_s[:], lepe_w.rearrange("t (k p) n -> p t k n", p=P)).then_inc(wl_in, 16)
            sp.dma_start(x[:, 2 * TB:, :], xv[:, 2 * TB:, :]).then_inc(x_in, 16)

            def store(b, par):
                sp.wait_ge(x1_ready, 2 * b + 2)
                sp.dma_start(token_rows(x_dram_out, b), sequence_tiles(x, b)).then_inc(x_stored, 16)
                sp.wait_ge(xg_ready, b + 1)
                sp.dma_start(token_rows(normed_dram, b), xg[:]).then_inc(xg_stored, 16)

            over_batches(sp, store)
            sp.wait_ge(x_stored, 16 * B)
            sp.wait_ge(xg_stored, 16 * B)

        @block.scalar
        def _(act):
            act.dma_start(cos_s[:, 0, :], cos_t).then_inc(tab_in, 16)
            act.dma_start(sin_s[:], sin_t).then_inc(tab_in, 16)
            act.dma_start(lepe_bias[:, 0, :], lepe_b.partition_broadcast(P)).then_inc(tab_in, 16)
            for k in range(KC):
                act.dma_start(gate_s[:, k, :], gate_w[:, k * P:(k + 1) * P].rearrange("e p -> p e"),
                              allow_slow_non_contiguous=True).then_inc(wg_in, 16)

            def evacuate_next(r, dst):
                act.wait_ge(t_filled, r + 1)
                for k in range(KC):
                    last = nc.scalar.activation(dst[:, k, 1:N + 1], tbk[k][:], ACT.Copy)
                last.then_inc(t_emptied, 1)

            def gate_part(b):
                r = round_gate(b)
                act.wait_ge(t_filled, r + 1)
                for k in range(KC):
                    last = nc.scalar.activation(xgT[:, k, :], tbk[k][:], ACT.Copy)
                last.then_inc(t_emptied, 1)
                act.wait_ge(t_filled, r + 2)
                nc.scalar.activation(sequence_tiles(logits, b - 1),
                                     tb0[:, 0:TB * EX].rearrange("p (t e) -> p t e", e=EX),
                                     ACT.Copy).then_inc(t_emptied, 1)

            evacuate_next(0, xnT[0])
            act.wait_ge(w_in, 32)

            def period(b, par):
                wait_count(act, q_ready, b)
                for n, m in enumerate(ORDER):
                    act.wait_ge(qk_done, 4 * b + n + 1)
                    nc.scalar.activation(ex[:, m, :], proj[m][:], ACT.Exp, bias=qk_bias[:, m:m + 1])
                    nc.scalar.activation(re[:, m, :], proj[m][:], ACT.Relu, bias=qk_bias[:, m:m + 1]).then_inc(qk_evac, 1)
                if not is_first(b):
                    gate_part(b)
                if not is_last(b):
                    evacuate_next(round_next(b), xnT[1 - par])
                act.wait_ge(t_filled, round_k(b) + 1)
                for k in range(KC):
                    last = nc.scalar.activation(krt[:, k, :, :].rearrange("p t d -> p (t d)"), tbk[k][:], ACT.Copy)
                last.then_inc(t_emptied, 1)

            over_batches(act, period)
            gate_part(B)

        @block.gpsimd
        def _(pool):
            own = OwnSteps(pool, own_pool, 4)

            def rstd(mvt, ready, done):
                own.link(nc.gpsimd.tensor_scalar(mvt[:, :, 1], mvt[:, :, 1], EPS, None, ALU.add))
                nc.gpsimd.tensor_tensor(mvt[:, :, 1], mvt[:, :, 1], neg_half[:, 0:TB], ALU.pow).then_inc(done, 1)

            def add_bias(b):
                xt = sequence_tiles(x, b)
                nc.gpsimd.tensor_tensor(xt, xt, lepe_bias[:].to_broadcast([P, TB, C]), ALU.add)

            own.round(0)
            pool.wait_ge(var_ready, 1)
            rstd(mv, var_ready, rstd_ready)
            pool.wait_ge(tab_in, 48)
            pool.wait_ge(xn_ready, 1)
            add_bias(0)
            own.pad()

            def period(b, par):
                own.round(b + 1)
                if not is_last(b):
                    wait_apart(pool, var_ready, b + 2, passed_pool)
                    rstd(mv, var_ready, rstd_ready)
                if not is_first(b):
                    wait_apart(pool, var2_ready, b, passed_pool)
                    rstd(mv2, var2_ready, rstd2_ready)
                pool.wait_ge(q_ready, b + 1)
                wait_count(pool, attn_done, 2 * b)
                nc.gpsimd.tensor_tensor(qA[:], el[:, 0:2, :], cos_s[:].to_broadcast([P, 2, N]), ALU.mult)
                nc.gpsimd.tensor_tensor(qB[:, 0, :], el[:, 1, :], nsin_s[:], ALU.mult)
                own.link(nc.gpsimd.tensor_tensor(qB[:, 1, :], el[:, 0, :], sin_s[:], ALU.mult))
                nc.gpsimd.tensor_tensor(qr[:], qA[:], qB[:], ALU.add).then_inc(qr_ready, 1)
                if not is_last(b):
                    wait_apart(pool, xn_ready, b + 2, passed_pool)
                    add_bias(b + 1)
                for h in range(2):
                    wait_apart(pool, v_ready, 2 * b + h + 1, passed_pool)
                    xt = x[:, bass.ds(b * TB + 2 * h, 2), :] if not isinstance(b, int) else x[:, b * TB + 2 * h:b * TB + 2 * h + 2, :]
                    nc.gpsimd.tensor_tensor(xt, xt, v[:, h, :, :], ALU.add).then_inc(x1_ready, 1)
                own.pad()

            over_batches(pool, period)
            own.round(B + 1)
            pool.wait_ge(var2_ready, B)
            rstd(mv2, var2_ready, rstd2_ready)

        @block.vector
        def _(dve):
            own = OwnSteps(dve, own_dve, 8)

            def statistics(bnt, mvt, b, done):
                for j in range(TB):
                    last = nc.vector.bn_stats(bnt[:, j, :], tile_of(x, b, j))
                own.link(last, passed_dve)
                for j in range(TB):
                    last = nc.vector.bn_aggr(mvt[:, j, :], bnt[:, j, :])
                last.then_inc(done, 1)

            def normalise(dst, mvt, b, done):
                for j in range(TB):
                    last = nc.vector.tensor_scalar(dst[:, j, :], tile_of(x, b, j), mvt[:, j, 0:1], mvt[:, j, 1:2],
                                                   ALU.subtract, ALU.mult)
                last.then_inc(done, 1)

            own.round(0)
            for t in xnT:
                nc.vector.memset(t[:, :, 0:1], 0.0)
                nc.vector.memset(t[:, :, N + 1:N + 2], 0.0)
            dve.wait_ge(x0_in, 16)
            statistics(bn, mv, 0, var_ready)
            dve.wait_ge(w_in, 32)
            for h in range(2):
                for par in range(2):
                    last = nc.vector.tensor_copy(qk_s[:, :, 2 * h + par, :],
                                                 qk_raw[:, :, h * C + par:(h + 1) * C:2])
            last.then_inc(w_ready, 1)
            dve.wait_ge(rstd_ready, 1)
            normalise(xn[0], mv, 0, xn_ready)
            dve.wait_ge(tab_in, 48)
            own.link(nc.vector.tensor_scalar(nsin_s[:], sin_s[:], -1.0, None, ALU.mult))
            dve.wait_ge(x1_in, 16)
            own.pad()

            def route_before(b):
                dve.wait_ge(rstd2_ready, b)
                wait_count(dve, xg_stored, 16 * (b - 1))
                normalise(xg, mv2, b - 1, xg_ready)

            def period(b, par):
                own.round(b + 1)
                if isinstance(b, int) and b == 1 or not isinstance(b, int):
                    dve.wait_ge(x_in, 16)
                if not is_last(b):
                    statistics(bn, mv, b + 1, var_ready)
                if not is_first(b):
                    dve.wait_ge(x1_ready, 2 * b)
                    statistics(bn2, mv2, b - 1, var2_ready)
                dve.wait_ge(qk_evac, 4 * b + 2)
                for m in (2, 3):
                    last = nc.vector.scalar_tensor_tensor(out=el[:, m, :], in0=ex[:, m, :], scalar=1.0, in1=re[:, m, :],
                                                          op0=ALU.min, op1=ALU.add, accum_out=ksum[:, m - 2:m - 1])
                own.link(last)
                if not is_first(b):
                    route_before(b)
                for m in range(2):
                    nc.vector.tensor_scalar(kz[:, m, :], head_mask[:], ksum[:, m:m + 1], None, ALU.mult)
                nc.vector.tensor_tensor(kA[:], el[:, 2:4, :], cos_s[:].to_broadcast([P, 2, N]), ALU.mult)
                nc.vector.tensor_tensor(kB[:, 0, :], el[:, 3, :], nsin_s[:], ALU.mult)
                own.link(nc.vector.tensor_tensor(kB[:, 1, :], el[:, 2, :], sin_s[:], ALU.mult))
                nc.vector.tensor_tensor(kr[:], kA[:], kB[:], ALU.add).then_inc(kr_ready, 1)
                dve.wait_ge(qk_evac, 4 * b + 4)
                wait_count(dve, qr_ready, b)
                nc.vector.scalar_tensor_tensor(out=el[:, 0:2, :], in0=ex[:, 0:2, :], scalar=1.0, in1=re[:, 0:2, :],
                                               op0=ALU.min, op1=ALU.add).then_inc(q_ready, 1)
                if not is_last(b):
                    dve.wait_ge(rstd_ready, b + 2)
                    normalise(xn[1 - par], mv, b + 1, xn_ready)
                dve.wait_ge(z_done, b + 1)
                own.link(nc.vector.tensor_scalar(zr[:], q1[:, 0:TB * HEADS], 1e-6, None, ALU.add))
                dve.wait_ge(kv_done, b + 1)
                nc.vector.tensor_tensor(kvb[:], q0[:, 0:C].rearrange("p (k e) -> p k e", k=KC),
                                        block_mask[:].unsqueeze(1).to_broadcast([P, KC, P]), ALU.mult).then_inc(kvb_ready, 1)
                own.link(nc.vector.reciprocal(zr[:], zr[:]))
                dve.wait_ge(lepe_done, 2 * b + 2)
                for h in range(2):
                    dve.wait_ge(attn_done, 2 * b + h + 1)
                    zb = zr[:, h * 2 * HEADS:(h + 1) * 2 * HEADS].unsqueeze(2).to_broadcast([P, 2 * HEADS, HD])
                    own.link(nc.vector.tensor_tensor(u[:, h, :].rearrange("p (g e) -> p g e", e=HD),
                                                     q[2 + h][:].rearrange("p (g e) -> p g e", e=HD), zb, ALU.mult))
                    wait_count(dve, x1_ready, 2 * b + h - 1)
                    nc.vector.tensor_tensor(v[:, h, :, :].rearrange("p t c -> p (t c)"), u[:, h, :], lb[h][:],
                                            ALU.add).then_inc(v_ready, 1)
                own.pad()

            over_batches(dve, period)
            own.round(B + 1)
            dve.wait_ge(x1_ready, 2 * B)
            statistics(bn2, mv2, B - 1, var2_ready)
            route_before(B)
            own.pad()

        @block.tensor
        def _(pe):
            def transposes(src, filled_round):
                wait_count(pe, t_emptied, filled_round)
                for k in range(KC):
                    for j in range(TB):
                        last = nc.tensor.transpose(tbk[k][:, j * P:(j + 1) * P], src[:, j, k * P:(k + 1) * P], ident[:])
                last.then_inc(t_filled, 1)

            def gate_transposes(b):
                pe.wait_ge(xg_ready, b)
                transposes(xg, round_gate(b))

            def gate_products(b):
                pe.wait_ge(t_emptied, round_gate(b) + 1)
                for j in range(TB):
                    for k in range(KC):
                        last = nc.tensor.matmul(tb0[:, j * EX:(j + 1) * EX], xgT[:, k, j * P:(j + 1) * P], gate_s[:, k, :],
                                                start=(k == 0), stop=(k == KC - 1))
                last.then_inc(t_filled, 1)

            def convolution(par, j, taps=range(LT)):
                for t in taps:
                    for k in range(KC):
                        last = nc.tensor.matmul(lb[j // 2][:, (j % 2) * C:(j % 2 + 1) * C],
                                                xnT[par][:, k, j * P + t:j * P + t + P], lepe_s[:, t, k, :],
                                                start=(t == k == 0), stop=(t == LT - 1 and k == KC - 1))
                if j % 2 and LT - 1 in taps:
                    last.then_inc(lepe_done, 1)

            pe.wait_ge(xn_ready, 1)
            transposes(xn[0], 0)
            pe.wait_ge(w_ready, 1)
            pe.wait_ge(w_in, 32)

            def period(b, par):
                pe.wait_ge(t_emptied, round_next(b - 1) + 1 if not is_first(b) else 1)
                for m in ORDER:
                    if m == 0:
                        wait_count(pe, v_ready, 2 * b)
                    for k in range(KC):
                        last = nc.tensor.matmul(proj[m][:], qk_s[:, k, m, :], xnT[par][:, k, 1:N + 1],
                                                start=(k == 0), stop=(k == KC - 1))
                    last.then_inc(qk_done, 1)
                if is_first(b):
                    pe.wait_ge(wl_in, 16)
                    pe.wait_ge(wg_in, 16 * KC)
                convolution(par, 0)
                convolution(par, 1)
                if not is_first(b):
                    gate_transposes(b)
                convolution(par, 2)
                if not is_first(b):
                    gate_products(b)
                convolution(par, 3, (0,))
                if not is_last(b):
                    pe.wait_ge(xn_ready, b + 2)
                    transposes(xn[1 - par], round_next(b))
                convolution(par, 3, (1,))
                pe.wait_ge(kr_ready, b + 1)
                pe.wait_ge(t_emptied, round_k(b))
                for k in range(KC):
                    for j in range(TB):
                        last = nc.tensor.transpose(tbk[k][:, j * P:(j + 1) * P], kr[:, k, j * P:(j + 1) * P], ident[:])
                last.then_inc(t_filled, 1)
                pe.wait_ge(q_ready, b + 1)
                for j in range(TB):
                    for m in range(2):
                        last = nc.tensor.matmul(q1[:, j * HEADS:(j + 1) * HEADS], el[:, m, j * P:(j + 1) * P], kz[:, m, :],
                                                start=(m == 0), stop=(m == 1))
                last.then_inc(z_done, 1)
                pe.wait_ge(t_emptied, round_k(b) + 1)
                for k in range(KC):
                    for j in range(TB):
                        last = nc.tensor.matmul(q0[:, k * P:(k + 1) * P], krt[:, k, j, :], xn[par][:, j, k * P:(k + 1) * P],
                                                start=(j == 0), stop=(j == TB - 1))
                last.then_inc(kv_done, 1)
                convolution(par, 3, (2,))
                pe.wait_ge(kvb_ready, b + 1)
                pe.wait_ge(qr_ready, b + 1)
                for j in range(TB):
                    for k in range(KC):
                        last = nc.tensor.matmul(q[2 + j // 2][:, (j % 2) * C + k * P:(j % 2) * C + (k + 1) * P],
                                                qr[:, k, j * P:(j + 1) * P], kvb[:, k, :], start=True, stop=True)
                    if j % 2:
                        last.then_inc(attn_done, 1)

            over_batches(pe, period)
            gate_transposes(B)
            gate_products(B)


def phase_route(nc, tag, logits, row_token, row_score, block_expert, bank):
    BLOCKS = NBLK
    with ExitStack() as ctx:
        def sb(name, shape, dt=F32):
            return ctx.enter_context(nc.sbuf_tensor(name, shape, dt))

        def sem(name):
            return ctx.enter_context(nc.semaphore(name))

        top = sb(tag + "r_top", [P, T, 8])
        topi = sb(tag + "r_topi", [P, T, 8], U32)
        idx = sb(tag + "r_idx", [P, TOPK, T])
        diff = sb(tag + "r_diff", [P, T, EX])
        prob = sb(tag + "r_prob", [P, T, EX])
        d2 = sb(tag + "r_d2", [P, T])
        p2 = sb(tag + "r_p2", [P, T])
        tot_p = sb(tag + "r_tot_p", [P, T])
        rz = sb(tag + "r_rz", [P, T])
        expert_id = sb(tag + "r_expert_id", [P, EX, T])
        keep = sb(tag + "r_keep", [P, EX * T])
        ones_e = sb(tag + "r_ones_e", [P, EX])
        hot = sb(tag + "r_hot", [P, TOPK, EX, T])
        both = sb(tag + "r_both", [P, EX, T])
        before = sb(tag + "r_before", [P, P])
        ones = sb(tag + "r_ones", [P, P])
        tot = sb(tag + "r_tot", [P, EX, T])
        incl = sb(tag + "r_incl", [P, EX, T])
        counti = sb(tag + "r_counti", [P, EX], I32)
        padded = sb(tag + "r_padded", [P, EX])
        endp = sb(tag + "r_endp", [P, EX])
        base = sb(tag + "r_base", [P, EX, 1])
        place = sb(tag + "r_place", [P, EX, T])
        prod = sb(tag + "r_prod", [P, TOPK, EX, T])
        posf = sb(tag + "r_posf", [P, TOPK, T])
        row0 = sb(tag + "r_row0", [1, BLOCKS, EX])
        past = sb(tag + "r_past", [1, BLOCKS, EX])
        ebf = sb(tag + "r_ebf", [1, BLOCKS])
        score = sb(tag + "r_score", [P, TOPK, T])
        posi = sb(tag + "r_posi", [P, 2, TOPK, T], I32)
        blk = sb(tag + "r_blk", [P, 2, TOPK, T])
        lane = sb(tag + "r_lane", [P, P])
        blocks = sb(tag + "r_blocks", [P, BLOCKS])
        lane_of = sb(tag + "r_lane_of", [P, 1])
        token = sb(tag + "r_token", [P, T])
        CH = 4
        row_hot = [sb(tag + f"r_row_hot{i}", [P, TOPK, CH, P]) for i in range(2)]
        block_hot = [sb(tag + f"r_block_hot{i}", [P, TOPK, CH, BLOCKS]) for i in range(2)]
        sent = [sb(tag + f"r_sent{i}", [P, TOPK, CH, 2, BLOCKS]) for i in range(2)]
        spare = sb(tag + "r_spare", [P, BLOCKS])
        own_dve, made, top_ready, exp_done, both_ready, count_done, pos_ready = (
            sem(tag + "r_own_dve"), sem(tag + "r_made"), sem(tag + "r_top_ready"), sem(tag + "r_exp_done"), sem(tag + "r_both_ready"),
            sem(tag + "r_count_done"), sem(tag + "r_pos_ready"))
        row_hot_ready, block_hot_ready, scores_sent, tokens_sent, sent_used = (
            sem(tag + "r_row_hot_ready"), sem(tag + "r_block_hot_ready"), sem(tag + "r_scores_sent"),
            sem(tag + "r_tokens_sent"), sem(tag + "r_sent_used"))
        block = ctx.enter_context(nc.Block())

        @block.gpsimd
        def _(pool):
            nc.gpsimd.iota(expert_id[:], pattern=[[1, EX], [0, T]], base=0, channel_multiplier=0,
                           allow_small_or_imprecise_dtypes=True).then_inc(made, 1)
            nc.gpsimd.iota(row0[:], pattern=[[P, BLOCKS], [0, EX]], base=0, channel_multiplier=0,
                           allow_small_or_imprecise_dtypes=True).then_inc(made, 1)
            nc.gpsimd.memset(keep[:], 1.0).then_inc(made, 1)
            nc.gpsimd.memset(ones_e[:], 1.0).then_inc(made, 1)
            nc.gpsimd.memset(ones[:], 1.0).then_inc(made, 1)
            nc.gpsimd.memset(before[:], 1.0).then_inc(made, 1)
            pool.wait_ge(made, 6)
            nc.gpsimd.memset(keep[:].rearrange("p (e t) -> p e t", t=T)[:, :, 0:1], 0.0).then_inc(made, 1)
            nc.gpsimd.affine_select(out=before[:], in_=before[:], compare_op=ALU.is_ge, fill=0.0, base=-1,
                                    pattern=[[1, P]], channel_multiplier=-1).then_inc(made, 1)
            nc.gpsimd.iota(lane[:], pattern=[[1, P]], base=0, channel_multiplier=0,
                           allow_small_or_imprecise_dtypes=True).then_inc(made, 1)
            nc.gpsimd.iota(blocks[:], pattern=[[1, BLOCKS]], base=0, channel_multiplier=0,
                           allow_small_or_imprecise_dtypes=True).then_inc(made, 1)
            nc.gpsimd.iota(lane_of[:], pattern=[[0, 1]], base=0, channel_multiplier=1,
                           allow_small_or_imprecise_dtypes=True).then_inc(made, 1)
            nc.gpsimd.iota(token[:], pattern=[[P, T]], base=-T * P, channel_multiplier=1,
                           allow_small_or_imprecise_dtypes=True).then_inc(made, 1)
            pool.wait_ge(made, 12)
            for g in range(T // CH):
                pool.wait_ge(block_hot_ready, g + 1)
                if g >= 2:
                    pool.wait_ge(sent_used, g - 1)
                ids = token[:, g * CH:(g + 1) * CH].unsqueeze(2).to_broadcast([P, CH, BLOCKS])
                for k in range(TOPK):
                    last = nc.gpsimd.tensor_tensor(sent[g % 2][:, k, :, 0, :], block_hot[g % 2][:, k, :, :], ids, ALU.mult)
                last.then_inc(tokens_sent, 1)

        @block.scalar
        def _(act):
            act.wait_ge(top_ready, 1)
            nc.scalar.activation(prob[:], diff[:], ACT.Exp)
            nc.scalar.activation(p2[:], d2[:], ACT.Exp).then_inc(exp_done, 1)

        @block.tensor
        def _(pe):
            pe.wait_ge(made, 8)
            pe.wait_ge(both_ready, 1)
            m = both[:].rearrange("p e t -> p (e t)")
            nc.tensor.matmul(bank[0][:, 0:EX * T], before[:], m, start=True, stop=True)
            nc.tensor.matmul(bank[1][:, 0:EX * T], ones[:], m, start=True, stop=True).then_inc(count_done, 1)
            out = bank[2][:, 0:2 * BLOCKS]
            for g in range(T // CH):
                pe.wait_ge(row_hot_ready, g + 1)
                pe.wait_ge(scores_sent, g + 1)
                pe.wait_ge(tokens_sent, g + 1)
                for k in range(TOPK):
                    for j in range(CH):
                        first, final = g == k == j == 0, g == T // CH - 1 and k == TOPK - 1 and j == CH - 1
                        last = nc.tensor.matmul(out, row_hot[g % 2][:, k, j, :],
                                                sent[g % 2][:, k, j, :, :].rearrange("p a b -> p (a b)"),
                                                start=first, stop=final)
                last.then_inc(sent_used, 1)

        @block.vector
        def _(dve):
            own = OwnSteps(dve, own_dve, 0)
            for t in range(T):
                last = nc.vector.max(top[:, t, :], logits[:, t, :])
            own.link(last)
            for t in range(T):
                last = nc.vector.max_index(topi[:, t, :], top[:, t, :], logits[:, t, :])
            nc.vector.tensor_tensor(d2[:], top[:, :, 1], top[:, :, 0], ALU.subtract)
            nc.vector.tensor_tensor(diff[:], logits[:], top[:, :, 0:1].to_broadcast([P, T, EX]),
                                    ALU.subtract).then_inc(top_ready, 1)
            dve.wait_ge(top_ready, 1)
            own.link(nc.vector.tensor_copy(idx[:], topi[:, :, 0:TOPK].rearrange("p t k -> p k t")))
            dve.wait_ge(made, 8)
            for k in range(TOPK):
                last = nc.vector.tensor_tensor(hot[:, k, :, :], idx[:, k:k + 1, :].to_broadcast([P, EX, T]),
                                               expert_id[:], ALU.is_equal)
            own.link(last)
            nc.vector.tensor_tensor(both[:], hot[:, 0, :, :], hot[:, 1, :, :], ALU.add).then_inc(both_ready, 1)
            dve.wait_ge(exp_done, 1)
            own.link(nc.vector.tensor_reduce(tot_p[:], prob[:], AXX, ALU.add))
            own.link(nc.vector.reciprocal(rz[:], tot_p[:]))
            nc.vector.tensor_copy(score[:, 0, :], rz[:])
            nc.vector.tensor_tensor(score[:, 1, :], p2[:], rz[:], ALU.mult)
            dve.wait_ge(count_done, 1)
            own.link(nc.vector.tensor_copy(tot[:].rearrange("p e t -> p (e t)"), bank[1][:, 0:EX * T]))
            own.link(nc.vector.tensor_tensor_scan(incl[:].rearrange("p e t -> p (e t)"), keep[:],
                                                  tot[:].rearrange("p e t -> p (e t)"), 0.0, ALU.mult, ALU.add))
            own.link(nc.vector.tensor_scalar(counti[:], incl[:, :, T - 1], float(P - 1), None, ALU.add))
            own.link(nc.vector.tensor_scalar(counti[:], counti[:], 7, 7, ALU.arith_shift_right, ALU.logical_shift_left))
            own.link(nc.vector.tensor_copy(padded[:], counti[:]))
            own.link(nc.vector.tensor_tensor_scan(endp[:], ones_e[:], padded[:], 0.0, ALU.mult, ALU.add))
            nc.vector.tensor_tensor(base[:, :, 0], endp[:], padded[:], ALU.subtract)
            own.link(nc.vector.tensor_tensor(place[:], incl[:], tot[:], ALU.subtract))
            own.link(nc.vector.tensor_tensor(place[:], place[:], base[:].to_broadcast([P, EX, T]), ALU.add))
            own.link(nc.vector.tensor_tensor(place[:], place[:], bank[0][:, 0:EX * T].rearrange("p (e t) -> p e t", t=T),
                                             ALU.add))
            own.link(nc.vector.tensor_tensor(prod[:], hot[:], place[:].unsqueeze(1).to_broadcast([P, TOPK, EX, T]), ALU.mult))
            own.link(nc.vector.tensor_reduce(posf[:], prod[:].rearrange("p k e t -> p k t e"), AXX, ALU.add))
            own.link(nc.vector.tensor_copy(posi[:, 0], posf[:]))
            own.link(nc.vector.tensor_scalar(posi[:, 1], posi[:, 0], P - 1, None, ALU.bitwise_and))
            own.link(nc.vector.tensor_scalar(posi[:, 0], posi[:, 0], 7, None, ALU.arith_shift_right))
            own.link(nc.vector.tensor_copy(blk[:], posi[:]))
            own.link(nc.vector.tensor_tensor(past[:], row0[:], endp[0:1, :].unsqueeze(1).to_broadcast([1, BLOCKS, EX]), ALU.is_ge))
            own.link(nc.vector.tensor_reduce(ebf[:], past[:], AXX, ALU.add))
            own.link(nc.vector.tensor_scalar(block_expert[:], ebf[:], float(EX - 1), None, ALU.min))
            dve.wait_ge(made, 12)
            for g in range(T // CH):
                if g >= 2:
                    dve.wait_ge(sent_used, g - 1)
                tiles = slice(g * CH, (g + 1) * CH)
                for k in range(TOPK):
                    last = nc.vector.tensor_tensor(
                        block_hot[g % 2][:, k], blk[:, 0, k, tiles].unsqueeze(2).to_broadcast([P, CH, BLOCKS]),
                        blocks[:].unsqueeze(1).to_broadcast([P, CH, BLOCKS]), ALU.is_equal)
                last.then_inc(block_hot_ready, 1)
                for k in range(TOPK):
                    last = nc.vector.tensor_tensor(
                        row_hot[g % 2][:, k], blk[:, 1, k, tiles].unsqueeze(2).to_broadcast([P, CH, P]),
                        lane[:].unsqueeze(1).to_broadcast([P, CH, P]), ALU.is_equal)
                last.then_inc(row_hot_ready, 1)
                dve.wait_ge(block_hot_ready, g + 1)
                for k in range(TOPK):
                    last = nc.vector.tensor_tensor(
                        sent[g % 2][:, k, :, 1, :], block_hot[g % 2][:, k],
                        score[:, k, tiles].unsqueeze(2).to_broadcast([P, CH, BLOCKS]), ALU.mult)
                last.then_inc(scores_sent, 1)
            dve.wait_ge(sent_used, T // CH)
            nc.vector.tensor_copy(row_score[:], bank[2][:, BLOCKS:2 * BLOCKS])
            own.link(nc.vector.tensor_scalar(spare[:], bank[2][:, 0:BLOCKS], 0.0, lane_of[:, 0:1], ALU.is_equal, ALU.mult))
            own.link(nc.vector.scalar_tensor_tensor(out=row_token[:], in0=bank[2][:, 0:BLOCKS], scalar=float(T * P),
                                                    in1=spare[:], op0=ALU.add, op1=ALU.add))


def over_blocks(engine, body):
    assert NBLK % 2 == 1
    for i in range(3):
        body(i, i % 2)
    with engine.Fori(3, NBLK - 3, 2) as i:
        body(i, 1)
        body(i + 1, 0)
    for i in range(NBLK - 2, NBLK):
        body(i, i % 2)


def phase_experts(nc, tag, normed_dram, x_dram, w1, w2, w3, logits, ident, bank):
    with ExitStack() as ctx:
        def sb(name, shape, dt=F32):
            return ctx.enter_context(nc.sbuf_tensor(tag + name, shape, dt))

        w1_s, w3_s, w2_s = (sb("w1", [P, EX, KC * H]), sb("w3", [P, EX, KC * H]), sb("w2", [P, EX, HC * C]))
        row_token = sb("row_token", [P, NBLK], U32)
        row_score = sb("row_score", [P, NBLK])
        block_expert = sb("block_expert", [1, NBLK], I32)
        w_in = [ctx.enter_context(nc.semaphore(tag + f"w{n}_in")) for n in (1, 2, 3)]
        load_weights(nc, w1, w2, w3, w1_s, w2_s, w3_s, w_in)
        phase_route(nc, tag, logits, row_token, row_score, block_expert, bank)
        phase_blocks(nc, tag, normed_dram, x_dram, w1_s, w2_s, w3_s, w_in, row_token, row_score, block_expert, ident, bank)


def load_weights(nc, w1, w2, w3, w1_s, w2_s, w3_s, w_in):
    block = nc.Block()
    with block:
        @block.sync
        def _(sp):
            for e in range(EX):
                sp.dma_start(w1_s[:, e, :].rearrange("p (k h) -> p k h", h=H),
                             w1[e].rearrange("(k p) h -> p k h", p=P)).then_inc(w_in[0], 16)
            for e in range(EX):
                sp.dma_start(w2_s[:, e, :].rearrange("p (k c) -> p k c", c=C),
                             w2[e].rearrange("(k p) c -> p k c", p=P)).then_inc(w_in[1], 16)

        @block.scalar
        def _(act):
            for e in range(EX):
                act.dma_start(w3_s[:, e, :].rearrange("p (k h) -> p k h", h=H),
                              w3[e].rearrange("(k p) h -> p k h", p=P)).then_inc(w_in[2], 16)


def phase_blocks(nc, tag, normed_dram, x_dram, w1_s, w2_s, w3_s, w_in, row_token, row_score, block_expert, ident, bank):
    a_bank, b_bank, th_bank, xt_bank, y_bank = bank[0:2], bank[2:4], bank[4:6], bank[6], bank[7]
    with ExitStack() as ctx:
        def sb(name, shape, dt=F32):
            return ctx.enter_context(nc.sbuf_tensor(name, shape, dt))

        def sem(name):
            return ctx.enter_context(nc.semaphore(name))

        xs = [sb(tag + f"m_xs{i}", [P, C]) for i in range(2)]
        xT = [sb(tag + f"m_xT{i}", [P, KC, P]) for i in range(2)]
        g = [sb(tag + f"m_g{i}", [P, H]) for i in range(2)]
        h = [sb(tag + f"m_h{i}", [P, H]) for i in range(2)]
        hT = [sb(tag + f"m_hT{i}", [P, HC, P]) for i in range(2)]
        y = [sb(tag + f"m_y{i}", [P, C]) for i in range(2)]
        gather_token = [sb(tag + f"m_gather_token{i}", [P, 1], U32) for i in range(2)]
        add_token = [sb(tag + f"m_add_token{i}", [P, 1], U32) for i in range(2)]
        loaded = [sem(tag + f"m_loaded{i}") for i in range(2)]
        added = sem(tag + "m_added")
        own_pool, passed_pool = sem(tag + "m_own_pool"), sem(tag + "m_passed_pool")
        a_done, b_done, th_done, xt_done, y_done = (sem(tag + "m_a_done"), sem(tag + "m_b_done"), sem(tag + "m_th_done"),
                                                    sem(tag + "m_xt_done"), sem(tag + "m_y_done"))
        silu_done, th_evac, h_ready, xT_ready, y_evac = (sem(tag + "m_silu_done"), sem(tag + "m_th_evac"), sem(tag + "m_h_ready"),
                                                         sem(tag + "m_xT_ready"), sem(tag + "m_y_evac"))
        block = ctx.enter_context(nc.Block())

        def column(t, i):
            return t[:, bass.ds(i, 1)] if not isinstance(i, int) else t[:, i:i + 1]

        @block.gpsimd
        def _(pool):
            own = OwnSteps(pool, own_pool, 2)

            def gather(i, par):
                wait_count(pool, xt_done, i - 1)
                own.link(nc.gpsimd.tensor_copy(gather_token[par][:], column(row_token, i)), passed_pool)
                nc.gpsimd.indirect_dma_start(xs[par][:], None, normed_dram[:],
                                             bass.IndirectOffsetOnAxis(ap=gather_token[par][:], axis=0)
                                             ).then_inc(loaded[par], 16)

            def add(i, par):
                pool.wait_ge(y_evac, i + 1)
                own.link(nc.gpsimd.tensor_copy(add_token[par][:], column(row_token, i)), passed_pool)
                if not is_first(i):
                    wait_apart(pool, added, 16 * i, passed_pool)
                nc.gpsimd.indirect_dma_start(x_dram[:], bass.IndirectOffsetOnAxis(ap=add_token[par][:], axis=0),
                                             y[par][:], None, compute_op=ALU.add).then_inc(added, 16)

            own.round(0)
            gather(0, 0)
            gather(1, 1)

            def step(i, par):
                own.round(i + 1)
                if not (isinstance(i, int) and i >= NBLK - 2):
                    gather(i + 2, par)
                if not is_first(i):
                    add(i - 1, 1 - par)
                own.pad()

            over_blocks(pool, step)
            own.round(NBLK + 1)
            add(NBLK - 1, 0)
            pool.wait_ge(added, 16 * NBLK)

        @block.scalar
        def _(act):
            def evacuate_h(i, par):
                act.wait_ge(th_done, i + 1)
                wait_count(act, y_done, i - 1)
                nc.scalar.activation(hT[par][:].rearrange("p k t -> p (k t)"), th_bank[par][:], ACT.Copy).then_inc(th_evac, 1)

            def step(i, par):
                act.wait_ge(a_done, i + 1)
                wait_count(act, h_ready, i - 1)
                nc.scalar.activation(g[par][:], a_bank[par][:], ACT.Silu).then_inc(silu_done, 1)
                if not is_first(i):
                    evacuate_h(i - 1, 1 - par)

            over_blocks(act, step)
            evacuate_h(NBLK - 1, 0)

        @block.vector
        def _(dve):
            def evacuate_x(i, par):
                dve.wait_ge(xt_done, i + 1)
                wait_count(dve, b_done, i - 1)
                nc.vector.tensor_copy(xT[par][:].rearrange("p k t -> p (k t)"), xt_bank[:, 0:C]).then_inc(xT_ready, 1)

            def evacuate_y(i, par):
                dve.wait_ge(y_done, i + 1)
                if not (isinstance(i, int) and i < 2):
                    dve.wait_ge(added, 16 * (i - 1))
                nc.vector.tensor_scalar(y[par][:], y_bank[:, 0:C], column(row_score, i), None, ALU.mult).then_inc(y_evac, 1)

            evacuate_x(0, 0)

            def step(i, par):
                dve.wait_ge(silu_done, i + 1)
                dve.wait_ge(b_done, i + 1)
                wait_count(dve, th_done, i - 1)
                nc.vector.tensor_tensor(h[par][:], g[par][:], b_bank[par][:], ALU.mult).then_inc(h_ready, 1)
                if not (isinstance(i, int) and i == NBLK - 1):
                    evacuate_x(i + 1, 1 - par)
                if not is_first(i):
                    evacuate_y(i - 1, 1 - par)

            over_blocks(dve, step)
            evacuate_y(NBLK - 1, 0)

        @block.tensor
        def _(pe):
            def transpose_x(i, par):
                pe.wait_ge(loaded[par], 8 * (i - par) + 16)
                wait_count(pe, xT_ready, i)
                for k in range(KC):
                    last = nc.tensor.transpose(xt_bank[:, k * P:(k + 1) * P], xs[par][:, k * P:(k + 1) * P], ident[:])
                last.then_inc(xt_done, 1)

            def expert_of(i):
                return pe.value_load(block_expert[0:1, bass.ds(i, 1)] if not isinstance(i, int) else block_expert[0:1, i:i + 1],
                                     min_val=0, max_val=EX - 1)

            def weights(w, e):
                return w[:, bass.ds(e, 1), :].rearrange("p a n -> p (a n)")

            def up(w, e, par, out, done):
                for k in range(KC):
                    last = nc.tensor.matmul(out[:], xT[par][:, k, :], weights(w, e)[:, k * H:(k + 1) * H],
                                            start=(k == 0), stop=(k == KC - 1))
                last.then_inc(done, 1)

            def transpose_h(i, par):
                pe.wait_ge(h_ready, i + 1)
                wait_count(pe, th_evac, i - 1)
                for k in range(HC):
                    last = nc.tensor.transpose(th_bank[par][:, k * P:(k + 1) * P], h[par][:, k * P:(k + 1) * P], ident[:])
                last.then_inc(th_done, 1)

            def down(i, par, e):
                pe.wait_ge(th_evac, i + 1)
                wait_count(pe, y_evac, i)
                for k in range(HC):
                    last = nc.tensor.matmul(y_bank[:, 0:C], hT[par][:, k, :], weights(w2_s, e)[:, k * C:(k + 1) * C],
                                            start=(k == 0), stop=(k == HC - 1))
                last.then_inc(y_done, 1)

            transpose_x(0, 0)
            for weight_in in w_in:
                pe.wait_ge(weight_in, 16 * EX)

            def step(i, par):
                e = expert_of(i)
                pe.wait_ge(xT_ready, i + 1)
                wait_count(pe, silu_done, i - 1)
                up(w1_s, e, par, a_bank[par], a_done)
                if not is_first(i):
                    transpose_h(i - 1, 1 - par)
                wait_count(pe, h_ready, i - 1)
                up(w3_s, e, par, b_bank[par], b_done)
                if not (isinstance(i, int) and i == NBLK - 1):
                    transpose_x(i + 1, 1 - par)
                if not is_first(i):
                    down(i - 1, 1 - par, expert_of(i - 1))

            over_blocks(pe, step)
            transpose_h(NBLK - 1, 0)
            down(NBLK - 1, 0, expert_of(NBLK - 1))


def phase_mix(nc, ln1_w, ln1_b, ln2_w, ln2_b, time_decay, time_first, mix_k, mix_v, mix_r, w_key, w_value, w_recept,
              w_output, f_mix_k, f_mix_r, f_w_key, f_w_recept, f_w_value, gate_w,
              x_from, normed_dram, x_to, logits, ident, neg_half, bank):
    tbk, xb_ = bank[0:2], bank[2:8]
    with ExitStack() as ctx:
        def sb(name, shape, dt=F32):
            return ctx.enter_context(nc.sbuf_tensor("b_" + name, shape, dt))

        def sem(name):
            return ctx.enter_context(nc.semaphore("b_" + name))

        x = sb("x", [P, T, C])
        wk_s, wv_s, wr_s, wo_s, wf_s = (sb(f"w{n}", [P, KC, C]) for n in "kvrof")
        fk_s, fv_s, gate_s = sb("fk", [P, KC, F]), sb("fv", [P, FCH, C]), sb("gate", [P, KC, EX])
        vec = {n: sb(f"v_{n}", [P, KC]) for n in ("ln1_w", "ln1_b", "ln2_w", "ln2_b", "decay", "first", "mk", "mv", "mr",
                                                  "fmk", "fmr", "ndecay")}
        bn, mv, bn1, mv1 = sb("bn", [P, TB, 6]), sb("mv", [P, TB, 2]), sb("bn1", [P, TB, 6]), sb("mv1", [P, TB, 2])
        bn2, mv2, bng, mvg = sb("bn2", [P, TB, 6]), sb("mv2", [P, TB, 2]), sb("bng", [P, TB, 6]), sb("mvg", [P, TB, 2])
        mv_all = sb("mv_all", [P, T, 2])
        a, xn = sb("a", [P, TB, C]), sb("xn", [P, TB, C])
        xnT = sb("xnT", [P, KC, N + 1])
        dT = sb("dT", [P, KC, N])
        xk, xv, xr = sb("xk", [P, KC, N]), sb("xv", [P, KC, N]), sb("xr", [P, KC, N])
        k, v, sg = sb("k", [P, KC, N]), sb("v", [P, KC, N]), sb("sg", [P, KC, N])
        eps = sb("eps", [P, KC, N + 1])
        e1, e2, d1, d2 = (sb(n, [P, KC, N]) for n in ("e1", "e2", "d1", "d2"))
        al, be = sb("al", [P, KC, N + 1]), sb("be", [P, KC, N + 1])
        dv, ev, gT = sb("dv", [P, KC, N]), sb("ev", [P, KC, N]), sb("gT", [P, KC, N])
        xb, xn2, xn2T = sb("xb", [P, TB, C]), sb("xn2", [P, TB, C]), sb("xn2T", [P, KC, N + 1])
        xfk, xfr = sb("xfk", [P, KC, N]), sb("xfr", [P, KC, N])
        hT, fs = sb("hT", [P, FCH, N]), sb("fs", [P, 2, N])
        xg, xgT = sb("xg", [P, TB, C]), sb("xgT", [P, KC, N])

        w_in, v_in, prep = sem("w_in"), sem("v_in"), sem("prep")
        x_in = [sem(f"x_in{i}") for i in range(3)]
        x_stored, xg_stored = sem("x_stored"), sem("xg_stored")
        own_f, own_m, own_r, own_w, own_g = (sem(f"own_{n}") for n in "fmrwg")
        eps_ready, a_ready, xb_added, passed_act = sem("eps_ready"), sem("a_ready"), sem("xb_added"), sem("passed_act")
        num_scaled, num_summed, num_ready = sem("num_scaled"), sem("num_summed"), sem("num_ready")
        own_pool, passed_dve, passed_pool = sem("own_pool"), sem("passed_dve"), sem("passed_pool")
        var_ready, rstd_ready, var1_ready, rstd1_ready = sem("var_ready"), sem("rstd_ready"), sem("var1_ready"), sem("rstd1_ready")
        var2_ready, rstd2_ready, varg_ready, rstdg_ready = sem("var2_ready"), sem("rstd2_ready"), sem("varg_ready"), sem("rstdg_ready")
        xn_ready, t_filled, t_emptied, mix_ready = sem("xn_ready"), sem("t_filled"), sem("t_emptied"), sem("mix_ready")
        kvr_done, kvr_evac, s_ready, d2_ready, expd = sem("kvr_done"), sem("kvr_evac"), sem("s_ready"), sem("d2_ready"), sem("expd")
        dv_ready, ev_ready, sg_ready, g_ready = sem("dv_ready"), sem("ev_ready"), sem("sg_ready"), sem("g_ready")
        wo_done, xb_ready, xn2_ready, mix2_ready = sem("wo_done"), sem("xb_ready"), sem("xn2_ready"), sem("mix2_ready")
        fk_done, h_relu, h_ready, fr_done = sem("fk_done"), sem("h_relu"), sem("h_ready"), sem("fr_done")
        fs_ready, fs2_ready, vk_done, sum_ready, x3_ready, xg_ready = (sem("fs_ready"), sem("fs2_ready"), sem("vk_done"),
                                                                       sem("sum_ready"), sem("x3_ready"), sem("xg_ready"))
        block = ctx.enter_context(nc.Block())

        def static(b, value):
            return isinstance(b, int) and b == value

        def round_xn2(b):
            return 2 if static(b, 0) else 4 * b - 1 if static(b, B - 1) else 4 * b

        def round_gate(b):
            return 4 * b if static(b, B - 1) else 4 * b - 2 if static(b, B) else 4 * b + 1

        def round_xn(b):
            return b if isinstance(b, int) and b < 2 else 4 * b - 5

        def has_next(b, n):
            return not (isinstance(b, int) and b + n >= B)

        def over_periods(engine, body):
            body(0)
            with engine.Fori(1, B - 2) as b:
                body(b)
            body(B - 2)
            body(B - 1)

        loads = (("ln1_w", ln1_w), ("ln1_b", ln1_b), ("ln2_w", ln2_w), ("ln2_b", ln2_b), ("decay", time_decay),
                 ("first", time_first), ("mk", mix_k), ("mv", mix_v), ("mr", mix_r), ("fmk", f_mix_k), ("fmr", f_mix_r))
        V_IN = 16 * len(loads)
        W_IN = 16 * (7 + KC)

        @block.sync
        def _(sp):
            def load_x(b):
                sp.dma_start(sequence_tiles(x, b), token_rows(x_from, b)).then_inc(x_in[min(b, 2)], 16)

            load_x(0)
            load_x(1)
            for dst, src in ((wk_s, w_key), (wv_s, w_value), (wr_s, w_recept), (wo_s, w_output), (wf_s, f_w_recept),
                             (fk_s, f_w_key), (fv_s, f_w_value)):
                sp.dma_start(dst[:], src.rearrange("(k p) n -> p k n", p=P)).then_inc(w_in, 16)
            for i in range(KC):
                sp.dma_start(gate_s[:, i, :], gate_w[:, i * P:(i + 1) * P].rearrange("e p -> p e"),
                             allow_slow_non_contiguous=True).then_inc(w_in, 16)
            for b in range(2, B):
                load_x(b)

            def store(b):
                sp.wait_ge(x3_ready, b + 1)
                sp.dma_start(token_rows(x_to, b), sequence_tiles(x, b)).then_inc(x_stored, 16)
                sp.wait_ge(xg_ready, b + 1)
                sp.dma_start(token_rows(normed_dram, b), xg[:]).then_inc(xg_stored, 16)

            over_periods(sp, store)
            sp.wait_ge(x_stored, 16 * B)
            sp.wait_ge(xg_stored, 16 * B)

        @block.scalar
        def _(act):
            for name, src in loads:
                flat = src if len(src.shape) == 1 else src.rearrange("a b c -> (a b c)")
                act.dma_start(vec[name][:], flat.rearrange("(k p) -> p k", p=P),
                              allow_slow_non_contiguous=True).then_inc(v_in, 16)
            act.wait_ge(v_in, V_IN)
            nc.scalar.activation(vec["decay"][:], vec["decay"][:], ACT.Exp).then_inc(prep, 1)

            def evacuate_norm(dst, w, bias, r):
                act.wait_ge(t_filled, r + 1)
                for i in range(KC):
                    last = nc.scalar.activation(dst[:, i, 1:N + 1], tbk[i][:], ACT.Identity, bias=vec[bias][:, i:i + 1],
                                                scale=vec[w][:, i:i + 1])
                last.then_inc(t_emptied, 1)

            def evacuate_xn(b):
                wait_count(act, mix_ready, 3 * b)
                evacuate_norm(xnT, "ln1_w", "ln1_b", round_xn(b))

            def evacuate(b, n, dst, src):
                act.wait_ge(kvr_done, 6 * b + n + 1)
                f, scale = (ACT.Tanh, 0.5) if dst is sg else (ACT.Copy, 1.0)
                nc.scalar.activation(dst[:, n % 2, :], xb_[src][:], f, scale=scale).then_inc(kvr_evac, 1)

            def evacuate_kv(b):
                wait_count(act, g_ready, b)
                for n, (dst, src) in enumerate(((k, 4), (k, 5), (v, 2), (v, 3))):
                    evacuate(b, n, dst, src)

            def evacuate_r(b):
                evacuate(b, 4, sg, 0)
                evacuate(b, 5, sg, 1)

            def exponential(b, step):
                if step == 0:
                    act.wait_ge(d2_ready, b + 1)
                    nc.scalar.activation(d2[:], d2[:], ACT.Exp).then_inc(expd, 1)
                elif step == 1:
                    act.wait_ge(s_ready, 2 * b + 1)
                    nc.scalar.activation(d1[:], d1[:], ACT.Exp).then_inc(expd, 1)
                elif step == 2:
                    act.wait_ge(s_ready, 2 * b + 2)
                    nc.scalar.activation(e2[:], e1[:], ACT.Relu, scale=-1.0).then_inc(expd, 1)
                elif step == 3:
                    act.wait_ge(expd, 6 * b + 3)
                    nc.scalar.activation(e1[:], e1[:], ACT.Relu).then_inc(expd, 1)
                elif step == 4:
                    nc.scalar.activation(e2[:], e2[:], ACT.Exp, scale=-1.0).then_inc(expd, 1)
                else:
                    act.wait_ge(expd, 6 * b + 4)
                    nc.scalar.activation(e1[:], e1[:], ACT.Exp, scale=-1.0).then_inc(expd, 1)

            def hidden(b):
                wait_count(act, vk_done, 2 * b)
                if has_next(b, 1):
                    exponential(b + 1, 0)
                    exponential(b + 1, 1)
                for m in range(FCH):
                    act.wait_ge(fk_done, FCH * b + m + 1)
                    nc.scalar.activation(hT[:, m, :], xb_[m % 4][:], ACT.Relu).then_inc(h_relu, 1)
                    act.wait_ge(h_relu, FCH * b + m + 1)
                    nc.scalar.activation(hT[:, m, :], hT[:, m, :], ACT.Square).then_inc(h_ready, 1)
                    if has_next(b, 1) and m < 4:
                        exponential(b + 1, m + 2)
                wait_count(act, x3_ready, b)
                for h in range(2):
                    act.wait_ge(fr_done, 2 * b + h + 1)
                    nc.scalar.activation(fs[:, h, :], xb_[4 + h][:], ACT.Tanh, scale=0.5).then_inc(fs_ready, 1)

            def gate_part(b):
                r = round_gate(b)
                act.wait_ge(t_filled, r + 1)
                for i in range(KC):
                    last = nc.scalar.activation(xgT[:, i, :], tbk[i][:], ACT.Copy)
                last.then_inc(t_emptied, 1)
                act.wait_ge(t_filled, r + 2)
                nc.scalar.activation(sequence_tiles(logits, b - 1),
                                     tbk[0][:, 0:TB * EX].rearrange("p (t e) -> p t e", e=EX),
                                     ACT.Copy).then_inc(t_emptied, 1)

            def carry(b):
                wait_count(act, xb_added, b)
                wait_count(act, xn2_ready, b)
                act.wait_ge(xn_ready, b + 1)
                act.sem_inc(passed_act, 1)
                for j in range(TB):
                    stat = tile_of(mv_all, b, j)
                    last = nc.scalar.activation(xb[:, j, :], tile_of(x, b, j), ACT.Identity, bias=stat[:, 0:1], scale=stat[:, 1:2])
                last.then_inc(a_ready, 1)

            evacuate_xn(0)
            evacuate_kv(0)
            evacuate_r(0)
            evacuate_xn(1)
            for step in range(6):
                exponential(0, step)
            carry(0)

            def period(b):
                if has_next(b, 1):
                    evacuate_kv(b + 1)
                wait_count(act, mix2_ready, 2 * b)
                evacuate_norm(xn2T, "ln2_w", "ln2_b", round_xn2(b))
                if has_next(b, 1):
                    evacuate_r(b + 1)
                if not static(b, 0):
                    gate_part(b)
                hidden(b)
                if has_next(b, 1):
                    carry(b + 1)
                if has_next(b, 2):
                    evacuate_xn(b + 2)

            over_periods(act, period)
            gate_part(B)

        @block.gpsimd
        def _(pool):
            def rstd(mvt, ready, done, count, value):
                wait_apart(pool, ready, count, passed_pool)
                nc.gpsimd.tensor_scalar(mvt[:, :, 1], mvt[:, :, 1], EPS, None, ALU.add).then_inc(own_pool, 1)
                pool.wait_ge(own_pool, value)
                nc.gpsimd.tensor_tensor(mvt[:, :, 1], mvt[:, :, 1], neg_half[:, 0:TB], ALU.pow).then_inc(done, 1)

            def norm_begun(b, value):
                rstd(mv, var_ready, rstd_ready, b + 1, value)

            def norm_begun1(b, value):
                rstd(mv1, var1_ready, rstd1_ready, b + 1, value)

            def gate_scaled(b):
                wait_count(pool, g_ready, b)
                wait_apart(pool, kvr_evac, 6 * b + 6, passed_pool)
                nc.gpsimd.tensor_scalar(sg[:], sg[:], 0.5, 0.5, ALU.mult, ALU.add).then_inc(sg_ready, 1)

            def entering_exponent(b):
                wait_apart(pool, eps_ready, b + 1, passed_pool)
                nc.gpsimd.tensor_tensor(d2[:], k[:], eps[:, :, 1:N + 1], ALU.subtract).then_inc(d2_ready, 1)

            def decayed_value(b):
                pool.wait_ge(expd, 6 * b + 1)
                nc.gpsimd.tensor_tensor(dv[:], d2[:], v[:], ALU.mult).then_inc(dv_ready, 1)

            def entering_value(b):
                pool.wait_ge(expd, 6 * b + 5)
                nc.gpsimd.tensor_tensor(ev[:], e2[:], v[:], ALU.mult).then_inc(ev_ready, 1)

            def numerator(b):
                wait_apart(pool, num_scaled, b + 1, passed_pool)
                wait_apart(pool, ev_ready, b + 1, passed_pool)
                nc.gpsimd.tensor_tensor(dv[:], dv[:], ev[:], ALU.add).then_inc(num_summed, 1)
                wait_apart(pool, num_summed, b + 1, passed_pool)
                nc.gpsimd.tensor_tensor(dv[:], dv[:], sg[:], ALU.mult).then_inc(num_ready, 1)

            def add_mixed(b):
                wait_apart(pool, xb_ready, 2 * b + 2, passed_pool)
                xt = sequence_tiles(x, b)
                nc.gpsimd.tensor_tensor(xt, xt, xb[:], ALU.add).then_inc(xb_added, 1)

            norm_begun(0, 1)
            norm_begun1(0, 2)
            norm_begun(1, 3)
            norm_begun1(1, 4)
            gate_scaled(0)
            entering_exponent(0)
            decayed_value(0)
            entering_value(0)
            numerator(0)

            def period(b):
                done = 4 if static(b, 0) else 4 * b + 3
                if static(b, B - 1):
                    done = 4 * (B - 2) + 3 + 2
                rstd(mv2, var2_ready, rstd2_ready, b + 1, done + 1)
                if not static(b, 0):
                    rstd(mvg, varg_ready, rstdg_ready, b, done + 2)
                    done = done + 1
                if has_next(b, 1):
                    gate_scaled(b + 1)
                    entering_exponent(b + 1)
                add_mixed(b)
                if has_next(b, 2):
                    norm_begun(b + 2, done + 2)
                if has_next(b, 1):
                    decayed_value(b + 1)
                if has_next(b, 2):
                    norm_begun1(b + 2, done + 3)
                if has_next(b, 1):
                    entering_value(b + 1)
                    numerator(b + 1)
                wait_apart(pool, fs_ready, 2 * b + 2, passed_pool)
                nc.gpsimd.tensor_scalar(fs[:], fs[:], 0.5, 0.5, ALU.mult, ALU.add).then_inc(fs2_ready, 1)
                wait_count(pool, xb_added, b + 1)
                wait_apart(pool, sum_ready, b + 1, passed_pool)
                xt = sequence_tiles(x, b)
                nc.gpsimd.tensor_tensor(xt, xt, fs[:].rearrange("p h (t c) -> p (h t) c", c=C), ALU.add).then_inc(x3_ready, 1)

            over_periods(pool, period)
            rstd(mvg, varg_ready, rstdg_ready, B, 4 * (B - 2) + 3 + 4 + 1)

        @block.vector
        def _(dve):
            f, m_, e_, r_, w_, g_ = (OwnSteps(dve, sm, n) for sm, n in ((own_f, 3), (own_m, 1), (eps_ready, 1), (own_r, 3),
                                                                        (own_w, 1), (own_g, 1)))
            m2 = OwnSteps(dve, sem("own_m2"), 1)

            def statistics(src, bnt, mvt, own, done):
                for j in range(TB):
                    last = nc.vector.bn_stats(bnt[:, j, :], src(j))
                own.link(last, passed_dve)
                for j in range(TB):
                    last = nc.vector.bn_aggr(mvt[:, j, :], bnt[:, j, :])
                last.then_inc(done, 1)

            def normalise(dst, src, mvt):
                for j in range(TB):
                    last = nc.vector.tensor_scalar(dst[:, j, :], src(j), mvt(j)[:, 0:1], mvt(j)[:, 1:2],
                                                   ALU.subtract, ALU.mult)
                return last

            def begin(b):
                f.round(b)
                statistics(lambda j: tile_of(x, b, j), bn, mv, f, var_ready)

            def begin_a(b):
                dve.wait_ge(rstd_ready, b + 1)
                nc.vector.tensor_copy(sequence_tiles(mv_all, b)[:, :, 1], mv[:, :, 1])
                nc.vector.scalar_tensor_tensor(out=sequence_tiles(mv_all, b)[:, :, 0], in0=mv[:, :, 0], scalar=-1.0,
                                               in1=mv[:, :, 1], op0=ALU.mult, op1=ALU.mult)
                f.link(normalise(a, lambda j: tile_of(x, b, j), lambda j: mv[:, j, :]))
                statistics(lambda j: a[:, j, :], bn1, mv1, f, var1_ready)

            def begin_xn(b):
                dve.wait_ge(rstd1_ready, b + 1)
                normalise(xn, lambda j: a[:, j, :], lambda j: mv1[:, j, :]).then_inc(xn_ready, 1)

            def mixes(own, src, outs, b, done):
                own.round(b)
                own.link(nc.vector.tensor_tensor(dT[:], src[:, :, 1:N + 1], src[:, :, 0:N], ALU.subtract))
                for dst, m in outs:
                    for i in range(KC):
                        last = nc.vector.scalar_tensor_tensor(out=dst[:, i, :], in0=dT[:, i, :], scalar=vec[m][:, i:i + 1],
                                                              in1=src[:, i, 0:N], op0=ALU.mult, op1=ALU.add)
                    last.then_inc(done, 1)

            def mix_time(b):
                dve.wait_ge(t_emptied, round_xn(b) + 1)
                wait_count(dve, kvr_done, 6 * b)
                mixes(m_, xnT, ((xk, "mk"), (xv, "mv"), (xr, "mr")), b, mix_ready)

            def exponent_scan(b):
                dve.wait_ge(kvr_evac, 6 * b + 2)
                e_.round(b)
                for i in range(KC):
                    last = nc.vector.tensor_tensor_scan(eps[:, i, 1:N + 1], vec["ndecay"][:, i:i + 1].to_broadcast([P, N]),
                                                        k[:, i, :], EPS_INIT, ALU.add, ALU.max)
                e_.link(last)

            def exponents(b):
                for i in range(KC):
                    last = nc.vector.scalar_tensor_tensor(out=d1[:, i, :], in0=eps[:, i, 0:N], scalar=vec["decay"][:, i:i + 1],
                                                          in1=eps[:, i, 1:N + 1], op0=ALU.subtract, op1=ALU.subtract)
                last.then_inc(s_ready, 1)
                for i in range(KC):
                    last = nc.vector.scalar_tensor_tensor(out=e1[:, i, :], in0=k[:, i, :], scalar=vec["first"][:, i:i + 1],
                                                          in1=eps[:, i, 0:N], op0=ALU.add, op1=ALU.subtract)
                last.then_inc(s_ready, 1)

            def recurrence(b):
                r_.round(b)
                dve.wait_ge(expd, 6 * b + 2)
                for i in range(KC):
                    nc.vector.tensor_tensor_scan(be[:, i, 1:N + 1], d1[:, i, :], d2[:, i, :], 0.0, ALU.mult, ALU.add)
                dve.wait_ge(dv_ready, b + 1)
                for i in range(KC):
                    last = nc.vector.tensor_tensor_scan(al[:, i, 1:N + 1], d1[:, i, :], dv[:, i, :], 0.0, ALU.mult, ALU.add)
                r_.link(last)

            def output(b):
                dve.wait_ge(expd, 6 * b + 6)
                nc.vector.tensor_tensor(d1[:], e1[:], be[:, :, 0:N], ALU.mult)
                nc.vector.tensor_tensor(dv[:], e1[:], al[:, :, 0:N], ALU.mult).then_inc(num_scaled, 1)
                dve.wait_ge(num_scaled, b + 1)
                r_.link(nc.vector.tensor_tensor(d1[:], d1[:], e2[:], ALU.add))

            def output_quotient(b):
                r_.link(nc.vector.reciprocal(d1[:], d1[:]))
                dve.wait_ge(num_ready, b + 1)
                nc.vector.tensor_tensor(gT[:], dv[:], d1[:], ALU.mult).then_inc(g_ready, 1)

            def time_output(b):
                w_.round(b)
                dve.wait_ge(a_ready, b + 1)
                for h in range(2):
                    dve.wait_ge(wo_done, 2 * b + h + 1)
                    t = xb[:, 2 * h:2 * h + 2, :].rearrange("p t c -> p (t c)")
                    nc.vector.tensor_tensor(t, t, xb_[h][:], ALU.add).then_inc(xb_ready, 1)
                dve.wait_ge(xb_ready, 2 * b + 2)
                statistics(lambda j: xb[:, j, :], bn2, mv2, w_, var2_ready)

            def norm2(b):
                dve.wait_ge(rstd2_ready, b + 1)
                normalise(xn2, lambda j: xb[:, j, :], lambda j: mv2[:, j, :]).then_inc(xn2_ready, 1)

            def mix_channel(b):
                dve.wait_ge(t_emptied, round_xn2(b) + 1)
                mixes(m2, xn2T, ((xfk, "fmk"), (xfr, "fmr")), b, mix2_ready)

            def route_statistics(b):
                g_.round(b)
                dve.wait_ge(x3_ready, b + 1)
                statistics(lambda j: tile_of(x, b, j), bng, mvg, g_, varg_ready)

            def route_norm(b):
                dve.wait_ge(rstdg_ready, b + 1)
                wait_count(dve, xg_stored, 16 * b)
                normalise(xg, lambda j: tile_of(x, b, j), lambda j: mvg[:, j, :]).then_inc(xg_ready, 1)

            def finish(b, h):
                dve.wait_ge(vk_done, 2 * b + h + 1)
                return nc.vector.tensor_tensor(fs[:, h, :], fs[:, h, :], xb_[2 + h][:], ALU.mult)

            nc.vector.memset(xnT[:, :, 0:1], 0.0)
            nc.vector.memset(xn2T[:, :, 0:1], 0.0)
            nc.vector.memset(eps[:, :, 0:1], EPS_INIT)
            nc.vector.memset(al[:, :, 0:1], 0.0)
            nc.vector.memset(be[:, :, 0:1], 0.0)
            dve.wait_ge(x_in[0], 16)
            begin(0)
            begin_a(0)
            begin_xn(0)
            dve.wait_ge(v_in, V_IN)
            dve.wait_ge(prep, 1)
            nc.vector.tensor_scalar(vec["ndecay"][:], vec["decay"][:], -1.0, None, ALU.mult).then_inc(prep, 1)
            dve.wait_ge(prep, 2)
            mix_time(0)
            dve.wait_ge(x_in[1], 16)
            begin(1)
            begin_a(1)
            begin_xn(1)
            exponent_scan(0)
            exponents(0)
            recurrence(0)
            output(0)
            output_quotient(0)
            mix_time(1)
            dve.wait_ge(x_in[2], 16 * (B - 2))

            def period(b):
                time_output(b)
                if not static(b, 0):
                    route_statistics(b - 1)
                norm2(b)
                if not static(b, 0):
                    route_norm(b - 1)
                if has_next(b, 1):
                    exponent_scan(b + 1)
                mix_channel(b)
                if has_next(b, 1):
                    exponents(b + 1)
                if has_next(b, 2):
                    begin(b + 2)
                if has_next(b, 1):
                    recurrence(b + 1)
                if has_next(b, 2):
                    begin_a(b + 2)
                if has_next(b, 1):
                    output(b + 1)
                if has_next(b, 2):
                    begin_xn(b + 2)
                if has_next(b, 1):
                    output_quotient(b + 1)
                dve.wait_ge(fs2_ready, b + 1)
                finish(b, 0)
                if has_next(b, 2):
                    mix_time(b + 2)
                finish(b, 1).then_inc(sum_ready, 1)

            over_periods(dve, period)
            route_statistics(B - 1)
            route_norm(B - 1)

        @block.tensor
        def _(pe):
            def transposes(src, r):
                wait_count(pe, t_emptied, r)
                for i in range(KC):
                    for j in range(TB):
                        last = nc.tensor.transpose(tbk[i][:, j * P:(j + 1) * P], src[:, j, i * P:(i + 1) * P], ident[:])
                last.then_inc(t_filled, 1)

            def token_product(out, src, w, chunks):
                for j in range(2):
                    for i in range(chunks):
                        last = nc.tensor.matmul(out[:, j * C:(j + 1) * C], src(i, j), w[:, i, :],
                                                start=(i == 0), stop=(i == chunks - 1))
                return last

            def cut(src, h):
                return lambda i, j: src[:, i, (2 * h + j) * P:(2 * h + j + 1) * P]

            def project(b, n, w, src, banks):
                pe.wait_ge(mix_ready, 3 * b + n + 1)
                for c in range(KC):
                    for i in range(KC):
                        last = nc.tensor.matmul(xb_[banks[c]][:], w[:, i, c * P:(c + 1) * P], src[:, i, :],
                                                start=(i == 0), stop=(i == KC - 1))
                    last.then_inc(kvr_done, 1)

            def project_kv(b):
                if not static(b, 0):
                    wait_count(pe, fs_ready, 2 * b - 2)
                project(b, 0, wk_s, xk, (4, 5))
                if not static(b, 0):
                    wait_count(pe, sum_ready, b - 1)
                project(b, 1, wv_s, xv, (2, 3))

            def project_r(b):
                if not static(b, 0):
                    pe.wait_ge(xb_ready, 2 * b)
                project(b, 2, wr_s, xr, (0, 1))

            def gate_part(b):
                r = round_gate(b)
                pe.wait_ge(xg_ready, b)
                transposes(xg, r)
                pe.wait_ge(t_emptied, r + 1)
                for j in range(TB):
                    for i in range(KC):
                        last = nc.tensor.matmul(tbk[0][:, j * EX:(j + 1) * EX], xgT[:, i, j * P:(j + 1) * P], gate_s[:, i, :],
                                                start=(i == 0), stop=(i == KC - 1))
                last.then_inc(t_filled, 1)

            pe.wait_ge(w_in, W_IN)
            pe.wait_ge(xn_ready, 1)
            transposes(xn, 0)
            project_kv(0)
            project_r(0)
            pe.wait_ge(xn_ready, 2)
            transposes(xn, 1)

            def period(b):
                pe.wait_ge(g_ready, b + 1)
                wait_count(pe, h_relu, FCH * b)
                if static(b, 0):
                    pe.wait_ge(kvr_evac, 6)
                for h in range(2):
                    token_product(xb_[h], cut(gT, h), wo_s, KC).then_inc(wo_done, 1)
                if has_next(b, 1):
                    project_kv(b + 1)
                pe.wait_ge(xn2_ready, b + 1)
                transposes(xn2, round_xn2(b))
                if has_next(b, 1):
                    project_r(b + 1)
                if not static(b, 0):
                    gate_part(b)
                pe.wait_ge(mix2_ready, 2 * b + 1)
                if has_next(b, 1):
                    pe.wait_ge(kvr_evac, 6 * b + 12)
                else:
                    pe.wait_ge(xb_ready, 2 * b + 2)
                    pe.wait_ge(sum_ready, b)
                for m in range(FCH):
                    if m >= 4:
                        pe.wait_ge(h_relu, FCH * b + m - 3)
                    for i in range(KC):
                        last = nc.tensor.matmul(xb_[m % 4][:], fk_s[:, i, m * P:(m + 1) * P], xfk[:, i, :],
                                                start=(i == 0), stop=(i == KC - 1))
                    last.then_inc(fk_done, 1)
                pe.wait_ge(mix2_ready, 2 * b + 2)
                wait_count(pe, fs_ready, 2 * b)
                for h in range(2):
                    token_product(xb_[4 + h], cut(xfr, h), wf_s, KC).then_inc(fr_done, 1)
                pe.wait_ge(h_ready, FCH * b + FCH)
                token_product(xb_[2], cut(hT, 0), fv_s, FCH).then_inc(vk_done, 1)
                if has_next(b, 2):
                    pe.wait_ge(xn_ready, b + 3)
                    transposes(xn, round_xn(b + 2))
                token_product(xb_[3], cut(hT, 1), fv_s, FCH).then_inc(vk_done, 1)

            over_periods(pe, period)
            gate_part(B)


def build(nc, x_in, qk_w, qk_b, lepe_w, lepe_b, ln1_w, ln1_b, ln2_w, ln2_b, time_decay, time_first, mix_k, mix_v, mix_r,
          w_key, w_value, w_recept, w_output, f_mix_k, f_mix_r, f_w_key, f_w_recept, f_w_value, gate_w, w1, w2, w3,
          cos_t, sin_t, out):
    x_mid = nc.dram_tensor("x_rows", (ROWS, C), F32, kind="Internal").ap()
    normed = nc.dram_tensor("normed_rows", (ROWS, C), F32, kind="Internal").ap()
    with ExitStack() as ctx:
        def sb(name, shape, dt=F32):
            return ctx.enter_context(nc.sbuf_tensor(name, shape, dt))

        logits = sb("logits", [P, T, EX])
        ident = sb("ident", [P, P])
        head_mask = sb("head_mask", [P, HEADS])
        block_mask = sb("block_mask", [P, P])
        neg_half = sb("neg_half", [P, TB])
        bank = [ctx.enter_context(nc.psum_tensor(f"bank{i}", [P, N], F32)) for i in range(8)]

        stage_constants(nc, ident, head_mask, block_mask, neg_half, (x_mid, normed, out))
        phase_attention(nc, x_in, qk_w, qk_b, lepe_w, lepe_b, gate_w, cos_t, sin_t, normed, x_mid, logits, ident,
                        head_mask, block_mask, neg_half, bank)
        phase_experts(nc, "first_", normed, x_mid, w1, w2, w3, logits, ident, bank)
        phase_mix(nc, ln1_w, ln1_b, ln2_w, ln2_b, time_decay, time_first, mix_k, mix_v, mix_r, w_key, w_value, w_recept,
                  w_output, f_mix_k, f_mix_r, f_w_key, f_w_recept, f_w_value, gate_w, x_mid, normed, out, logits, ident,
                  neg_half, bank)
        phase_experts(nc, "second_", normed, out, w1, w2, w3, logits, ident, bank)


_INS = ["L0_attn_a_x", "L0_attn_a_qk_w", "L0_attn_a_qk_b", "L0_attn_a_lepe_w", "L0_attn_a_lepe_b",
        "L0_attn_b_ln1_w", "L0_attn_b_ln1_b", "L0_attn_b_ln2_w", "L0_attn_b_ln2_b", "L0_attn_b_time_decay",
        "L0_attn_b_time_first", "L0_attn_b_time_mix_k", "L0_attn_b_time_mix_v", "L0_attn_b_time_mix_r",
        "L0_attn_b_w_key", "L0_attn_b_w_value", "L0_attn_b_w_recept", "L0_attn_b_w_output", "L0_attn_b_f_time_mix_k",
        "L0_attn_b_f_time_mix_r", "L0_attn_b_f_w_key", "L0_attn_b_f_w_recept", "L0_attn_b_f_w_value",
        "L0_ffn_gate_w", "L0_ffn_w1", "L0_ffn_w2", "L0_ffn_w3"]


def kernel(**inputs):
    import numpy as _np
    import concourse.bacc as _bacc
    from concourse import mybir as _mybir
    from concourse.bass_utils import run_bass_kernel_spmd as _run

    nc = _bacc.Bacc("TRN2", target_bir_lowering=False, num_devices=1)
    f = _np.float32
    theta = (f(1.0) / f(10000.0) ** (_np.arange(C // 2, dtype=f) / f(C // 2))).astype(f)
    angles = (theta[:, None] * _np.arange(N, dtype=f)[None, :]).astype(f)
    arrays, args = {}, []
    for name, a in [(n, inputs[n]) for n in _INS] + [("rope_cos", _np.cos(angles)), ("rope_sin", _np.sin(angles))]:
        a = _np.ascontiguousarray(a)
        arrays[f"in_{name}"] = a
        args.append(nc.dram_tensor(f"in_{name}", a.shape, _mybir.dt.from_np(a.dtype), kind="ExternalInput").ap())
    args.append(nc.dram_tensor("out_x", (ROWS, C), F32, kind="ExternalOutput").ap())
    build(nc, *args)
    r = _run(nc, [arrays], core_ids=[0])
    return r.results[0]["out_x"][:B * N].reshape(B, N, C)
```

```python
import concourse.bass as bass
from concourse import mybir
from contextlib import ExitStack

F32 = mybir.dt.float32
F32R = mybir.dt.float32r
I32 = mybir.dt.int32
U32 = mybir.dt.uint32
ALU = mybir.AluOpType
ACT = mybir.ActivationFunctionType
AXX = mybir.AxisListType.X

P = 128
B, N, C = 8, 512, 256
TB = N // P
T = B * TB
KC = C // P
HEADS, HD = 8, C // 8
LT = 3
EX, H = 8, 512
HC = H // P
TOPK = 2
NBLK = TOPK * B * N // P + EX - 1
ROWS = T * P + P
F = 4 * C
FCH = F // P
EPS = 1e-5
EPS_INIT = -1e30


def over_batches(engine, body):
    body(0, 0)
    with engine.Fori(1, B - 2, 2) as b:
        body(b, 1)
        body(b + 1, 0)
    body(B - 1, 1)


def is_first(b):
    return isinstance(b, int) and b == 0


def is_last(b):
    return isinstance(b, int) and b == B - 1


def wait_count(engine, sem, value):
    if isinstance(value, int) and value <= 0:
        return
    engine.wait_ge(sem, value)


def wait_apart(engine, sem, value, passed):
    wait_count(engine, sem, value)
    engine.sem_inc(passed, 1)


class OwnSteps:

    def __init__(self, engine, sem, per_round):
        self.engine, self.sem, self.per_round = engine, sem, per_round
        self.base, self.k = 0, 0

    def round(self, r):
        assert self.k in (0, self.per_round), (self.k, self.per_round)
        self.base, self.k = r * self.per_round, 0

    def link(self, ins, passed=None):
        self.k += 1
        ins.then_inc(self.sem, 1)
        self.engine.wait_ge(self.sem, self.base + self.k)
        if passed is not None:
            self.engine.sem_inc(passed, 1)

    def pad(self):
        while self.k < self.per_round:
            self.k += 1
            self.engine.sem_inc(self.sem, 1)


def sequence_tiles(x, b):
    return x[:, bass.ds(b * TB, TB)] if not isinstance(b, int) else x[:, b * TB:(b + 1) * TB]


def tile_of(x, b, j):
    if isinstance(b, int):
        return x[:, b * TB + j, :]
    return x[:, bass.ds(b * TB + j, 1), :].rearrange("p a c -> p (a c)")


def split_product(nc, out, hi, lo, other_hi, other_lo, start, stop):
    nc.tensor.matmul(out, hi, other_hi, start=start, stop=False)
    nc.tensor.matmul(out, hi, other_lo, start=False, stop=False)
    return nc.tensor.matmul(out, lo, other_hi, start=False, stop=stop)


def token_rows(table, b):
    first = b * TB * P
    rows = table[first:first + TB * P, :] if isinstance(b, int) else table[bass.ds(first, TB * P), :]
    return rows.rearrange("(t p) c -> p t c", p=P)


def stage_constants(nc, ident, head_mask, block_mask, neg_half, tables, vectors, gate, vectors_s, gate_s):
    with ExitStack() as ctx:
        made = ctx.enter_context(nc.semaphore("const_made"))
        zeros = ctx.enter_context(nc.sbuf_tensor("zeros", [P, C], F32))
        cleared = ctx.enter_context(nc.semaphore("const_cleared"))
        written = ctx.enter_context(nc.semaphore("const_written"))
        loaded = ctx.enter_context(nc.semaphore("const_loaded"))
        block = ctx.enter_context(nc.Block())

        @block.gpsimd
        def _(pool):
            nc.gpsimd.memset(neg_half[:], -0.5).then_inc(made, 1)
            nc.gpsimd.memset(ident[:], 0.0).then_inc(made, 1)
            nc.gpsimd.memset(head_mask[:], 1.0 / N).then_inc(made, 1)
            nc.gpsimd.memset(block_mask[:], 1.0 / float(N) ** 0.5).then_inc(made, 1)
            pool.wait_ge(made, 4)
            nc.gpsimd.affine_select(out=ident[:], in_=ident[:], compare_op=ALU.not_equal, fill=1.0, base=0,
                                    pattern=[[-1, P]], channel_multiplier=1).then_inc(made, 1)
            pair = HD // 2
            nc.gpsimd.affine_select(out=head_mask[:], in_=head_mask[:], compare_op=ALU.is_ge, fill=0.0, base=0,
                                    pattern=[[-pair, HEADS]], channel_multiplier=1).then_inc(made, 1)
            bm = block_mask[:].rearrange("p (g e) -> p g e", e=HD)
            nc.gpsimd.affine_select(out=bm, in_=bm, compare_op=ALU.is_ge, fill=0.0, base=0,
                                    pattern=[[-HD, P // HD], [0, HD]], channel_multiplier=1).then_inc(made, 1)
            pool.wait_ge(made, 7)
            nc.gpsimd.affine_select(out=head_mask[:], in_=head_mask[:], compare_op=ALU.is_ge, fill=0.0,
                                    base=pair - 1, pattern=[[pair, HEADS]], channel_multiplier=-1).then_inc(made, 1)
            nc.gpsimd.affine_select(out=bm, in_=bm, compare_op=ALU.is_ge, fill=0.0, base=HD - 1,
                                    pattern=[[HD, P // HD], [0, HD]], channel_multiplier=-1).then_inc(made, 1)
            pool.wait_ge(made, 9)

        @block.vector
        def _(dve):
            nc.vector.memset(zeros[:], 0.0).then_inc(cleared, 1)

        @block.sync
        def _(sp):
            sp.dma_start(vectors_s[:], vectors).then_inc(loaded, 16)
            sp.dma_start(gate_s[:], gate).then_inc(loaded, 16)
            sp.wait_ge(cleared, 1)
            for table in tables:
                sp.dma_start(table[T * P:ROWS, :], zeros[:]).then_inc(written, 16)
            sp.wait_ge(written, 16 * len(tables))
            sp.wait_ge(loaded, 32)


def phase_attention(nc, x_dram, qk_w, qk_b, lepe_w, lepe_b, gate_s, cos_t, sin_t,
                    normed_dram, x_dram_out, logits, ident, head_mask, block_mask, neg_half, bank, passed):
    tb0, tb1, q0, q1, q2, q3, l0, l1 = bank
    q, tbk, lb = [q0, q1, q2, q3], [tb0, tb1], [l0, l1]
    ORDER = (2, 3, 0, 1)
    proj = {2: q0, 3: q1, 0: q2, 1: q3}
    sems = []
    with ExitStack() as ctx:
        def sb(name, shape, dt=F32):
            return ctx.enter_context(nc.sbuf_tensor(name, shape, dt))

        def sem(name):
            sems.append(nc.alloc_semaphore(name))
            return sems[-1]

        x = sb("a_x", [P, T, C])
        qk_raw = sb("a_qk_raw", [P, KC, 2 * C])
        edge = sb("a_edge", [P, KC, 1])
        qk_hi, qk_lo = (sb(f"a_qk_{part}", [P, KC, 4, P], F32R) for part in ("hi", "lo"))
        qk_bias = sb("a_qk_bias", [P, 4])
        lepe_raw = sb("a_lepe_raw", [P, LT, KC, C])
        lepe_hi, lepe_lo = (sb(f"a_lepe_{part}", [P, LT, KC, C], F32R) for part in ("hi", "lo"))
        lepe_bias = sb("a_lepe_bias", [P, 1, C])
        cos_s = sb("a_cos", [P, 1, N])
        sin_s = sb("a_sin", [P, N])
        nsin_s = sb("a_nsin", [P, N])
        bn = sb("a_bn", [P, TB, 6])
        mv = sb("a_mv", [P, TB, 2])
        bn2 = sb("a_bn2", [P, TB, 6])
        mv2 = sb("a_mv2", [P, TB, 2])
        xn = [sb(f"a_xn{i}", [P, TB, C]) for i in range(2)]
        xnT_hi, xnT_lo = ([sb(f"a_xnT_{part}{i}", [P, KC, N + 2], F32R) for i in range(2)] for part in ("hi", "lo"))
        ex = sb("a_ex", [P, 4, N])
        re = sb("a_re", [P, 4, N])
        el = sb("a_el", [P, 4, N])
        ksum = sb("a_ksum", [P, 2])
        kz = sb("a_kz", [P, 2, HEADS])
        kA = sb("a_kA", [P, 2, N])
        kB = sb("a_kB", [P, 2, N])
        kr = sb("a_kr", [P, 2, N])
        qA = sb("a_qA", [P, 2, N])
        qB = sb("a_qB", [P, 2, N])
        qr = sb("a_qr", [P, 2, N])
        krt = sb("a_krt", [P, KC, TB, P])
        kvb = sb("a_kvb", [P, KC, P])
        zr = sb("a_zr", [P, TB * HEADS])
        u = sb("a_u", [P, 2, N])
        v = sb("a_v", [P, 2, 2, C])
        xg = sb("a_xg", [P, TB, C])
        xgT = sb("a_xgT", [P, KC, N])

        x1_in, wl_in = sem("a_x1_in"), sem("a_wl_in")
        xnT_hi_ready, lepe_hi_ready, lepe_ready = sem("a_xnT_hi_ready"), sem("a_lepe_hi_ready"), sem("a_lepe_ready")
        x0_in, x_in, w_in, tab_in = sem("a_x0_in"), sem("a_x_in"), sem("a_w_in"), sem("a_tab_in")
        own_dve, own_pool = sem("a_own_dve"), sem("a_own_pool")
        var_ready, rstd_ready, xn_ready = sem("a_var_ready"), sem("a_rstd_ready"), sem("a_xn_ready")
        qk_done, qk_evac, q_ready, kr_ready, qr_ready = (sem("a_qk_done"), sem("a_qk_evac"), sem("a_q_ready"),
                                                         sem("a_kr_ready"), sem("a_qr_ready"))
        t_filled, t_emptied = sem("a_t_filled"), sem("a_t_emptied")
        lepe_done, kv_done, z_done, attn_done, kvb_ready = (sem("a_lepe_done"), sem("a_kv_done"), sem("a_z_done"),
                                                            sem("a_attn_done"), sem("a_kvb_ready"))
        v_ready, x1_ready = sem("a_v_ready"), sem("a_x1_ready")
        var2_ready, rstd2_ready, xg_ready = sem("a_var2_ready"), sem("a_rstd2_ready"), sem("a_xg_ready")
        w_ready = sem("a_w_ready")
        x_stored, xg_stored = sem("a_x_stored"), sem("a_xg_stored")
        block = ctx.enter_context(nc.Block())

        def round_gate(b):
            return 4 * b - 1 if not (isinstance(b, int) and b == B) else 4 * B - 2

        def round_next(b):
            return 4 * b + 2

        def round_k(b):
            return 4 * b + 1

        @block.sync
        def _(sp):
            xv = x_dram.rearrange("b (t p) c -> p (b t) c", p=P)
            sp.dma_start(x[:, 0:TB, :], xv[:, 0:TB, :]).then_inc(x0_in, 16)
            sp.dma_start(qk_raw[:], qk_w.rearrange("(k p) n -> p k n", p=P)).then_inc(w_in, 16)
            sp.dma_start(qk_bias[:].rearrange("p (h two) -> p h two", two=2),
                         qk_b.rearrange("(h i two) -> i h two", h=2, two=2)).then_inc(w_in, 16)
            sp.dma_start(x[:, TB:2 * TB, :], xv[:, TB:2 * TB, :]).then_inc(x1_in, 16)
            sp.dma_start(lepe_raw[:], lepe_w.rearrange("t (k p) n -> p t k n", p=P)).then_inc(wl_in, 16)
            sp.dma_start(x[:, 2 * TB:, :], xv[:, 2 * TB:, :]).then_inc(x_in, 16)

            def store(b, par):
                sp.wait_ge(x1_ready, 2 * b + 2)
                sp.dma_start(token_rows(x_dram_out, b), sequence_tiles(x, b)).then_inc(x_stored, 16)
                sp.wait_ge(xg_ready, b + 1)
                sp.dma_start(token_rows(normed_dram, b), xg[:]).then_inc(xg_stored, 16)

            over_batches(sp, store)
            sp.wait_ge(x_stored, 16 * B)
            sp.wait_ge(xg_stored, 16 * B)

        @block.scalar
        def _(act):
            act.dma_start(cos_s[:, 0, :], cos_t).then_inc(tab_in, 16)
            act.dma_start(sin_s[:], sin_t).then_inc(tab_in, 16)
            act.dma_start(lepe_bias[:, 0, :], lepe_b.partition_broadcast(P)).then_inc(tab_in, 16)

            def evacuate_next(r, par):
                act.wait_ge(t_filled, r + 1)
                for k in range(KC):
                    last = nc.scalar.activation(xnT_hi[par][:, k, 1:N + 1], tbk[k][:], ACT.Copy)
                last.then_inc(xnT_hi_ready, 1)

            def gate_part(b):
                r = round_gate(b)
                act.wait_ge(t_filled, r + 1)
                for k in range(KC):
                    last = nc.scalar.activation(xgT[:, k, :], tbk[k][:], ACT.Copy)
                last.then_inc(t_emptied, 1)
                act.wait_ge(t_filled, r + 2)
                nc.scalar.activation(sequence_tiles(logits, b - 1),
                                     tb0[:, 0:TB * EX].rearrange("p (t e) -> p t e", e=EX),
                                     ACT.Copy).then_inc(t_emptied, 1)

            evacuate_next(0, 0)
            act.wait_ge(wl_in, 16)
            nc.scalar.activation(lepe_hi[:], lepe_raw[:], ACT.Copy).then_inc(lepe_hi_ready, 1)
            act.wait_ge(w_in, 32)

            def period(b, par):
                wait_count(act, q_ready, b)
                for n, m in enumerate(ORDER):
                    act.wait_ge(qk_done, 4 * b + n + 1)
                    nc.scalar.activation(ex[:, m, :], proj[m][:], ACT.Exp, bias=qk_bias[:, m:m + 1])
                    nc.scalar.activation(re[:, m, :], proj[m][:], ACT.Relu, bias=qk_bias[:, m:m + 1]).then_inc(qk_evac, 1)
                if not is_first(b):
                    gate_part(b)
                act.wait_ge(t_filled, round_k(b) + 1)
                for k in range(KC):
                    last = nc.scalar.activation(krt[:, k, :, :].rearrange("p t d -> p (t d)"), tbk[k][:], ACT.Copy)
                last.then_inc(t_emptied, 1)
                if not is_last(b):
                    evacuate_next(round_next(b), 1 - par)

            over_batches(act, period)
            gate_part(B)

        @block.gpsimd
        def _(pool):
            own = OwnSteps(pool, own_pool, 4)

            def rstd(mvt, ready, done):
                own.link(nc.gpsimd.tensor_scalar(mvt[:, :, 1], mvt[:, :, 1], EPS, None, ALU.add))
                nc.gpsimd.tensor_tensor(mvt[:, :, 1], mvt[:, :, 1], neg_half[:, 0:TB], ALU.pow).then_inc(done, 1)

            def add_bias(b):
                xt = sequence_tiles(x, b)
                nc.gpsimd.tensor_tensor(xt, xt, lepe_bias[:].to_broadcast([P, TB, C]), ALU.add)

            own.round(0)
            pool.wait_ge(var_ready, 1)
            rstd(mv, var_ready, rstd_ready)
            pool.wait_ge(tab_in, 48)
            pool.wait_ge(xn_ready, 1)
            add_bias(0)
            own.pad()

            def period(b, par):
                own.round(b + 1)
                if not is_last(b):
                    wait_apart(pool, var_ready, b + 2, passed["pool"])
                    rstd(mv, var_ready, rstd_ready)
                if not is_first(b):
                    wait_apart(pool, var2_ready, b, passed["pool"])
                    rstd(mv2, var2_ready, rstd2_ready)
                pool.wait_ge(q_ready, b + 1)
                wait_count(pool, attn_done, 2 * b)
                nc.gpsimd.tensor_tensor(qA[:], el[:, 0:2, :], cos_s[:].to_broadcast([P, 2, N]), ALU.mult)
                nc.gpsimd.tensor_tensor(qB[:, 0, :], el[:, 1, :], nsin_s[:], ALU.mult)
                own.link(nc.gpsimd.tensor_tensor(qB[:, 1, :], el[:, 0, :], sin_s[:], ALU.mult))
                nc.gpsimd.tensor_tensor(qr[:], qA[:], qB[:], ALU.add).then_inc(qr_ready, 1)
                if not is_last(b):
                    wait_apart(pool, xn_ready, b + 2, passed["pool"])
                    add_bias(b + 1)
                for h in range(2):
                    wait_apart(pool, v_ready, 2 * b + h + 1, passed["pool"])
                    xt = x[:, bass.ds(b * TB + 2 * h, 2), :] if not isinstance(b, int) else x[:, b * TB + 2 * h:b * TB + 2 * h + 2, :]
                    nc.gpsimd.tensor_tensor(xt, xt, v[:, h, :, :], ALU.add).then_inc(x1_ready, 1)
                own.pad()

            over_batches(pool, period)
            own.round(B + 1)
            pool.wait_ge(var2_ready, B)
            rstd(mv2, var2_ready, rstd2_ready)

        @block.vector
        def _(dve):
            own = OwnSteps(dve, own_dve, 8)

            def statistics(bnt, mvt, b, done):
                for j in range(TB):
                    last = nc.vector.bn_stats(bnt[:, j, :], tile_of(x, b, j))
                own.link(last, passed["dve"])
                for j in range(TB):
                    last = nc.vector.bn_aggr(mvt[:, j, :], bnt[:, j, :])
                last.then_inc(done, 1)

            def normalise(dst, mvt, b, done):
                for j in range(TB):
                    last = nc.vector.tensor_scalar(dst[:, j, :], tile_of(x, b, j), mvt[:, j, 0:1], mvt[:, j, 1:2],
                                                   ALU.subtract, ALU.mult)
                last.then_inc(done, 1)

            def low_part(b, par):
                dve.wait_ge(xnT_hi_ready, b + 1)
                for k in range(KC):
                    last = nc.vector.tensor_tensor(xnT_lo[par][:, k, 1:N + 1], tbk[k][:],
                                                   xnT_hi[par][:, k, 1:N + 1].bitcast(F32), ALU.subtract)
                last.then_inc(t_emptied, 1)

            own.round(0)
            own.link(nc.vector.memset(edge[:], 0.0))
            for t in xnT_hi + xnT_lo:
                nc.vector.tensor_copy(t[:, :, 0:1], edge[:])
                nc.vector.tensor_copy(t[:, :, N + 1:N + 2], edge[:])
            dve.wait_ge(x0_in, 16)
            statistics(bn, mv, 0, var_ready)
            dve.wait_ge(w_in, 32)
            for h in range(2):
                for par in range(2):
                    last = nc.vector.tensor_copy(qk_hi[:, :, 2 * h + par, :],
                                                 qk_raw[:, :, h * C + par:(h + 1) * C:2])
            own.link(last)
            for h in range(2):
                for par in range(2):
                    last = nc.vector.tensor_tensor(qk_lo[:, :, 2 * h + par, :],
                                                   qk_raw[:, :, h * C + par:(h + 1) * C:2],
                                                   qk_hi[:, :, 2 * h + par, :].bitcast(F32), ALU.subtract)
            last.then_inc(w_ready, 1)
            dve.wait_ge(rstd_ready, 1)
            normalise(xn[0], mv, 0, xn_ready)
            dve.wait_ge(tab_in, 48)
            own.link(nc.vector.tensor_scalar(nsin_s[:], sin_s[:], -1.0, None, ALU.mult))
            low_part(0, 0)
            dve.wait_ge(lepe_hi_ready, 1)
            nc.vector.tensor_tensor(lepe_lo[:], lepe_raw[:], lepe_hi[:].bitcast(F32), ALU.subtract).then_inc(lepe_ready, 1)
            dve.wait_ge(x1_in, 16)
            own.pad()

            def route_before(b):
                dve.wait_ge(rstd2_ready, b)
                wait_count(dve, xg_stored, 16 * (b - 1))
                normalise(xg, mv2, b - 1, xg_ready)

            def period(b, par):
                own.round(b + 1)
                if isinstance(b, int) and b == 1 or not isinstance(b, int):
                    dve.wait_ge(x_in, 16)
                if not is_last(b):
                    statistics(bn, mv, b + 1, var_ready)
                if not is_first(b):
                    dve.wait_ge(x1_ready, 2 * b)
                    statistics(bn2, mv2, b - 1, var2_ready)
                dve.wait_ge(qk_evac, 4 * b + 2)
                for m in (2, 3):
                    last = nc.vector.scalar_tensor_tensor(out=el[:, m, :], in0=ex[:, m, :], scalar=1.0, in1=re[:, m, :],
                                                          op0=ALU.min, op1=ALU.add, accum_out=ksum[:, m - 2:m - 1])
                own.link(last)
                if not is_first(b):
                    route_before(b)
                if not is_last(b):
                    dve.wait_ge(rstd_ready, b + 2)
                    normalise(xn[1 - par], mv, b + 1, xn_ready)
                for m in range(2):
                    nc.vector.tensor_scalar(kz[:, m, :], head_mask[:], ksum[:, m:m + 1], None, ALU.mult)
                nc.vector.tensor_tensor(kA[:], el[:, 2:4, :], cos_s[:].to_broadcast([P, 2, N]), ALU.mult)
                nc.vector.tensor_tensor(kB[:, 0, :], el[:, 3, :], nsin_s[:], ALU.mult)
                own.link(nc.vector.tensor_tensor(kB[:, 1, :], el[:, 2, :], sin_s[:], ALU.mult))
                nc.vector.tensor_tensor(kr[:], kA[:], kB[:], ALU.add).then_inc(kr_ready, 1)
                dve.wait_ge(qk_evac, 4 * b + 4)
                wait_count(dve, qr_ready, b)
                nc.vector.scalar_tensor_tensor(out=el[:, 0:2, :], in0=ex[:, 0:2, :], scalar=1.0, in1=re[:, 0:2, :],
                                               op0=ALU.min, op1=ALU.add).then_inc(q_ready, 1)
                dve.wait_ge(z_done, b + 1)
                own.link(nc.vector.tensor_scalar(zr[:], q1[:, 0:TB * HEADS], 1e-6, None, ALU.add))
                dve.wait_ge(kv_done, b + 1)
                nc.vector.tensor_tensor(kvb[:], q0[:, 0:C].rearrange("p (k e) -> p k e", k=KC),
                                        block_mask[:].unsqueeze(1).to_broadcast([P, KC, P]), ALU.mult).then_inc(kvb_ready, 1)
                own.link(nc.vector.reciprocal(zr[:], zr[:]))
                if not is_last(b):
                    low_part(b + 1, 1 - par)
                dve.wait_ge(lepe_done, 2 * b + 2)
                for h in range(2):
                    dve.wait_ge(attn_done, 2 * b + h + 1)
                    zb = zr[:, h * 2 * HEADS:(h + 1) * 2 * HEADS].unsqueeze(2).to_broadcast([P, 2 * HEADS, HD])
                    own.link(nc.vector.tensor_tensor(u[:, h, :].rearrange("p (g e) -> p g e", e=HD),
                                                     q[2 + h][:].rearrange("p (g e) -> p g e", e=HD), zb, ALU.mult))
                    wait_count(dve, x1_ready, 2 * b + h - 1)
                    nc.vector.tensor_tensor(v[:, h, :, :].rearrange("p t c -> p (t c)"), u[:, h, :], lb[h][:],
                                            ALU.add).then_inc(v_ready, 1)
                own.pad()

            over_batches(dve, period)
            own.round(B + 1)
            dve.wait_ge(x1_ready, 2 * B)
            statistics(bn2, mv2, B - 1, var2_ready)
            route_before(B)
            own.pad()

        @block.tensor
        def _(pe):
            def transposes(src, filled_round):
                wait_count(pe, t_emptied, filled_round)
                for k in range(KC):
                    for j in range(TB):
                        last = nc.tensor.transpose(tbk[k][:, j * P:(j + 1) * P], src[:, j, k * P:(k + 1) * P], ident[:])
                last.then_inc(t_filled, 1)

            def gate_transposes(b):
                pe.wait_ge(xg_ready, b)
                transposes(xg, round_gate(b))

            def gate_products(b):
                pe.wait_ge(t_emptied, round_gate(b) + 1)
                for j in range(TB):
                    for k in range(KC):
                        last = nc.tensor.matmul(tb0[:, j * EX:(j + 1) * EX], xgT[:, k, j * P:(j + 1) * P], gate_s[:, k, :],
                                                start=(k == 0), stop=(k == KC - 1))
                last.then_inc(t_filled, 1)

            def convolution(par, j, taps=range(LT)):
                for t in taps:
                    for k in range(KC):
                        hi, lo = (x[par][:, k, j * P + t:j * P + t + P] for x in (xnT_hi, xnT_lo))
                        last = split_product(nc, lb[j // 2][:, (j % 2) * C:(j % 2 + 1) * C], hi, lo, lepe_hi[:, t, k, :],
                                       lepe_lo[:, t, k, :], t == k == 0, t == LT - 1 and k == KC - 1)
                if j % 2 and LT - 1 in taps:
                    last.then_inc(lepe_done, 1)

            pe.wait_ge(xn_ready, 1)
            transposes(xn[0], 0)
            pe.wait_ge(w_ready, 1)
            pe.wait_ge(w_in, 32)

            def period(b, par):
                pe.wait_ge(t_emptied, round_next(b - 1) + 1 if not is_first(b) else 1)
                for m in ORDER:
                    if m == 0:
                        wait_count(pe, v_ready, 2 * b)
                    for k in range(KC):
                        hi, lo = xnT_hi[par][:, k, 1:N + 1], xnT_lo[par][:, k, 1:N + 1]
                        last = split_product(nc, proj[m][:], qk_hi[:, k, m, :], qk_lo[:, k, m, :], hi, lo, k == 0, k == KC - 1)
                    last.then_inc(qk_done, 1)
                if is_first(b):
                    pe.wait_ge(lepe_ready, 1)
                convolution(par, 0)
                convolution(par, 1)
                if not is_first(b):
                    gate_transposes(b)
                convolution(par, 2)
                if not is_first(b):
                    gate_products(b)
                convolution(par, 3, (0,))
                pe.wait_ge(kr_ready, b + 1)
                pe.wait_ge(t_emptied, round_k(b))
                for k in range(KC):
                    for j in range(TB):
                        last = nc.tensor.transpose(tbk[k][:, j * P:(j + 1) * P], kr[:, k, j * P:(j + 1) * P], ident[:])
                last.then_inc(t_filled, 1)
                pe.wait_ge(q_ready, b + 1)
                for j in range(TB):
                    for m in range(2):
                        last = nc.tensor.matmul(q1[:, j * HEADS:(j + 1) * HEADS], el[:, m, j * P:(j + 1) * P], kz[:, m, :],
                                                start=(m == 0), stop=(m == 1))
                last.then_inc(z_done, 1)
                convolution(par, 3, (1,))
                pe.wait_ge(t_emptied, round_k(b) + 1)
                for k in range(KC):
                    for j in range(TB):
                        last = nc.tensor.matmul(q0[:, k * P:(k + 1) * P], krt[:, k, j, :], xn[par][:, j, k * P:(k + 1) * P],
                                                start=(j == 0), stop=(j == TB - 1))
                last.then_inc(kv_done, 1)
                if not is_last(b):
                    pe.wait_ge(xn_ready, b + 2)
                    transposes(xn[1 - par], round_next(b))
                convolution(par, 3, (2,))
                pe.wait_ge(kvb_ready, b + 1)
                pe.wait_ge(qr_ready, b + 1)
                for j in range(TB):
                    for k in range(KC):
                        last = nc.tensor.matmul(q[2 + j // 2][:, (j % 2) * C + k * P:(j % 2) * C + (k + 1) * P],
                                                qr[:, k, j * P:(j + 1) * P], kvb[:, k, :], start=True, stop=True)
                    if j % 2:
                        last.then_inc(attn_done, 1)

            over_batches(pe, period)
            gate_transposes(B)
            gate_products(B)
    nc.clear_and_free_semaphores(sems)
    nc.all_engine_barrier()


def phase_route(nc, tag, logits, row_token, row_score, block_expert, weights, bank, passed):
    w1, w2, w3, up_hi, up_lo, w2_s, w2_in = weights
    BLOCKS = NBLK
    with ExitStack() as ctx:
        def sb(name, shape, dt=F32):
            return ctx.enter_context(nc.sbuf_tensor(name, shape, dt))

        def sem(name):
            return ctx.enter_context(nc.semaphore(name))

        top = sb(tag + "r_top", [P, T, 8])
        topi = sb(tag + "r_topi", [P, T, 8], U32)
        idx = sb(tag + "r_idx", [P, TOPK, T])
        diff = sb(tag + "r_diff", [P, T, EX])
        d2 = sb(tag + "r_d2", [P, T])
        p2 = sb(tag + "r_p2", [P, T])
        tot_p = sb(tag + "r_tot_p", [P, T])
        rz = sb(tag + "r_rz", [P, T])
        expert_id = sb(tag + "r_expert_id", [P, EX, T])
        keep = sb(tag + "r_keep", [P, EX * T])
        ones_e = sb(tag + "r_ones_e", [P, EX])
        hot = sb(tag + "r_hot", [P, TOPK, EX, T])
        both = sb(tag + "r_both", [P, EX, T])
        before = sb(tag + "r_before", [P, P])
        ones = sb(tag + "r_ones", [P, P])
        tot = sb(tag + "r_tot", [P, EX, T])
        incl = both
        counti = sb(tag + "r_counti", [P, EX], I32)
        padded = sb(tag + "r_padded", [P, EX])
        endp = sb(tag + "r_endp", [P, EX])
        base = sb(tag + "r_base", [P, EX, 1])
        posf = sb(tag + "r_posf", [P, TOPK, T])
        row0 = sb(tag + "r_row0", [1, BLOCKS, EX])
        ebf = sb(tag + "r_ebf", [1, BLOCKS])
        score = sb(tag + "r_score", [P, TOPK, T])
        posi = sb(tag + "r_posi", [P, 2, TOPK, T], I32)
        blk = sb(tag + "r_blk", [P, 2, TOPK, T])
        lane = sb(tag + "r_lane", [P, P])
        blocks = sb(tag + "r_blocks", [P, BLOCKS])
        lane_of = sb(tag + "r_lane_of", [P, 1])
        token = sb(tag + "r_token", [P, T])
        DEPTH = 3
        CH = 2
        row_hot = [sb(tag + f"r_row_hot{i}", [P, TOPK, CH, P]) for i in range(DEPTH)]
        block_hot = [sb(tag + f"r_block_hot{i}", [P, TOPK, CH, BLOCKS]) for i in range(DEPTH)]
        sent = [sb(tag + f"r_sent{i}", [P, TOPK, CH, 2, BLOCKS]) for i in range(DEPTH)]
        spare = sb(tag + "r_spare", [P, BLOCKS])
        own_dve, made, top_ready, exp_done, both_ready, count_done, pos_ready = (
            sem(tag + "r_own_dve"), sem(tag + "r_made"), sem(tag + "r_top_ready"), sem(tag + "r_exp_done"), sem(tag + "r_both_ready"),
            sem(tag + "r_count_done"), sem(tag + "r_pos_ready"))
        RAW = 6
        raw = sb(tag + "r_raw", [P, RAW, H])
        raw_in = [sem(tag + f"r_raw_in{i}") for i in range(RAW)]
        hi_ready, lo_pool, lo_dve = sem(tag + "r_hi_ready"), sem(tag + "r_lo_pool"), sem(tag + "r_lo_dve")
        block_hot_ready, row_hot_ready, scores_sent, tokens_sent, sent_used = (
            sem(tag + "r_block_hot_ready"), sem(tag + "r_row_hot_ready"), sem(tag + "r_scores_sent"),
            sem(tag + "r_tokens_sent"), sem(tag + "r_sent_used"))
        block = ctx.enter_context(nc.Block())

        CHUNKS = EX * 2 * KC
        EARLY = 8
        DVE_CHUNKS = range(EARLY, CHUNKS, 2)
        POOL_CHUNKS = [c for c in range(CHUNKS) if c not in DVE_CHUNKS]

        def lows_before(chunks, c):
            return len([n for n in chunks if n < c])

        def low_part(engine, c, done):
            engine.wait_ge(hi_ready, c + 1)
            e, n, k = c // (2 * KC), c // KC % 2, c % KC
            part = slice(k * H, (k + 1) * H)
            engine.tensor_tensor(up_lo[n][:, e, part], raw[:, c % RAW, :], up_hi[n][:, e, part].bitcast(F32),
                                 ALU.subtract).then_inc(done, 1)

        @block.sync
        def _(sp):
            for c in range(CHUNKS):
                if c >= RAW:
                    before = c - RAW + 1
                    wait_count(sp, lo_dve, lows_before(DVE_CHUNKS, before))
                    wait_count(sp, lo_pool, lows_before(POOL_CHUNKS, before))
                e, n, k = c // (2 * KC), c // KC % 2, c % KC
                sp.dma_start(raw[:, c % RAW, :], (w1, w3)[n][e, k * P:(k + 1) * P, :]).then_inc(raw_in[c % RAW], 16)
                if c % (CHUNKS // EX) == CHUNKS // EX - 1:
                    sp.dma_start(w2_s[:, e, :].rearrange("p (k c) -> p k c", c=C),
                                 w2[e].rearrange("(k p) c -> p k c", p=P)).then_inc(w2_in, 16)

        @block.gpsimd
        def _(pool):
            nc.gpsimd.iota(expert_id[:], pattern=[[1, EX], [0, T]], base=0, channel_multiplier=0,
                           allow_small_or_imprecise_dtypes=True).then_inc(made, 1)
            nc.gpsimd.iota(row0[:], pattern=[[P, BLOCKS], [0, EX]], base=0, channel_multiplier=0,
                           allow_small_or_imprecise_dtypes=True).then_inc(made, 1)
            nc.gpsimd.memset(keep[:], 1.0).then_inc(made, 1)
            nc.gpsimd.memset(ones_e[:], 1.0).then_inc(made, 1)
            nc.gpsimd.memset(ones[:], 1.0).then_inc(made, 1)
            nc.gpsimd.memset(before[:], 1.0).then_inc(made, 1)
            pool.wait_ge(made, 6)
            nc.gpsimd.memset(keep[:].rearrange("p (e t) -> p e t", t=T)[:, :, 0:1], 0.0).then_inc(made, 1)
            nc.gpsimd.affine_select(out=before[:], in_=before[:], compare_op=ALU.is_ge, fill=0.0, base=-1,
                                    pattern=[[1, P]], channel_multiplier=-1).then_inc(made, 1)
            nc.gpsimd.iota(lane[:], pattern=[[1, P]], base=0, channel_multiplier=0,
                           allow_small_or_imprecise_dtypes=True).then_inc(made, 1)
            nc.gpsimd.iota(blocks[:], pattern=[[1, BLOCKS]], base=0, channel_multiplier=0,
                           allow_small_or_imprecise_dtypes=True).then_inc(made, 1)
            nc.gpsimd.iota(lane_of[:], pattern=[[0, 1]], base=0, channel_multiplier=1,
                           allow_small_or_imprecise_dtypes=True).then_inc(made, 1)
            nc.gpsimd.iota(token[:], pattern=[[P, T]], base=-T * P, channel_multiplier=1,
                           allow_small_or_imprecise_dtypes=True).then_inc(made, 1)
            pool.wait_ge(made, 12)
            for c in POOL_CHUNKS[:EARLY]:
                low_part(nc.gpsimd, c, lo_pool)
            for g in range(T // CH):
                pool.wait_ge(block_hot_ready, g + 1)
                if g >= DEPTH:
                    pool.wait_ge(sent_used, g - DEPTH + 1)
                ids = token[:, g * CH:(g + 1) * CH].unsqueeze(2).to_broadcast([P, CH, BLOCKS])
                for k in range(TOPK):
                    last = nc.gpsimd.tensor_tensor(sent[g % DEPTH][:, k, :, 0, :], block_hot[g % DEPTH][:, k, :, :], ids, ALU.mult)
                last.then_inc(tokens_sent, 1)
                if EARLY + g < len(POOL_CHUNKS):
                    low_part(nc.gpsimd, POOL_CHUNKS[EARLY + g], lo_pool)

        @block.scalar
        def _(act):
            def high_part(c):
                act.wait_ge(raw_in[c % RAW], 16 * (c // RAW + 1))
                e, n, k = c // (2 * KC), c // KC % 2, c % KC
                nc.scalar.activation(up_hi[n][:, e, k * H:(k + 1) * H], raw[:, c % RAW, :], ACT.Copy).then_inc(hi_ready, 1)

            act.wait_ge(top_ready, 1)
            nc.scalar.activation(diff[:], diff[:], ACT.Exp)
            nc.scalar.activation(p2[:], d2[:], ACT.Exp).then_inc(exp_done, 1)
            for c in range(EARLY + RAW):
                high_part(c)
            for g in range(T // CH):
                act.wait_ge(block_hot_ready, g + 1)
                if g >= DEPTH:
                    act.wait_ge(sent_used, g - DEPTH + 1)
                for k in range(TOPK):
                    for j in range(CH):
                        t = g * CH + j
                        last = nc.scalar.activation(sent[g % DEPTH][:, k, j, 1, :], block_hot[g % DEPTH][:, k, j, :], ACT.Copy,
                                                    scale=score[:, k, t:t + 1])
                last.then_inc(scores_sent, 1)
                if g >= 1:
                    for c in range(EARLY + RAW + 2 * (g - 1), min(EARLY + RAW + 2 * g, CHUNKS)):
                        high_part(c)

        @block.tensor
        def _(pe):
            pe.wait_ge(made, 8)
            pe.wait_ge(both_ready, 1)
            m = both[:].rearrange("p e t -> p (e t)")
            nc.tensor.matmul(bank[0][:, 0:EX * T], before[:], m, start=True, stop=True)
            nc.tensor.matmul(bank[1][:, 0:EX * T], ones[:], m, start=True, stop=True).then_inc(count_done, 1)
            out = bank[2][:, 0:2 * BLOCKS]
            for g in range(T // CH):
                pe.wait_ge(row_hot_ready, g + 1)
                pe.wait_ge(scores_sent, g + 1)
                pe.wait_ge(tokens_sent, g + 1)
                for k in range(TOPK):
                    for j in range(CH):
                        first, final = g == k == j == 0, g == T // CH - 1 and k == TOPK - 1 and j == CH - 1
                        last = nc.tensor.matmul(out, row_hot[g % DEPTH][:, k, j, :],
                                                sent[g % DEPTH][:, k, j, :, :].rearrange("p a b -> p (a b)"),
                                                start=first, stop=final)
                last.then_inc(sent_used, 1)

        @block.vector
        def _(dve):
            own = OwnSteps(dve, own_dve, 0)
            for t in range(T):
                last = nc.vector.max(top[:, t, :], logits[:, t, :])
            own.link(last)
            for t in range(T):
                last = nc.vector.max_index(topi[:, t, :], top[:, t, :], logits[:, t, :])
            nc.vector.tensor_tensor(d2[:], top[:, :, 1], top[:, :, 0], ALU.subtract)
            nc.vector.tensor_tensor(diff[:], logits[:], top[:, :, 0:1].to_broadcast([P, T, EX]),
                                    ALU.subtract).then_inc(top_ready, 1)
            dve.wait_ge(top_ready, 1)
            own.link(nc.vector.tensor_copy(idx[:], topi[:, :, 0:TOPK].rearrange("p t k -> p k t")))
            dve.wait_ge(made, 8)
            for k in range(TOPK):
                last = nc.vector.tensor_tensor(hot[:, k, :, :], idx[:, k:k + 1, :].to_broadcast([P, EX, T]),
                                               expert_id[:], ALU.is_equal)
            own.link(last)
            nc.vector.tensor_tensor(both[:], hot[:, 0, :, :], hot[:, 1, :, :], ALU.add).then_inc(both_ready, 1)
            dve.wait_ge(exp_done, 1)
            own.link(nc.vector.tensor_reduce(tot_p[:], diff[:], AXX, ALU.add))
            own.link(nc.vector.reciprocal(rz[:], tot_p[:]))
            nc.vector.tensor_copy(score[:, 0, :], rz[:])
            nc.vector.tensor_tensor(score[:, 1, :], p2[:], rz[:], ALU.mult)
            dve.wait_ge(count_done, 1)
            own.link(nc.vector.tensor_copy(tot[:].rearrange("p e t -> p (e t)"), bank[1][:, 0:EX * T]))
            own.link(nc.vector.tensor_tensor_scan(incl[:].rearrange("p e t -> p (e t)"), keep[:],
                                                  tot[:].rearrange("p e t -> p (e t)"), 0.0, ALU.mult, ALU.add))
            own.link(nc.vector.tensor_scalar(counti[:], incl[:, :, T - 1], float(P - 1), None, ALU.add))
            own.link(nc.vector.tensor_scalar(counti[:], counti[:], 7, 7, ALU.arith_shift_right, ALU.logical_shift_left))
            own.link(nc.vector.tensor_copy(padded[:], counti[:]))
            own.link(nc.vector.tensor_tensor_scan(endp[:], ones_e[:], padded[:], 0.0, ALU.mult, ALU.add))
            nc.vector.tensor_tensor(base[:, :, 0], endp[:], padded[:], ALU.subtract)
            own.link(nc.vector.tensor_tensor(tot[:], incl[:], tot[:], ALU.subtract))
            own.link(nc.vector.tensor_tensor(tot[:], tot[:], base[:].to_broadcast([P, EX, T]), ALU.add))
            own.link(nc.vector.tensor_tensor(tot[:], tot[:], bank[0][:, 0:EX * T].rearrange("p (e t) -> p e t", t=T),
                                             ALU.add))
            own.link(nc.vector.tensor_tensor(hot[:], hot[:], tot[:].unsqueeze(1).to_broadcast([P, TOPK, EX, T]), ALU.mult))
            own.link(nc.vector.tensor_reduce(posf[:], hot[:].rearrange("p k e t -> p k t e"), AXX, ALU.add))
            own.link(nc.vector.tensor_copy(posi[:, 0], posf[:]))
            own.link(nc.vector.tensor_scalar(posi[:, 1], posi[:, 0], P - 1, None, ALU.bitwise_and))
            own.link(nc.vector.tensor_scalar(posi[:, 0], posi[:, 0], 7, None, ALU.arith_shift_right))
            own.link(nc.vector.tensor_copy(blk[:], posi[:]))
            own.link(nc.vector.tensor_tensor(row0[:], row0[:], endp[0:1, :].unsqueeze(1).to_broadcast([1, BLOCKS, EX]), ALU.is_ge))
            own.link(nc.vector.tensor_reduce(ebf[:], row0[:], AXX, ALU.add))
            own.link(nc.vector.tensor_scalar(block_expert[:], ebf[:], float(EX - 1), None, ALU.min))
            dve.wait_ge(made, 12)
            for g in range(T // CH):
                if g >= DEPTH:
                    dve.wait_ge(sent_used, g - DEPTH + 1)
                tiles = slice(g * CH, (g + 1) * CH)
                for k in range(TOPK):
                    last = nc.vector.tensor_tensor(
                        block_hot[g % DEPTH][:, k], blk[:, 0, k, tiles].unsqueeze(2).to_broadcast([P, CH, BLOCKS]),
                        blocks[:].unsqueeze(1).to_broadcast([P, CH, BLOCKS]), ALU.is_equal)
                last.then_inc(block_hot_ready, 1)
                for k in range(TOPK):
                    last = nc.vector.tensor_tensor(
                        row_hot[g % DEPTH][:, k], blk[:, 1, k, tiles].unsqueeze(2).to_broadcast([P, CH, P]),
                        lane[:].unsqueeze(1).to_broadcast([P, CH, P]), ALU.is_equal)
                last.then_inc(row_hot_ready, 1)
                if g < len(DVE_CHUNKS):
                    low_part(nc.vector, DVE_CHUNKS[g], lo_dve)
            dve.wait_ge(sent_used, T // CH)
            nc.vector.tensor_copy(row_score[:], bank[2][:, BLOCKS:2 * BLOCKS])
            own.link(nc.vector.tensor_scalar(spare[:], bank[2][:, 0:BLOCKS], 0.0, lane_of[:, 0:1], ALU.is_equal, ALU.mult))
            own.link(nc.vector.scalar_tensor_tensor(out=row_token[:], in0=bank[2][:, 0:BLOCKS], scalar=float(T * P),
                                                    in1=spare[:], op0=ALU.add, op1=ALU.add))


def over_blocks(engine, body):
    assert NBLK % 2 == 1
    for i in range(3):
        body(i, i % 2)
    with engine.Fori(3, NBLK - 3, 2) as i:
        body(i, 1)
        body(i + 1, 0)
    for i in range(NBLK - 2, NBLK):
        body(i, i % 2)


def phase_experts(nc, tag, normed_dram, x_dram, w1, w2, w3, logits, ident, bank, passed):
    with ExitStack() as ctx:
        def sb(name, shape, dt=F32):
            return ctx.enter_context(nc.sbuf_tensor(tag + name, shape, dt))

        up_hi = [sb(f"up_hi{n}", [P, EX, KC * H], F32R) for n in range(2)]
        up_lo = [sb(f"up_lo{n}", [P, EX, KC * H], F32R) for n in range(2)]
        w2_s = sb("w2", [P, EX, HC * C])
        row_token = sb("row_token", [P, NBLK], U32)
        row_score = sb("row_score", [P, NBLK])
        block_expert = sb("block_expert", [1, NBLK], I32)
        w2_in = ctx.enter_context(nc.semaphore(tag + "w2_in"))
        phase_route(nc, tag, logits, row_token, row_score, block_expert, (w1, w2, w3, up_hi, up_lo, w2_s, w2_in), bank, passed)
        phase_blocks(nc, tag, normed_dram, x_dram, up_hi, up_lo, w2_s, w2_in, row_token, row_score, block_expert, ident, bank, passed)


def phase_blocks(nc, tag, normed_dram, x_dram, up_hi, up_lo, w2_s, w2_in, row_token, row_score, block_expert, ident, bank, passed):
    a_bank, b_bank, th_bank, xt_bank, y_bank = bank[0:2], bank[2:4], bank[4:6], bank[6], bank[7]
    with ExitStack() as ctx:
        def sb(name, shape, dt=F32):
            return ctx.enter_context(nc.sbuf_tensor(name, shape, dt))

        def sem(name):
            return ctx.enter_context(nc.semaphore(name))

        xs = [sb(tag + f"m_xs{i}", [P, C]) for i in range(2)]
        xT_hi = [sb(tag + f"m_xT_hi{i}", [P, KC * P], F32R) for i in range(2)]
        xT_lo = [sb(tag + f"m_xT_lo{i}", [P, KC * P], F32R) for i in range(2)]
        g = [sb(tag + f"m_g{i}", [P, H]) for i in range(2)]
        h = [sb(tag + f"m_h{i}", [P, H]) for i in range(2)]
        hT = [sb(tag + f"m_hT{i}", [P, HC, P]) for i in range(2)]
        y = [sb(tag + f"m_y{i}", [P, C]) for i in range(2)]
        gather_token = [sb(tag + f"m_gather_token{i}", [P, 1], U32) for i in range(2)]
        add_token = [sb(tag + f"m_add_token{i}", [P, 1], U32) for i in range(2)]
        loaded = [sem(tag + f"m_loaded{i}") for i in range(2)]
        added = sem(tag + "m_added")
        own_pool = sem(tag + "m_own_pool")
        hi_ready = sem(tag + "m_hi_ready")
        a_done, b_done, th_done, xt_done, y_done = (sem(tag + "m_a_done"), sem(tag + "m_b_done"), sem(tag + "m_th_done"),
                                                    sem(tag + "m_xt_done"), sem(tag + "m_y_done"))
        silu_done, th_evac, h_ready, xT_ready, y_evac = (sem(tag + "m_silu_done"), sem(tag + "m_th_evac"), sem(tag + "m_h_ready"),
                                                         sem(tag + "m_xT_ready"), sem(tag + "m_y_evac"))
        block = ctx.enter_context(nc.Block())

        def column(t, i):
            return t[:, bass.ds(i, 1)] if not isinstance(i, int) else t[:, i:i + 1]

        @block.gpsimd
        def _(pool):
            own = OwnSteps(pool, own_pool, 2)

            def gather(i, par):
                wait_count(pool, xt_done, i - 1)
                own.link(nc.gpsimd.tensor_copy(gather_token[par][:], column(row_token, i)), passed["pool"])
                nc.gpsimd.indirect_dma_start(xs[par][:], None, normed_dram[:],
                                             bass.IndirectOffsetOnAxis(ap=gather_token[par][:], axis=0)
                                             ).then_inc(loaded[par], 16)

            def add(i, par):
                pool.wait_ge(y_evac, i + 1)
                own.link(nc.gpsimd.tensor_copy(add_token[par][:], column(row_token, i)), passed["pool"])
                if not is_first(i):
                    wait_apart(pool, added, 16 * i, passed["pool"])
                nc.gpsimd.indirect_dma_start(x_dram[:], bass.IndirectOffsetOnAxis(ap=add_token[par][:], axis=0),
                                             y[par][:], None, compute_op=ALU.add).then_inc(added, 16)

            own.round(0)
            gather(0, 0)
            gather(1, 1)

            def step(i, par):
                own.round(i + 1)
                if not (isinstance(i, int) and i >= NBLK - 2):
                    gather(i + 2, par)
                if not is_first(i):
                    add(i - 1, 1 - par)
                own.pad()

            over_blocks(pool, step)
            own.round(NBLK + 1)
            add(NBLK - 1, 0)
            pool.wait_ge(added, 16 * NBLK)

        @block.scalar
        def _(act):
            def evacuate_h(i, par):
                act.wait_ge(th_done, i + 1)
                wait_count(act, y_done, i - 1)
                nc.scalar.activation(hT[par][:].rearrange("p k t -> p (k t)"), th_bank[par][:], ACT.Copy).then_inc(th_evac, 1)

            def step(i, par):
                act.wait_ge(a_done, i + 1)
                wait_count(act, h_ready, i - 1)
                nc.scalar.activation(g[par][:], a_bank[par][:], ACT.Silu).then_inc(silu_done, 1)
                if not is_first(i):
                    evacuate_h(i - 1, 1 - par)

            over_blocks(act, step)
            evacuate_h(NBLK - 1, 0)

        @block.vector
        def _(dve):
            def evacuate_x(i, par):
                dve.wait_ge(xt_done, i + 1)
                wait_count(dve, b_done, i - 1)
                nc.vector.tensor_copy(xT_hi[par][:], xt_bank[:, 0:C]).then_inc(hi_ready, 1)
                dve.wait_ge(hi_ready, i + 1)
                nc.vector.tensor_tensor(xT_lo[par][:], xt_bank[:, 0:C], xT_hi[par][:].bitcast(F32), ALU.subtract).then_inc(xT_ready, 1)

            def evacuate_y(i, par):
                dve.wait_ge(y_done, i + 1)
                if not (isinstance(i, int) and i < 2):
                    dve.wait_ge(added, 16 * (i - 1))
                nc.vector.tensor_scalar(y[par][:], y_bank[:, 0:C], column(row_score, i), None, ALU.mult).then_inc(y_evac, 1)

            evacuate_x(0, 0)

            def step(i, par):
                dve.wait_ge(silu_done, i + 1)
                dve.wait_ge(b_done, i + 1)
                wait_count(dve, th_done, i - 1)
                nc.vector.tensor_tensor(h[par][:], g[par][:], b_bank[par][:], ALU.mult).then_inc(h_ready, 1)
                if not (isinstance(i, int) and i == NBLK - 1):
                    evacuate_x(i + 1, 1 - par)
                if not is_first(i):
                    evacuate_y(i - 1, 1 - par)

            over_blocks(dve, step)
            evacuate_y(NBLK - 1, 0)

        @block.tensor
        def _(pe):
            def transpose_x(i, par):
                pe.wait_ge(loaded[par], 8 * (i - par) + 16)
                wait_count(pe, xT_ready, i)
                for k in range(KC):
                    last = nc.tensor.transpose(xt_bank[:, k * P:(k + 1) * P], xs[par][:, k * P:(k + 1) * P], ident[:])
                last.then_inc(xt_done, 1)

            def expert_of(i):
                return pe.value_load(block_expert[0:1, bass.ds(i, 1)] if not isinstance(i, int) else block_expert[0:1, i:i + 1],
                                     min_val=0, max_val=EX - 1)

            def weights(w, e):
                return w[:, bass.ds(e, 1), :].rearrange("p a n -> p (a n)")

            def up(n, e, par, out, done):
                for k in range(KC):
                    hi, lo = (t[par][:, k * P:(k + 1) * P] for t in (xT_hi, xT_lo))
                    w_hi, w_lo = (weights(w[n], e)[:, k * H:(k + 1) * H] for w in (up_hi, up_lo))
                    last = split_product(nc, out[:], hi, lo, w_hi, w_lo, k == 0, k == KC - 1)
                last.then_inc(done, 1)

            def transpose_h(i, par):
                pe.wait_ge(h_ready, i + 1)
                wait_count(pe, th_evac, i - 1)
                for k in range(HC):
                    last = nc.tensor.transpose(th_bank[par][:, k * P:(k + 1) * P], h[par][:, k * P:(k + 1) * P], ident[:])
                last.then_inc(th_done, 1)

            def down(i, par, e):
                pe.wait_ge(th_evac, i + 1)
                wait_count(pe, y_evac, i)
                for k in range(HC):
                    last = nc.tensor.matmul(y_bank[:, 0:C], hT[par][:, k, :], weights(w2_s, e)[:, k * C:(k + 1) * C],
                                            start=(k == 0), stop=(k == HC - 1))
                last.then_inc(y_done, 1)

            transpose_x(0, 0)
            pe.wait_ge(w2_in, 16 * EX)

            def step(i, par):
                e = expert_of(i)
                pe.wait_ge(xT_ready, i + 1)
                wait_count(pe, silu_done, i - 1)
                up(0, e, par, a_bank[par], a_done)
                if not is_first(i):
                    transpose_h(i - 1, 1 - par)
                wait_count(pe, h_ready, i - 1)
                up(1, e, par, b_bank[par], b_done)
                if not (isinstance(i, int) and i == NBLK - 1):
                    transpose_x(i + 1, 1 - par)
                if not is_first(i):
                    down(i - 1, 1 - par, expert_of(i - 1))

            over_blocks(pe, step)
            transpose_h(NBLK - 1, 0)
            down(NBLK - 1, 0, expert_of(NBLK - 1))


def phase_mix(nc, vec, w_key, w_value, w_recept, w_output, f_w_key, f_w_recept, f_w_value, gate_s,
              x_from, normed_dram, x_to, logits, ident, neg_half, bank, passed):
    tbk, xb_ = bank[0:2], bank[2:8]
    with ExitStack() as ctx:
        def sb(name, shape, dt=F32):
            return ctx.enter_context(nc.sbuf_tensor("b_" + name, shape, dt))

        def sem(name):
            return ctx.enter_context(nc.semaphore("b_" + name))

        x = sb("x", [P, T, C])
        wk_s, wv_s, wr_s, wo_s, wf_s = (sb(f"w{n}", [P, KC, C]) for n in "kvrof")
        fk_s, fv_s = sb("fk", [P, KC, F]), sb("fv", [P, FCH, C])
        decay, ndecay = sb("decay", [P, KC]), sb("ndecay", [P, KC])
        bn, mv, bn1, mv1 = sb("bn", [P, TB, 6]), sb("mv", [P, TB, 2]), sb("bn1", [P, TB, 6]), sb("mv1", [P, TB, 2])
        bn2, mv2, bng, mvg = sb("bn2", [P, TB, 6]), sb("mv2", [P, TB, 2]), sb("bng", [P, TB, 6]), sb("mvg", [P, TB, 2])
        mv_all = sb("mv_all", [P, T, 2])
        a, xn = sb("a", [P, TB, C]), sb("xn", [P, TB, C])
        xnT = sb("xnT", [P, KC, N + 1])
        dT = sb("dT", [P, KC, N])
        xk, xv, xr = sb("xk", [P, KC, N]), sb("xv", [P, KC, N]), sb("xr", [P, KC, N])
        k, v, sg = sb("k", [P, KC, N]), sb("v", [P, KC, N]), sb("sg", [P, KC, N])
        eps = sb("eps", [P, KC, N + 1])
        e1, e2, d1, d2 = (sb(n, [P, KC, N]) for n in ("e1", "e2", "d1", "d2"))
        al, be = sb("al", [P, KC, N + 1]), sb("be", [P, KC, N + 1])
        dv, ev, gT = sb("dv", [P, KC, N]), sb("ev", [P, KC, N]), sb("gT", [P, KC, N])
        xb, xn2, xn2T = sb("xb", [P, TB, C]), sb("xn2", [P, TB, C]), sb("xn2T", [P, KC, N + 1])
        xfk, xfr = sb("xfk", [P, KC, N]), sb("xfr", [P, KC, N])
        hT, fs = sb("hT", [P, FCH, N]), sb("fs", [P, 2, N])
        xg, xgT = sb("xg", [P, TB, C]), sb("xgT", [P, KC, N])

        w_time_in, w_in, prep = sem("w_time_in"), sem("w_in"), sem("prep")
        x_in = [sem(f"x_in{i}") for i in range(3)]
        x_stored, xg_stored = sem("x_stored"), sem("xg_stored")
        own_f, own_m, own_r, own_w, own_g = (sem(f"own_{n}") for n in "fmrwg")
        eps_ready, a_ready, xb_added = sem("eps_ready"), sem("a_ready"), sem("xb_added")
        num_scaled, num_summed, num_ready = sem("num_scaled"), sem("num_summed"), sem("num_ready")
        own_pool = sem("own_pool")
        var_ready, rstd_ready, var1_ready, rstd1_ready = sem("var_ready"), sem("rstd_ready"), sem("var1_ready"), sem("rstd1_ready")
        var2_ready, rstd2_ready, varg_ready, rstdg_ready = sem("var2_ready"), sem("rstd2_ready"), sem("varg_ready"), sem("rstdg_ready")
        xn_ready, t_filled, t_emptied, mix_ready = sem("xn_ready"), sem("t_filled"), sem("t_emptied"), sem("mix_ready")
        kvr_done, kvr_evac, s_ready, d2_ready, expd = sem("kvr_done"), sem("kvr_evac"), sem("s_ready"), sem("d2_ready"), sem("expd")
        dv_ready, ev_ready, sg_ready, g_ready = sem("dv_ready"), sem("ev_ready"), sem("sg_ready"), sem("g_ready")
        wo_done, xb_ready, xn2_ready, mix2_ready = sem("wo_done"), sem("xb_ready"), sem("xn2_ready"), sem("mix2_ready")
        fk_done, h_relu, h_ready, fr_done = sem("fk_done"), sem("h_relu"), sem("h_ready"), sem("fr_done")
        fs_ready, fs2_ready, vk_done, sum_ready, x3_ready, xg_ready = (sem("fs_ready"), sem("fs2_ready"), sem("vk_done"),
                                                                       sem("sum_ready"), sem("x3_ready"), sem("xg_ready"))
        block = ctx.enter_context(nc.Block())

        def static(b, value):
            return isinstance(b, int) and b == value

        def round_xn2(b):
            return 2 if static(b, 0) else 4 * b - 1 if static(b, B - 1) else 4 * b

        def round_gate(b):
            return 4 * b if static(b, B - 1) else 4 * b - 2 if static(b, B) else 4 * b + 1

        def round_xn(b):
            return b if isinstance(b, int) and b < 2 else 4 * b - 5

        def has_next(b, n):
            return not (isinstance(b, int) and b + n >= B)

        def over_periods(engine, body):
            body(0)
            with engine.Fori(1, B - 2) as b:
                body(b)
            body(B - 2)
            body(B - 1)

        @block.sync
        def _(sp):
            def load_x(b):
                sp.dma_start(sequence_tiles(x, b), token_rows(x_from, b)).then_inc(x_in[min(b, 2)], 16)

            def load_weight(dst, src, done):
                sp.dma_start(dst[:], src.rearrange("(k p) n -> p k n", p=P)).then_inc(done, 16)

            load_x(0)
            for dst, src in ((wk_s, w_key), (wv_s, w_value), (wr_s, w_recept)):
                load_weight(dst, src, w_time_in)
            load_x(1)
            for dst, src in ((wo_s, w_output), (wf_s, f_w_recept), (fk_s, f_w_key), (fv_s, f_w_value)):
                load_weight(dst, src, w_in)
            for b in range(2, B):
                load_x(b)

            def store(b):
                sp.wait_ge(x3_ready, b + 1)
                sp.dma_start(token_rows(x_to, b), sequence_tiles(x, b)).then_inc(x_stored, 16)
                sp.wait_ge(xg_ready, b + 1)
                sp.dma_start(token_rows(normed_dram, b), xg[:]).then_inc(xg_stored, 16)

            over_periods(sp, store)
            sp.wait_ge(x_stored, 16 * B)
            sp.wait_ge(xg_stored, 16 * B)

        @block.scalar
        def _(act):
            nc.scalar.activation(decay[:], vec["time_decay"], ACT.Exp).then_inc(prep, 1)

            def evacuate_norm(dst, w, bias, r):
                act.wait_ge(t_filled, r + 1)
                for i in range(KC):
                    last = nc.scalar.activation(dst[:, i, 1:N + 1], tbk[i][:], ACT.Identity, bias=vec[bias][:, i:i + 1],
                                                scale=vec[w][:, i:i + 1])
                last.then_inc(t_emptied, 1)

            def evacuate_xn(b):
                wait_count(act, mix_ready, 3 * b)
                evacuate_norm(xnT, "ln1_w", "ln1_b", round_xn(b))

            def evacuate(b, n, dst, src):
                act.wait_ge(kvr_done, 6 * b + n + 1)
                f, scale = (ACT.Tanh, 0.5) if dst is sg else (ACT.Copy, 1.0)
                nc.scalar.activation(dst[:, n % 2, :], xb_[src][:], f, scale=scale).then_inc(kvr_evac, 1)

            def evacuate_kv(b):
                wait_count(act, g_ready, b)
                for n, (dst, src) in enumerate(((k, 4), (k, 5), (v, 2), (v, 3))):
                    evacuate(b, n, dst, src)

            def evacuate_r(b):
                evacuate(b, 4, sg, 0)
                evacuate(b, 5, sg, 1)

            def exponential(b, step):
                if step == 0:
                    act.wait_ge(d2_ready, b + 1)
                    nc.scalar.activation(d2[:], d2[:], ACT.Exp).then_inc(expd, 1)
                elif step == 1:
                    act.wait_ge(s_ready, 2 * b + 1)
                    nc.scalar.activation(d1[:], d1[:], ACT.Exp).then_inc(expd, 1)
                elif step == 2:
                    act.wait_ge(s_ready, 2 * b + 2)
                    nc.scalar.activation(e2[:], e1[:], ACT.Relu, scale=-1.0).then_inc(expd, 1)
                elif step == 3:
                    act.wait_ge(expd, 6 * b + 3)
                    nc.scalar.activation(e1[:], e1[:], ACT.Relu).then_inc(expd, 1)
                elif step == 4:
                    nc.scalar.activation(e2[:], e2[:], ACT.Exp, scale=-1.0).then_inc(expd, 1)
                else:
                    act.wait_ge(expd, 6 * b + 4)
                    nc.scalar.activation(e1[:], e1[:], ACT.Exp, scale=-1.0).then_inc(expd, 1)

            def hidden(b):
                wait_count(act, vk_done, 2 * b)
                if has_next(b, 1):
                    exponential(b + 1, 0)
                    exponential(b + 1, 1)
                for m in range(FCH):
                    act.wait_ge(fk_done, FCH * b + m + 1)
                    nc.scalar.activation(hT[:, m, :], xb_[m % 4][:], ACT.Relu).then_inc(h_relu, 1)
                    act.wait_ge(h_relu, FCH * b + m + 1)
                    nc.scalar.activation(hT[:, m, :], hT[:, m, :], ACT.Square).then_inc(h_ready, 1)
                    if has_next(b, 1) and m < 4:
                        exponential(b + 1, m + 2)
                wait_count(act, x3_ready, b)
                for h in range(2):
                    act.wait_ge(fr_done, 2 * b + h + 1)
                    nc.scalar.activation(fs[:, h, :], xb_[4 + h][:], ACT.Tanh, scale=0.5).then_inc(fs_ready, 1)

            def gate_part(b):
                r = round_gate(b)
                act.wait_ge(t_filled, r + 1)
                for i in range(KC):
                    last = nc.scalar.activation(xgT[:, i, :], tbk[i][:], ACT.Copy)
                last.then_inc(t_emptied, 1)
                act.wait_ge(t_filled, r + 2)
                nc.scalar.activation(sequence_tiles(logits, b - 1),
                                     tbk[0][:, 0:TB * EX].rearrange("p (t e) -> p t e", e=EX),
                                     ACT.Copy).then_inc(t_emptied, 1)

            def carry(b):
                wait_count(act, xb_added, b)
                wait_count(act, xn2_ready, b)
                act.wait_ge(xn_ready, b + 1)
                act.sem_inc(passed["act"], 1)
                for j in range(TB):
                    stat = tile_of(mv_all, b, j)
                    last = nc.scalar.activation(xb[:, j, :], tile_of(x, b, j), ACT.Identity, bias=stat[:, 0:1], scale=stat[:, 1:2])
                last.then_inc(a_ready, 1)

            evacuate_xn(0)
            evacuate_kv(0)
            evacuate_r(0)
            evacuate_xn(1)
            for step in range(6):
                exponential(0, step)
            carry(0)

            def period(b):
                if has_next(b, 1):
                    evacuate_kv(b + 1)
                wait_count(act, mix2_ready, 2 * b)
                evacuate_norm(xn2T, "ln2_w", "ln2_b", round_xn2(b))
                if has_next(b, 1):
                    evacuate_r(b + 1)
                if not static(b, 0):
                    gate_part(b)
                hidden(b)
                if has_next(b, 1):
                    carry(b + 1)
                if has_next(b, 2):
                    evacuate_xn(b + 2)

            over_periods(act, period)
            gate_part(B)

        @block.gpsimd
        def _(pool):
            def rstd(mvt, ready, done, count, value):
                wait_apart(pool, ready, count, passed["pool"])
                nc.gpsimd.tensor_scalar(mvt[:, :, 1], mvt[:, :, 1], EPS, None, ALU.add).then_inc(own_pool, 1)
                pool.wait_ge(own_pool, value)
                nc.gpsimd.tensor_tensor(mvt[:, :, 1], mvt[:, :, 1], neg_half[:, 0:TB], ALU.pow).then_inc(done, 1)

            def norm_begun(b, value):
                rstd(mv, var_ready, rstd_ready, b + 1, value)

            def norm_begun1(b, value):
                rstd(mv1, var1_ready, rstd1_ready, b + 1, value)

            def gate_scaled(b):
                wait_count(pool, g_ready, b)
                wait_apart(pool, kvr_evac, 6 * b + 6, passed["pool"])
                nc.gpsimd.tensor_scalar(sg[:], sg[:], 0.5, 0.5, ALU.mult, ALU.add).then_inc(sg_ready, 1)

            def entering_exponent(b):
                wait_apart(pool, eps_ready, b + 1, passed["pool"])
                nc.gpsimd.tensor_tensor(d2[:], k[:], eps[:, :, 1:N + 1], ALU.subtract).then_inc(d2_ready, 1)

            def decayed_value(b):
                pool.wait_ge(expd, 6 * b + 1)
                nc.gpsimd.tensor_tensor(dv[:], d2[:], v[:], ALU.mult).then_inc(dv_ready, 1)

            def entering_value(b):
                pool.wait_ge(expd, 6 * b + 5)
                nc.gpsimd.tensor_tensor(ev[:], e2[:], v[:], ALU.mult).then_inc(ev_ready, 1)

            def numerator(b):
                wait_apart(pool, num_scaled, b + 1, passed["pool"])
                wait_apart(pool, ev_ready, b + 1, passed["pool"])
                nc.gpsimd.tensor_tensor(dv[:], dv[:], ev[:], ALU.add).then_inc(num_summed, 1)
                wait_apart(pool, num_summed, b + 1, passed["pool"])
                nc.gpsimd.tensor_tensor(dv[:], dv[:], sg[:], ALU.mult).then_inc(num_ready, 1)

            def add_mixed(b):
                wait_apart(pool, xb_ready, 2 * b + 2, passed["pool"])
                xt = sequence_tiles(x, b)
                nc.gpsimd.tensor_tensor(xt, xt, xb[:], ALU.add).then_inc(xb_added, 1)

            norm_begun(0, 1)
            norm_begun1(0, 2)
            norm_begun(1, 3)
            norm_begun1(1, 4)
            gate_scaled(0)
            entering_exponent(0)
            decayed_value(0)
            entering_value(0)
            numerator(0)
            rstd(mv2, var2_ready, rstd2_ready, 1, 5)

            def period(b):
                done = 5 if static(b, 0) else 4 * b + 4
                if static(b, B - 1):
                    done = 4 * (B - 2) + 4 + 2
                if not static(b, 0):
                    rstd(mvg, varg_ready, rstdg_ready, b, done + 1)
                    done = done + 1
                if has_next(b, 1):
                    gate_scaled(b + 1)
                    entering_exponent(b + 1)
                add_mixed(b)
                if has_next(b, 2):
                    norm_begun(b + 2, done + 1)
                if has_next(b, 1):
                    decayed_value(b + 1)
                if has_next(b, 2):
                    norm_begun1(b + 2, done + 2)
                    done = done + 2
                if has_next(b, 1):
                    entering_value(b + 1)
                    numerator(b + 1)
                wait_apart(pool, fs_ready, 2 * b + 2, passed["pool"])
                nc.gpsimd.tensor_scalar(fs[:], fs[:], 0.5, 0.5, ALU.mult, ALU.add).then_inc(fs2_ready, 1)
                if has_next(b, 1):
                    rstd(mv2, var2_ready, rstd2_ready, b + 2, done + 1)
                wait_count(pool, xb_added, b + 1)
                wait_apart(pool, sum_ready, b + 1, passed["pool"])
                xt = sequence_tiles(x, b)
                nc.gpsimd.tensor_tensor(xt, xt, fs[:].rearrange("p h (t c) -> p (h t) c", c=C), ALU.add).then_inc(x3_ready, 1)

            over_periods(pool, period)
            rstd(mvg, varg_ready, rstdg_ready, B, 4 * (B - 2) + 4 + 2 + 2)

        @block.vector
        def _(dve):
            f, m_, e_, r_, w_, g_ = (OwnSteps(dve, sm, n) for sm, n in ((own_f, 3), (own_m, 1), (eps_ready, 1), (own_r, 3),
                                                                        (own_w, 1), (own_g, 1)))
            m2 = OwnSteps(dve, sem("own_m2"), 1)

            def statistics(src, bnt, mvt, own, done):
                for j in range(TB):
                    last = nc.vector.bn_stats(bnt[:, j, :], src(j))
                own.link(last, passed["dve"])
                for j in range(TB):
                    last = nc.vector.bn_aggr(mvt[:, j, :], bnt[:, j, :])
                last.then_inc(done, 1)

            def normalise(dst, src, mvt):
                for j in range(TB):
                    last = nc.vector.tensor_scalar(dst[:, j, :], src(j), mvt(j)[:, 0:1], mvt(j)[:, 1:2],
                                                   ALU.subtract, ALU.mult)
                return last

            def begin(b):
                f.round(b)
                statistics(lambda j: tile_of(x, b, j), bn, mv, f, var_ready)

            def begin_a(b):
                dve.wait_ge(rstd_ready, b + 1)
                nc.vector.tensor_copy(sequence_tiles(mv_all, b)[:, :, 1], mv[:, :, 1])
                nc.vector.scalar_tensor_tensor(out=sequence_tiles(mv_all, b)[:, :, 0], in0=mv[:, :, 0], scalar=-1.0,
                                               in1=mv[:, :, 1], op0=ALU.mult, op1=ALU.mult)
                f.link(normalise(a, lambda j: tile_of(x, b, j), lambda j: mv[:, j, :]))
                statistics(lambda j: a[:, j, :], bn1, mv1, f, var1_ready)

            def begin_xn(b):
                dve.wait_ge(rstd1_ready, b + 1)
                normalise(xn, lambda j: a[:, j, :], lambda j: mv1[:, j, :]).then_inc(xn_ready, 1)

            def mixes(own, src, outs, b, done):
                own.round(b)
                own.link(nc.vector.tensor_tensor(dT[:], src[:, :, 1:N + 1], src[:, :, 0:N], ALU.subtract))
                for dst, m in outs:
                    for i in range(KC):
                        last = nc.vector.scalar_tensor_tensor(out=dst[:, i, :], in0=dT[:, i, :], scalar=vec[m][:, i:i + 1],
                                                              in1=src[:, i, 0:N], op0=ALU.mult, op1=ALU.add)
                    last.then_inc(done, 1)

            def mix_time(b):
                dve.wait_ge(t_emptied, round_xn(b) + 1)
                wait_count(dve, kvr_done, 6 * b)
                mixes(m_, xnT, ((xk, "time_mix_k"), (xv, "time_mix_v"), (xr, "time_mix_r")), b, mix_ready)

            def exponent_scan(b):
                dve.wait_ge(kvr_evac, 6 * b + 2)
                e_.round(b)
                for i in range(KC):
                    last = nc.vector.tensor_tensor_scan(eps[:, i, 1:N + 1], ndecay[:, i:i + 1].to_broadcast([P, N]),
                                                        k[:, i, :], EPS_INIT, ALU.add, ALU.max)
                e_.link(last)

            def exponents(b):
                for i in range(KC):
                    last = nc.vector.scalar_tensor_tensor(out=d1[:, i, :], in0=eps[:, i, 0:N], scalar=decay[:, i:i + 1],
                                                          in1=eps[:, i, 1:N + 1], op0=ALU.subtract, op1=ALU.subtract)
                last.then_inc(s_ready, 1)
                for i in range(KC):
                    last = nc.vector.scalar_tensor_tensor(out=e1[:, i, :], in0=k[:, i, :], scalar=vec["time_first"][:, i:i + 1],
                                                          in1=eps[:, i, 0:N], op0=ALU.add, op1=ALU.subtract)
                last.then_inc(s_ready, 1)

            def recurrence(b):
                r_.round(b)
                dve.wait_ge(expd, 6 * b + 2)
                for i in range(KC):
                    nc.vector.tensor_tensor_scan(be[:, i, 1:N + 1], d1[:, i, :], d2[:, i, :], 0.0, ALU.mult, ALU.add)
                dve.wait_ge(dv_ready, b + 1)
                for i in range(KC):
                    last = nc.vector.tensor_tensor_scan(al[:, i, 1:N + 1], d1[:, i, :], dv[:, i, :], 0.0, ALU.mult, ALU.add)
                r_.link(last)

            def output(b):
                dve.wait_ge(expd, 6 * b + 6)
                nc.vector.tensor_tensor(d1[:], e1[:], be[:, :, 0:N], ALU.mult)
                nc.vector.tensor_tensor(dv[:], e1[:], al[:, :, 0:N], ALU.mult).then_inc(num_scaled, 1)
                dve.wait_ge(num_scaled, b + 1)
                r_.link(nc.vector.tensor_tensor(d1[:], d1[:], e2[:], ALU.add))

            def output_quotient(b):
                r_.link(nc.vector.reciprocal(d1[:], d1[:]))
                dve.wait_ge(num_ready, b + 1)
                nc.vector.tensor_tensor(gT[:], dv[:], d1[:], ALU.mult).then_inc(g_ready, 1)

            def time_output(b):
                w_.round(b)
                dve.wait_ge(a_ready, b + 1)
                for h in range(2):
                    dve.wait_ge(wo_done, 2 * b + h + 1)
                    t = xb[:, 2 * h:2 * h + 2, :].rearrange("p t c -> p (t c)")
                    nc.vector.tensor_tensor(t, t, xb_[h][:], ALU.add).then_inc(xb_ready, 1)
                dve.wait_ge(xb_ready, 2 * b + 2)
                statistics(lambda j: xb[:, j, :], bn2, mv2, w_, var2_ready)

            def norm2(b):
                dve.wait_ge(rstd2_ready, b + 1)
                normalise(xn2, lambda j: xb[:, j, :], lambda j: mv2[:, j, :]).then_inc(xn2_ready, 1)

            def mix_channel(b):
                dve.wait_ge(t_emptied, round_xn2(b) + 1)
                mixes(m2, xn2T, ((xfk, "f_time_mix_k"), (xfr, "f_time_mix_r")), b, mix2_ready)

            def route_statistics(b):
                g_.round(b)
                dve.wait_ge(x3_ready, b + 1)
                statistics(lambda j: tile_of(x, b, j), bng, mvg, g_, varg_ready)

            def route_norm(b):
                dve.wait_ge(rstdg_ready, b + 1)
                wait_count(dve, xg_stored, 16 * b)
                normalise(xg, lambda j: tile_of(x, b, j), lambda j: mvg[:, j, :]).then_inc(xg_ready, 1)

            def finish(b, h):
                dve.wait_ge(vk_done, 2 * b + h + 1)
                return nc.vector.tensor_tensor(fs[:, h, :], fs[:, h, :], xb_[2 + h][:], ALU.mult)

            nc.vector.memset(xnT[:, :, 0:1], 0.0)
            nc.vector.memset(xn2T[:, :, 0:1], 0.0)
            nc.vector.memset(eps[:, :, 0:1], EPS_INIT)
            nc.vector.memset(al[:, :, 0:1], 0.0)
            nc.vector.memset(be[:, :, 0:1], 0.0)
            dve.wait_ge(x_in[0], 16)
            begin(0)
            begin_a(0)
            begin_xn(0)
            dve.wait_ge(prep, 1)
            nc.vector.tensor_scalar(ndecay[:], decay[:], -1.0, None, ALU.mult).then_inc(prep, 1)
            dve.wait_ge(prep, 2)
            mix_time(0)
            dve.wait_ge(x_in[1], 16)
            begin(1)
            begin_a(1)
            begin_xn(1)
            exponent_scan(0)
            exponents(0)
            recurrence(0)
            output(0)
            output_quotient(0)
            mix_time(1)
            dve.wait_ge(x_in[2], 16 * (B - 2))

            time_output(0)
            norm2(0)

            def period(b):
                if not static(b, 0):
                    route_statistics(b - 1)
                    route_norm(b - 1)
                if has_next(b, 1):
                    exponent_scan(b + 1)
                mix_channel(b)
                if has_next(b, 1):
                    exponents(b + 1)
                if has_next(b, 2):
                    begin(b + 2)
                if has_next(b, 1):
                    recurrence(b + 1)
                if has_next(b, 2):
                    begin_a(b + 2)
                if has_next(b, 1):
                    output(b + 1)
                if has_next(b, 2):
                    begin_xn(b + 2)
                if has_next(b, 1):
                    output_quotient(b + 1)
                dve.wait_ge(fs2_ready, b + 1)
                finish(b, 0)
                if has_next(b, 2):
                    mix_time(b + 2)
                if has_next(b, 1):
                    time_output(b + 1)
                    norm2(b + 1)
                finish(b, 1).then_inc(sum_ready, 1)

            over_periods(dve, period)
            route_statistics(B - 1)
            route_norm(B - 1)

        @block.tensor
        def _(pe):
            def transposes(src, r):
                wait_count(pe, t_emptied, r)
                for i in range(KC):
                    for j in range(TB):
                        last = nc.tensor.transpose(tbk[i][:, j * P:(j + 1) * P], src[:, j, i * P:(i + 1) * P], ident[:])
                last.then_inc(t_filled, 1)

            def token_product(out, src, w, chunks):
                for j in range(2):
                    for i in range(chunks):
                        last = nc.tensor.matmul(out[:, j * C:(j + 1) * C], src(i, j), w[:, i, :],
                                                start=(i == 0), stop=(i == chunks - 1))
                return last

            def cut(src, h):
                return lambda i, j: src[:, i, (2 * h + j) * P:(2 * h + j + 1) * P]

            def project(b, n, w, src, banks):
                pe.wait_ge(mix_ready, 3 * b + n + 1)
                for c in range(KC):
                    for i in range(KC):
                        last = nc.tensor.matmul(xb_[banks[c]][:], w[:, i, c * P:(c + 1) * P], src[:, i, :],
                                                start=(i == 0), stop=(i == KC - 1))
                    last.then_inc(kvr_done, 1)

            def project_kv(b):
                if not static(b, 0):
                    wait_count(pe, fs_ready, 2 * b - 2)
                project(b, 0, wk_s, xk, (4, 5))
                if not static(b, 0):
                    wait_count(pe, sum_ready, b - 1)
                project(b, 1, wv_s, xv, (2, 3))

            def project_r(b):
                if not static(b, 0):
                    pe.wait_ge(xb_ready, 2 * b)
                project(b, 2, wr_s, xr, (0, 1))

            def time_product(b):
                pe.wait_ge(g_ready, b + 1)
                wait_count(pe, h_relu, FCH * b)
                if static(b, 0):
                    pe.wait_ge(kvr_evac, 6)
                for h in range(2):
                    token_product(xb_[h], cut(gT, h), wo_s, KC).then_inc(wo_done, 1)

            def gate_part(b):
                r = round_gate(b)
                pe.wait_ge(xg_ready, b)
                transposes(xg, r)
                pe.wait_ge(t_emptied, r + 1)
                for j in range(TB):
                    for i in range(KC):
                        last = nc.tensor.matmul(tbk[0][:, j * EX:(j + 1) * EX], xgT[:, i, j * P:(j + 1) * P], gate_s[:, i, :],
                                                start=(i == 0), stop=(i == KC - 1))
                last.then_inc(t_filled, 1)

            pe.wait_ge(w_time_in, 48)
            pe.wait_ge(xn_ready, 1)
            transposes(xn, 0)
            project_kv(0)
            project_r(0)
            pe.wait_ge(xn_ready, 2)
            transposes(xn, 1)
            pe.wait_ge(w_in, 64)
            time_product(0)

            def period(b):
                if has_next(b, 1):
                    project_kv(b + 1)
                pe.wait_ge(xn2_ready, b + 1)
                transposes(xn2, round_xn2(b))
                if has_next(b, 1):
                    project_r(b + 1)
                if not static(b, 0):
                    gate_part(b)
                pe.wait_ge(mix2_ready, 2 * b + 1)
                if has_next(b, 1):
                    pe.wait_ge(kvr_evac, 6 * b + 12)
                else:
                    pe.wait_ge(xb_ready, 2 * b + 2)
                    pe.wait_ge(sum_ready, b)
                for m in range(FCH):
                    if m >= 4:
                        pe.wait_ge(h_relu, FCH * b + m - 3)
                    for i in range(KC):
                        last = nc.tensor.matmul(xb_[m % 4][:], fk_s[:, i, m * P:(m + 1) * P], xfk[:, i, :],
                                                start=(i == 0), stop=(i == KC - 1))
                    last.then_inc(fk_done, 1)
                pe.wait_ge(mix2_ready, 2 * b + 2)
                wait_count(pe, fs_ready, 2 * b)
                for h in range(2):
                    token_product(xb_[4 + h], cut(xfr, h), wf_s, KC).then_inc(fr_done, 1)
                pe.wait_ge(h_ready, FCH * b + FCH)
                token_product(xb_[2], cut(hT, 0), fv_s, FCH).then_inc(vk_done, 1)
                if has_next(b, 2):
                    pe.wait_ge(xn_ready, b + 3)
                    transposes(xn, round_xn(b + 2))
                if has_next(b, 1):
                    time_product(b + 1)
                token_product(xb_[3], cut(hT, 1), fv_s, FCH).then_inc(vk_done, 1)

            over_periods(pe, period)
            gate_part(B)


VECTORS = ("ln1_w", "ln1_b", "ln2_w", "ln2_b", "time_decay", "time_first", "time_mix_k", "time_mix_v", "time_mix_r",
           "f_time_mix_k", "f_time_mix_r")


def build(nc, x_in, qk_w, qk_b, lepe_w, lepe_b, w_key, w_value, w_recept, w_output, f_w_key, f_w_recept, f_w_value,
          w1, w2, w3, gate, vectors, cos_t, sin_t, out):
    x_mid = nc.dram_tensor("x_rows", (ROWS, C), F32, kind="Internal").ap()
    normed = nc.dram_tensor("normed_rows", (ROWS, C), F32, kind="Internal").ap()
    with ExitStack() as ctx:
        def sb(name, shape, dt=F32):
            return ctx.enter_context(nc.sbuf_tensor(name, shape, dt))

        logits = sb("logits", [P, T, EX])
        ident = sb("ident", [P, P])
        head_mask = sb("head_mask", [P, HEADS])
        block_mask = sb("block_mask", [P, P])
        neg_half = sb("neg_half", [P, TB])
        gate_s = sb("gate", [P, KC, EX])
        vectors_s = sb("vectors", [P, len(VECTORS), KC])
        vec = {name: vectors_s[:, n, :] for n, name in enumerate(VECTORS)}
        bank = [ctx.enter_context(nc.psum_tensor(f"bank{i}", [P, N], F32)) for i in range(8)]
        passed = {engine: ctx.enter_context(nc.semaphore("passed_" + engine)) for engine in ("dve", "pool", "act")}

        stage_constants(nc, ident, head_mask, block_mask, neg_half, (x_mid, normed, out), vectors, gate,
                        vectors_s, gate_s)
        phase_attention(nc, x_in, qk_w, qk_b, lepe_w, lepe_b, gate_s, cos_t, sin_t, normed, x_mid, logits, ident,
                        head_mask, block_mask, neg_half, bank, passed)
        phase_experts(nc, "first_", normed, x_mid, w1, w2, w3, logits, ident, bank, passed)
        phase_mix(nc, vec, w_key, w_value, w_recept, w_output, f_w_key, f_w_recept, f_w_value, gate_s, x_mid, normed, out,
                  logits, ident, neg_half, bank, passed)
        phase_experts(nc, "second_", normed, out, w1, w2, w3, logits, ident, bank, passed)


_INS = ["L0_attn_a_x", "L0_attn_a_qk_w", "L0_attn_a_qk_b", "L0_attn_a_lepe_w", "L0_attn_a_lepe_b",
        "L0_attn_b_w_key", "L0_attn_b_w_value", "L0_attn_b_w_recept", "L0_attn_b_w_output", "L0_attn_b_f_w_key",
        "L0_attn_b_f_w_recept", "L0_attn_b_f_w_value", "L0_ffn_w1", "L0_ffn_w2", "L0_ffn_w3"]


def kernel(**inputs):
    import numpy as _np
    import concourse.bacc as _bacc
    from concourse import mybir as _mybir
    from concourse.bass_utils import run_bass_kernel_spmd as _run

    nc = _bacc.Bacc("TRN2", target_bir_lowering=False, num_devices=1)
    f = _np.float32
    theta = (f(1.0) / f(10000.0) ** (_np.arange(C // 2, dtype=f) / f(C // 2))).astype(f)
    angles = (theta[:, None] * _np.arange(N, dtype=f)[None, :]).astype(f)
    gate = _np.asarray(inputs["L0_ffn_gate_w"]).reshape(EX, KC, P).transpose(2, 1, 0)
    vectors = _np.stack([_np.asarray(inputs["L0_attn_b_" + n]).reshape(KC, P).T for n in VECTORS], axis=1)
    arrays, args = {}, []
    for name, a in [(n, inputs[n]) for n in _INS] + [("gate", gate), ("vectors", vectors), ("rope_cos", _np.cos(angles)), ("rope_sin", _np.sin(angles))]:
        a = _np.ascontiguousarray(a)
        arrays[f"in_{name}"] = a
        args.append(nc.dram_tensor(f"in_{name}", a.shape, _mybir.dt.from_np(a.dtype), kind="ExternalInput").ap())
    args.append(nc.dram_tensor("out_x", (ROWS, C), F32, kind="ExternalOutput").ap())
    build(nc, *args)
    r = _run(nc, [arrays], core_ids=[0])
    return r.results[0]["out_x"][:B * N].reshape(B, N, C)
```
